# Optimizing a Trainium2 kernel written in Bass

```python
import numpy as np
import jax
import jax.numpy as jnp

def _softmax(x, axis=-1):
    return jax.nn.softmax(x, axis=axis)

def _gelu(x):
    return jax.nn.gelu(x, approximate=True)

def _silu(x):
    return jax.nn.silu(x)

def _sigmoid(x):
    return jax.nn.sigmoid(x)

def _layernorm(x, axis=-1, eps=1e-05):
    m = jnp.mean(x, axis=axis, keepdims=True)
    v = jnp.var(x, axis=axis, keepdims=True)
    return (x - m) / jnp.sqrt(v + eps)

def _scatter_add(tgt, idx, src, axis=0):
    return tgt.at[idx].add(src)

def _segment_sum(src, seg, n):
    return jax.ops.segment_sum(src, seg, n)
kernel_name = 'mk_macaron_d1_jaxref_r8_440fea'

def setup_inputs(seed: int=0):
    np.random.seed(seed)
    _w = jnp.asarray

    def _L0_attn_setup():
        import jax, jax.numpy as jnp
        import numpy as np
        B, S, D = (2, 256, 256)
        H, KVH = (16, 4)
        HD = D // H
        KVD = KVH * HD
        BASE = 10000.0
        EPS = 1.1920929e-07

        def _rms_norm(t):
            return t * jax.lax.rsqrt(jnp.mean(t * t, axis=-1, keepdims=True) + EPS)

        def _rope_tables(s, dtype):
            inv_freq = 1.0 / BASE ** (jnp.arange(0, HD, 2, dtype=jnp.float32) / HD)
            t = jnp.arange(s, dtype=jnp.float32)
            freqs = jnp.outer(t, inv_freq)
            cos = jnp.cos(freqs)[None, None].astype(dtype)
            sin = jnp.sin(freqs)[None, None].astype(dtype)
            return (cos, sin)

        def _apply_rope(t, cos, sin):
            half = t.shape[-1] // 2
            t1, t2 = (t[..., :half], t[..., half:])
            return jnp.concatenate([t1 * cos + t2 * sin, -t1 * sin + t2 * cos], axis=-1)
        key = jax.random.key(seed)
        ks = jax.random.split(key, 9)
        sd = 1.0 / np.sqrt(D)
        x = jax.random.normal(ks[0], (B, S, D), jnp.float32)
        Wq = jax.random.normal(ks[1], (D, D), jnp.float32) * sd
        bq = jnp.zeros((D,), jnp.float32)
        Wk = jax.random.normal(ks[2], (KVD, D), jnp.float32) * sd
        bk = jnp.zeros((KVD,), jnp.float32)
        Wv = jax.random.normal(ks[3], (KVD, D), jnp.float32) * sd
        bv = jnp.zeros((KVD,), jnp.float32)
        Wo = jax.random.normal(ks[4], (D, D), jnp.float32) * sd
        bo = jnp.zeros((D,), jnp.float32)
        q_gain = jnp.ones((H,), jnp.float32)
        return {'x': x, 'Wq': Wq, 'bq': bq, 'Wk': Wk, 'bk': bk, 'Wv': Wv, 'bv': bv, 'Wo': Wo, 'bo': bo, 'q_gain': q_gain}
    _L0_attn_in = _L0_attn_setup()

    def _L0_ffn_setup():
        import jax, jax.numpy as jnp
        import numpy as np
        TOP_P = 0.9
        S, B, H, I, E = (256, 4, 256, 512, 8)

        def _top_p_weights(probs, top_p):
            order = jnp.argsort(-probs, axis=-1)
            sp = jnp.take_along_axis(probs, order, axis=-1)
            cum = jnp.cumsum(sp, axis=-1)
            exceed = cum > top_p
            first_idx = jnp.argmax(exceed, axis=-1)
            first = jnp.arange(probs.shape[-1])[None, :] == first_idx[:, None]
            keep = ~exceed | first
            kept = jnp.where(keep, sp, 0.0)
            t_idx = jnp.arange(probs.shape[0])[:, None]
            return jnp.zeros_like(probs).at[t_idx, order].set(kept)
        key = jax.random.key(seed)
        ks = jax.random.split(key, 5)
        scale = 0.02
        return {'hidden_states': jax.random.normal(ks[0], (S, B, H), dtype=jnp.float32), 'router_w': jax.random.normal(ks[1], (E, H), dtype=jnp.float32) * scale, 'gate_w': jax.random.normal(ks[2], (E, I, H), dtype=jnp.float32) * scale, 'up_w': jax.random.normal(ks[3], (E, I, H), dtype=jnp.float32) * scale, 'down_w': jax.random.normal(ks[4], (E, H, I), dtype=jnp.float32) * scale}
    _L0_ffn_in = _L0_ffn_setup()
    _d = {'L0_attn_x': _L0_attn_in['x'], 'L0_attn_Wq': _L0_attn_in['Wq'], 'L0_attn_bq': _L0_attn_in['bq'], 'L0_attn_Wk': _L0_attn_in['Wk'], 'L0_attn_bk': _L0_attn_in['bk'], 'L0_attn_Wv': _L0_attn_in['Wv'], 'L0_attn_bv': _L0_attn_in['bv'], 'L0_attn_Wo': _L0_attn_in['Wo'], 'L0_attn_bo': _L0_attn_in['bo'], 'L0_attn_q_gain': _L0_attn_in['q_gain'], 'L0_ffn_router_w': _L0_ffn_in['router_w'], 'L0_ffn_gate_w': _L0_ffn_in['gate_w'], 'L0_ffn_up_w': _L0_ffn_in['up_w'], 'L0_ffn_down_w': _L0_ffn_in['down_w']}
    _x0 = _d['L0_attn_x']
    _d['L0_attn_x'] = jax.random.normal(jax.random.fold_in(jax.random.key(seed), 1), (8, 256, 256), dtype=_x0.dtype)
    del _x0
    return _d

def reference(L0_attn_x, L0_attn_Wq, L0_attn_bq, L0_attn_Wk, L0_attn_bk, L0_attn_Wv, L0_attn_bv, L0_attn_Wo, L0_attn_bo, L0_attn_q_gain, L0_ffn_router_w, L0_ffn_gate_w, L0_ffn_up_w, L0_ffn_down_w):

    def _L0_attn_ref(x, Wq, bq, Wk, bk, Wv, bv, Wo, bo, q_gain):
        import jax, jax.numpy as jnp
        import numpy as np
        B, S, D = (2, 256, 256)
        H, KVH = (16, 4)
        HD = D // H
        KVD = KVH * HD
        BASE = 10000.0
        EPS = 1.1920929e-07

        def _rms_norm(t):
            return t * jax.lax.rsqrt(jnp.mean(t * t, axis=-1, keepdims=True) + EPS)

        def _rope_tables(s, dtype):
            inv_freq = 1.0 / BASE ** (jnp.arange(0, HD, 2, dtype=jnp.float32) / HD)
            t = jnp.arange(s, dtype=jnp.float32)
            freqs = jnp.outer(t, inv_freq)
            cos = jnp.cos(freqs)[None, None].astype(dtype)
            sin = jnp.sin(freqs)[None, None].astype(dtype)
            return (cos, sin)

        def _apply_rope(t, cos, sin):
            half = t.shape[-1] // 2
            t1, t2 = (t[..., :half], t[..., half:])
            return jnp.concatenate([t1 * cos + t2 * sin, -t1 * sin + t2 * cos], axis=-1)
        b, s, d = x.shape
        q = (jnp.einsum('bsd,ed->bse', x, Wq) + bq).reshape(b, s, H, HD).transpose(0, 2, 1, 3)
        k = (jnp.einsum('bsd,ed->bse', x, Wk) + bk).reshape(b, s, KVH, HD).transpose(0, 2, 1, 3)
        v = (jnp.einsum('bsd,ed->bse', x, Wv) + bv).reshape(b, s, KVH, HD).transpose(0, 2, 1, 3)
        q = _rms_norm(q)
        k = _rms_norm(k)
        cos, sin = _rope_tables(s, q.dtype)
        q = _apply_rope(q, cos, sin)
        k = _apply_rope(k, cos, sin)
        q = q * q_gain[None, :, None, None]
        rep = H // KVH
        k = jnp.repeat(k, rep, axis=1)
        v = jnp.repeat(v, rep, axis=1)
        scale = HD ** (-0.5)
        attn = jnp.einsum('bhqd,bhkd->bhqk', q * scale, k)
        causal = jnp.tril(jnp.ones((s, s), dtype=bool))
        attn = jnp.where(causal[None, None], attn, -jnp.inf)
        attn = jax.nn.softmax(attn, axis=-1)
        out = jnp.einsum('bhqk,bhkd->bqhd', attn, v).reshape(b, s, d)
        return jnp.einsum('bsd,ed->bse', out, Wo) + bo

    def _L0_ffn_ref(hidden_states, router_w, gate_w, up_w, down_w):
        import jax, jax.numpy as jnp
        import numpy as np
        TOP_P = 0.9
        S, B, H, I, E = (256, 4, 256, 512, 8)

        def _top_p_weights(probs, top_p):
            order = jnp.argsort(-probs, axis=-1)
            sp = jnp.take_along_axis(probs, order, axis=-1)
            cum = jnp.cumsum(sp, axis=-1)
            exceed = cum > top_p
            first_idx = jnp.argmax(exceed, axis=-1)
            first = jnp.arange(probs.shape[-1])[None, :] == first_idx[:, None]
            keep = ~exceed | first
            kept = jnp.where(keep, sp, 0.0)
            t_idx = jnp.arange(probs.shape[0])[:, None]
            return jnp.zeros_like(probs).at[t_idx, order].set(kept)
        s, b, h = hidden_states.shape
        x = hidden_states.reshape(-1, h)
        probs = jax.nn.softmax(x @ router_w.T, axis=-1)
        w = _top_p_weights(probs, TOP_P)
        out = jnp.zeros_like(x)
        n_exp = router_w.shape[0]
        for e in range(n_exp):
            g = jax.nn.silu(x @ gate_w[e].T)
            u = x @ up_w[e].T
            y = g * u @ down_w[e].T
            out = out + y * w[:, e:e + 1]
        return out.reshape(s, b, h)
    x = L0_attn_x
    x = x + 0.5 * _L0_ffn_ref(_layernorm(x, axis=-1), L0_ffn_router_w, L0_ffn_gate_w, L0_ffn_up_w, L0_ffn_down_w)
    x = x + _L0_attn_ref(_layernorm(x, axis=-1), L0_attn_Wq, L0_attn_bq, L0_attn_Wk, L0_attn_bk, L0_attn_Wv, L0_attn_bv, L0_attn_Wo, L0_attn_bo, L0_attn_q_gain)
    x = x + 0.5 * _L0_ffn_ref(_layernorm(x, axis=-1), L0_ffn_router_w, L0_ffn_gate_w, L0_ffn_up_w, L0_ffn_down_w)
    return x

_drawn_inputs = setup_inputs


def setup_inputs(seed=0):
    import zlib

    import numpy as np

    out = dict(_drawn_inputs(seed))
    spreads = {'L0_attn_bq': (0.0, 0.454),
     'L0_attn_bk': (0.0, 0.6),
     'L0_attn_bv': (0.0, 0.1),
     'L0_attn_bo': (0.0, 0.1),
     'L0_attn_q_gain': (1.0, 0.6)}
    factors = {'L0_ffn_router_w': 8.0,
     'L0_ffn_gate_w': 6.741,
     'L0_ffn_up_w': 6.641,
     'L0_ffn_down_w': 6.643}
    for name, (base, spread) in spreads.items():
        noise = np.random.default_rng([zlib.crc32(name.encode()), seed]).standard_normal(out[name].shape)
        drawn = base * np.exp(spread * noise) if base else spread * noise
        out[name] = jnp.asarray(drawn.astype(out[name].dtype))
    for name, factor in factors.items():
        out[name] = (out[name] * factor).astype(out[name].dtype)
    return out
```

```python
from contextlib import ExitStack

import concourse.bass as bass
from concourse import mybir

F32, F16, BF16 = mybir.dt.float32, mybir.dt.float16, mybir.dt.bfloat16
I32 = mybir.dt.int32
ALU, ACT, AX = mybir.AluOpType, mybir.ActivationFunctionType, mybir.AxisListType

P = 128
B, S, D = 8, 256, 256
H, KVH = 16, 4
HD = D // H
E, I = 8, 512
TOP_P = 0.9
LN_EPS = 1e-5
RMS_EPS = 1.1920929e-07
NT = B * S // P
BT = 4
BLK = BT * P
KD = D // P
KI = I // P
QKVW = D + 2 * KVH * HD
QK = H + KVH
G = H // KVH
W3 = KD * I
VW = 3 * HD + 1

XS = 1024.0
WTOP = 14
TANH_C = 0.5 * 2.0 ** -WTOP / XS
H_C = 2.0 ** (-3 - 1 - 2 * WTOP - 20)
CF_C = 0.5 * 2.0 ** (3 - WTOP)
MASKED = -64.0

RANGES = {"fp": (0, 31), "wp": (3, 6), "ff": (4, 35), "ap": (8, 23), "a3": (9, 24), "hd": (10, 25),
          "pw": (11, 26), "op": (12, 27), "st": (24, 35)}
RUNS = [(4, 5), (5, 7), (7, 8), (8, 9), (9, 10), (10, 11), (11, 12), (12, 24), (24, 25), (25, 26),
        (26, 27), (27, 28), (28, 32), (32, 36)]


def active(n):
    return {f for f, (a, b) in RANGES.items() if a <= n <= b}


class Lane:

    def __init__(self, sem, stage, labels, extra=0):
        self.sem, self.labels = sem, labels
        self.first = RANGES[stage][0]
        self.per = len(labels)
        self.credit = self.per + extra

    def inc(self, instr, label):
        assert label in self.labels
        instr.then_inc(self.sem, 1)

    def value(self, n, label):
        return self.per * (n - self.first + 1) + self.labels.index(label) + 1

    def wait(self, eng, n, label):
        eng.wait_ge(self.sem, self.value(n, label))


BANK_USES = [
    ("a3", {"A": ("a_a3", "qe"), "B": ("v_a3", "ke1")}),
    ("pw", {"C": ("v_pw", "rd")}),
    ("fp", {"A": ("a_xt", "xt")}),
    ("hd", {"A": ("a_hd", "e0.3"), "B": ("a_hd", "e0.7"), "C": ("a_hd", "e0.7")}),
    ("hd", {"A": ("v_hd", "l0.0"), "B": ("v_hd", "l0.1"), "C": ("v_hd", "l0.2")}),
    ("ap", {"A": ("a_ap", "xt")}),
    ("op", {"B": ("a_op", "ot")}),
    ("hd", {"C": ("v_hd", "rd0")}),
    ("ap", {"A": ("v_ap", "qb")}),
    ("op", {"B": ("v_op", "ad")}),
    ("fp", {"C": ("a_rt", "ex")}),
    ("hd", {"A": ("a_hd", "e1.3"), "B": ("a_hd", "e1.7"), "C": ("a_hd", "e1.7")}),
    ("hd", {"A": ("v_pw", "l0"), "B": ("v_pw", "l1"), "C": ("v_pw", "l2")}),
]
USE = {"a3": 0, "pw": 1, "fp.tp": 2, "sc0": 3, "pt0": 4, "ap.tp": 5, "op.tp": 6, "pv0": 7, "ap.qkv": 8,
       "op.mm": 9, "fp.lg": 10, "sc1": 11, "pt1": 12}


def build(nc, d):
    with ExitStack() as ctx:
        def sb(name, shape, dt):
            return ctx.enter_context(nc.sbuf_tensor(name, shape, dt))

        def sem(name):
            return ctx.enter_context(nc.semaphore(name))

        X = sb("X", [P, NT, D], F32)
        W = sb("W", [P, E, 2, 3, W3], F16)
        room = sb("room", [P, 3 * W3], F32)
        stage = room[:, :].rearrange("p (j w) -> p j w", j=3)
        NP3 = 3 * G * P
        P32 = room[:, 0:NP3].rearrange("p (b g k) -> p b g k", b=3, g=G)
        PH, PL = (room[:, NP3 + j * NP3 // 2:NP3 + (j + 1) * NP3 // 2].bitcast(F16).rearrange(
            "p (b g k) -> p b g k", b=3, g=G) for j in range(2))
        XS16 = sb("XS16", [P, 2, 2, KD, BT, P], F16)
        HS = sb("HS", [P, 2, 2, KI, BLK], F16)
        TS = sb("TS", [P, 2, BLK], F32)
        H32 = sb("H32", [P, 2, BLK], F32)
        WT = sb("WT", [P, NT // BT, BT, E], F32)
        WTC = sb("WTC", [P, 2, BT], F32)
        MXW = sb("MXW", [P, 3], F32)
        MAW = sb("MAW", [P, 3], F32)
        PEW = sb("PEW", [P, 3], F32)
        SCW = sb("SCW", [P, 3], F32)
        GUD = sb("GUD", [P, 1], F32)
        TSC = sb("TSC", [P, E, 1], F32)
        CF = sb("CF", [P, E, 1], F32)
        RW = sb("RW", [P, KD, E], F32)
        WQKV = sb("WQKV", [P, KD, QKVW], F32)
        WO = sb("WO", [P, KD, D], F32)
        BQKV = sb("BQKV", [P, QKVW], F32)
        BO = sb("BO", [P, D], F32)
        GN = sb("GN", [P, H], F32)
        AG = sb("AG", [P, KVH, G], F32)
        SGN = sb("SGN", [P, H], F32)
        COS = sb("COS", [P, 2, HD // 2], F32)
        SIN = sb("SIN", [P, 2, HD // 2], F32)
        NSIN = sb("NSIN", [P, 2, HD // 2], F32)
        ident = sb("ident", [P, P], F32)
        ident16 = sb("ident16", [P, P], F16)
        MB = sb("MB", [P, G, P], F16)
        LOW = sb("LOW", [P, E, E], F32)
        MH = sb("MH", [P, QK], F32)
        LN = {k: (sb(f"ST{k}", [P, 6], F32), sb(f"MV{k}", [P, 2], F32), sb(f"VE{k}", [P, 1], F32),
                  sb(f"RS{k}", [P, 1], F32), sb(f"XN{k}", [P, D], F32), sb(f"XT{k}", [P, KD, P], F32))
              for k in ("f", "a")}
        NM = sb("NM", [P, 1], F32)
        EX = sb("EX", [P, E], F32)
        ES = sb("ES", [P, 1], F32)
        EC = sb("EC", [P, 1], F32)
        PR = sb("PR", [P, E], F32)
        EQ = sb("EQ", [P, E, E], F32)
        GT = sb("GT", [P, E, E], F32)
        CUM = sb("CUM", [P, E], F32)
        QKV = sb("QKV", [P, QKVW], F32)
        SQ = sb("SQ", [P, QK * HD], F32)
        SS = sb("SS", [P, QK], F32)
        MS = sb("MS", [P, QK], F32)
        RR = sb("RR", [P, QK], F32)
        QN = sb("QN", [P, QK * HD], F32)
        RA = sb("RA", [P, QK * HD], F32)
        RB = sb("RB", [P, QK, 2, HD // 2], F32)
        QS = sb("QS", [P, H, 4, HD], F16)
        KS = sb("KS", [P, KVH, 2, 4, HD], F16)
        VR = sb("VR", [P, 2, KVH, HD], F32)
        VS = sb("VS", [P, 2, 2, KVH, VW], BF16)
        QT = sb("QT", [P, 2, 2, H // 2, P], F16)
        KT = sb("KT", [P, 2, KVH, 2, 2, P], F16)
        MX = sb("MX", [P, 2, G], F32)
        NB = sb("NB", [P, 2, G], F32)
        RC = sb("RC", [P, 2 * G], F32)
        RD = sb("RD", [P, 2 * G, HD], F32)
        OB = sb("OB", [P, 2, 2, KVH, G * HD], F32)
        OS = sb("OS", [P, D], F32)
        OT = sb("OT", [P, KD, P], F32)

        GB = [ctx.enter_context(nc.psum_tensor(f"G{i}", [P, BLK], F32)) for i in range(2)]
        UB = [ctx.enter_context(nc.psum_tensor(f"U{i}", [P, BLK], F32)) for i in range(2)]
        YB = ctx.enter_context(nc.psum_tensor("YB", [P, BLK], F32))
        BA, BB, BC = (ctx.enter_context(nc.psum_tensor(f"B{c}", [P, BLK], F32)) for c in "ABC")

        s_x0, s_x1 = sem("s_x0"), sem("s_x1")
        s_rw, s_aw = sem("s_rw"), sem("s_aw")
        s_w = [sem(f"s_w{j}") for j in range(3)]
        s_i1, s_i2 = sem("s_i1"), sem("s_i2")
        s_ag, s_apart = sem("s_ag"), sem("s_apart")
        N_I1 = 8
        s_st = sem("s_st")

        items = range(2)
        L = {}
        for name, stage_, labels in [
            ("p_gu", "ff", [f"gu{i}" for i in range(8)]),
            ("p_y", "ff", [f"y{i}" for i in range(8)]),
            ("p_fp", "fp", ["tp"]), ("p_lg", "fp", ["lg"]),
            ("p_ap", "ap", ["tp", "qkv"]), ("p_a3", "a3", ["qt", "kt"]),
            ("p_hd", "hd", ["sa0", "sb0", "pt0.0", "pt0.1", "pt0.2", "pv0", "sa1", "sb1", "pt1.0", "pt1.1", "pt1.2"]),
            ("p_pw", "pw", ["pv"]), ("p_op", "op", ["tp", "mm"]),
            ("a_ff", "ff", [f"{s}{i}" for i in range(8) for s in ("tanh", "hi")]),
            ("a_xt", "fp", ["xt"]), ("a_rt", "fp", ["ex"]),
            ("a_wp", "wp", [f"hi{x}.{j}" for x in items for j in range(3)]),
            ("a_ap", "ap", ["xt", "qhi", "khi0", "khi1"]), ("a_a3", "a3", ["qe"]),
            ("a_hd", "hd", [f"e0.{i}" for i in range(8)] + [f"h0.{i}" for i in range(3)] + [f"e1.{i}" for i in range(8)]),
            ("a_pw", "pw", [f"h{i}" for i in range(3)]), ("a_op", "op", ["ot"]),
            ("v_ff", "ff", [f"{s}{i}" for i in range(8) for s in ("t", "h")]),
            ("v_y", "ff", [f"y{i}" for i in range(8)]), ("v_wc", "ff", ["wc0", "wc1"]),
            ("v_ln", "fp", ["stats", "aggr", "eps", "xn"]), ("v_sp", "fp", ["xh", "xl"]),
            ("v_rt", "fp", ["mx", "rc", "p", "eq", "gt", "cum", "wt"]),
            ("v_wp", "wp", [f"{s}{x}" for x in items for s in ("mx.0.", "mx.1.", "mx.2.", "cl", "pe", "rc", "sc", "tsc", "gu", "cf", "lo.0.", "lo.1.", "lo.2.")]),
            ("v_al", "ap", ["stats", "aggr", "eps", "xn"]),
            ("v_ap", "ap", ["qb", "ss", "ms", "qn", "rb0", "rb1", "r", "qlo", "klo0", "klo1"]),
            ("v_a3", "a3", ["ke0", "ke1"]),
            ("v_hd", "hd", ["mx0.0", "mx0.1", "mx0.2", "nb0", "l0.0", "l0.1", "l0.2", "rc0", "rd0", "ob0",
                            "mx1.0", "mx1.1", "mx1.2", "nb1"]),
            ("v_pw", "pw", ["l0", "l1", "l2", "rc", "rd", "ob"]), ("v_op", "op", ["ad"]),
            ("g_ff", "ff", [f"lo{i}" for i in range(8)]),
            ("g_ln", "fp", ["rs"]), ("g_rt", "fp", ["eq", "b", "bp"]), ("g_wp", "wp", ["ar0", "ar1"]),
            ("g_al", "ap", ["rs", "bo"]), ("g_ap", "ap", ["sq", "rr", "sg", "ra", "v1", "r1", "v2", "r2", "v3"]),
            ("g_op", "op", ["os"]),
            ("g_hd", "hd", ["k0.0", "k0.1", "k1.0", "k1.1"]),
        ]:
            L[name] = Lane(sem(name), stage_, labels, extra=4 if name in ("p_y", "v_y") else 0)

        def give_credit(eng, prefix):
            for name, lane in L.items():
                if name.startswith(prefix):
                    eng.sem_inc(lane.sem, lane.credit)

        def wait_apart(lane, eng, n, label):
            lane.wait(eng, n, label)
            if not isinstance(n, int):
                eng.sem_inc(s_apart, 1)

        def steps(eng, body):
            for a, b in RUNS:
                if b - a == 1:
                    body(a, active(a))
                else:
                    with eng.Fori(a, b) as n:
                        body(n, active(a))

        def blk(n):
            return ((n - 4) // BT) % (NT // BT)

        def xpar(n):
            return (n // BT + 1) % 2

        def bank_ready(eng, n, act, use, banks="ABC"):
            before = active(n - 1) if isinstance(n, int) else act
            for bank in banks:
                if bank not in BANK_USES[USE[use]][1]:
                    continue
                found = None
                for f, who in reversed(BANK_USES[:USE[use]]):
                    if f in act and bank in who:
                        found = (who[bank], n)
                        break
                if found is None:
                    for f, who in reversed(BANK_USES):
                        if f in before and bank in who:
                            found = (who[bank], n if who[bank][0] == "v_pw" and f == "hd" else n - 1)
                            break
                if found is not None:
                    (lane, label), m = found
                    L[lane].wait(eng, m, label)

        def pe_gu(eng, n, act, i):
            h, m = divmod(i, 4)
            e = (n % 4) * 2 + h
            if i == 0:
                L["v_sp"].wait(eng, n - 1 if "fp" in act else 31, "xl")
                if "wp" in act or (isinstance(n, int) and n == 7):
                    L["a_wp"].wait(eng, n - 1, "hi1.2")
                    L["v_wp"].wait(eng, n - 1, "lo.2.1")
            if i < 2:
                L["v_ff"].wait(eng, n - 1, f"h{i + 6}")
            else:
                L["v_ff"].wait(eng, n, f"h{i - 2}")
            for j, bank in ((0, GB[i % 2]), (1, UB[i % 2])):
                q = 0
                for k in range(KD):
                    for wl, xl in ((0, 0), (0, 1), (1, 0)):
                        mm = eng.matmul(bank[:, :], W[:, e, wl, j, k * I + m * P:k * I + (m + 1) * P],
                                        XS16[:, xpar(n), xl, k, :, :].rearrange("p a b -> p (a b)"),
                                        start=(q == 0), stop=(q == 3 * KD - 1))
                        q += 1
            L["p_gu"].inc(mm, f"gu{i}")

        def pe_y(eng, n, i):
            h, m = divmod(i, 4)
            par = 1 - h
            e = (n % 4) * 2 if h else ((n + 3) % 4) * 2 + 1
            if i == 0:
                L["a_ff"].wait(eng, n - 1, "hi7")
            elif i == 4:
                L["a_ff"].wait(eng, n, "hi3")
            L["v_y"].wait(eng, n - 1 if i == 0 else n, f"y{(i - 1) % 8}")
            q = 0
            for hl, wl in ((0, 0), (0, 1), (1, 0)):
                if hl == 1 and i == 0:
                    L["g_ff"].wait(eng, n - 1, "lo7")
                if hl == 1 and i == 4:
                    L["g_ff"].wait(eng, n, "lo3")
                for k in range(KI):
                    mm = eng.matmul(YB[:, 0:D], HS[:, par, hl, k, m * P:(m + 1) * P],
                                    W[:, e, wl, 2, k * D:(k + 1) * D], start=(q == 0), stop=(q == 3 * KI - 1))
                    q += 1
            L["p_y"].inc(mm, f"y{i}")

        def pe_fp_tp(eng, n, act):
            bank_ready(eng, n, act, "fp.tp")
            L["v_ln"].wait(eng, n, "xn")
            for k in range(KD):
                mm = eng.transpose(BA[:, k * P:(k + 1) * P], LN["f"][4][:, k * P:(k + 1) * P], ident[:, :])
            L["p_fp"].inc(mm, "tp")

        def pe_fp_lg(eng, n, act):
            bank_ready(eng, n, act, "fp.lg")
            L["a_xt"].wait(eng, n, "xt")
            for k in range(KD):
                mm = eng.matmul(BC[:, 0:E], LN["f"][5][:, k, :], RW[:, k, :], start=(k == 0), stop=(k == KD - 1))
            L["p_lg"].inc(mm, "lg")

        def pe_ap_tp(eng, n, act):
            bank_ready(eng, n, act, "ap.tp")
            L["v_al"].wait(eng, n, "xn")
            for k in range(KD):
                mm = eng.transpose(BA[:, k * P:(k + 1) * P], LN["a"][4][:, k * P:(k + 1) * P], ident[:, :])
            L["p_ap"].inc(mm, "tp")

        def pe_ap_qkv(eng, n, act):
            L["a_ap"].wait(eng, n, "xt")
            for k in range(KD):
                mm = eng.matmul(BA[:, 0:QKVW], LN["a"][5][:, k, :], WQKV[:, k, :], start=(k == 0), stop=(k == KD - 1))
            L["p_ap"].inc(mm, "qkv")

        def pe_a3(eng, n, act):
            bank_ready(eng, n, act, "a3")
            L["v_ap"].wait(eng, n - 1, "klo1")
            L["a_ap"].wait(eng, n - 1, "khi1")
            qs = QS[:, :, :, :].rearrange("p h s c -> p (h s c)")
            ks = KS[:, :, :, :, :].rearrange("p h u s c -> p (h u s c)")
            a16, b16 = BA[:, :].bitcast(F16), BB[:, :].bitcast(F16)
            for j in range(H // 2):
                mm = eng.transpose(a16[:, j * P:(j + 1) * P], qs[:, j * P:(j + 1) * P], ident16[:, :])
            L["p_a3"].inc(mm, "qt")
            for j in range(KVH):
                mm = eng.transpose(b16[:, j * P:(j + 1) * P], ks[:, j * P:(j + 1) * P], ident16[:, :])
            L["p_a3"].inc(mm, "kt")

        def pe_scores(eng, n, act, it):
            par, kv = ((n - 10) // 2) % 2, 2 * (n % 2) + it
            if it == 0 and "a3" in act:
                L["a_a3"].wait(eng, n, "qe")
                L["v_a3"].wait(eng, n, "ke1")
            bank_ready(eng, n, act, f"sc{it}", "A")
            for jj in range(2):
                eng.matmul(BA[:, jj * 2 * P:(jj + 1) * 2 * P], QT[:, par, 0, 2 * kv + jj, :],
                           KT[:, par, kv, :, 0, :], start=(jj == 0), stop=False, skip_group_check=True)
            mm = eng.matmul(BA[:, :], ident16[:, :], MB[:, :, :].rearrange("p a b -> p (a b)"), start=False, stop=True,
                            skip_group_check=True)
            L["p_hd"].inc(mm, f"sa{it}")
            bank_ready(eng, n, act, f"sc{it}", "BC")
            for jj, bank in ((0, BB), (1, BC)):
                eng.matmul(bank[:, :], QT[:, par, 1, 2 * kv + jj, :],
                           KT[:, par, kv, :, :, :].rearrange("p a b c -> p (a b c)"), start=True, stop=False,
                           skip_group_check=True)
                mm = eng.matmul(bank[:, :].rearrange("p (a b) -> p a b", a=2)[:, :, P:2 * P], ident16[:, :],
                                MB[:, 0:2, :], start=False, stop=True, skip_group_check=True)
            L["p_hd"].inc(mm, f"sb{it}")

        def pe_pt(eng, n, act, it):
            for b, bank in enumerate((BA, BB, BC)):
                if b == 0:
                    L["g_hd"].wait(eng, n, f"k{it}.0")
                elif b == 1:
                    L["a_hd"].wait(eng, n, f"e{it}.7")
                else:
                    L["g_hd"].wait(eng, n, f"k{it}.1")
                bank_ready(eng, n, act, f"pt{it}", "ABC"[b])
                for g in range(G):
                    mm = eng.transpose(bank[:, g * P:(g + 1) * P], P32[:, b, g, :], ident[:, :])
                L["p_hd"].inc(mm, f"pt{it}.{b}")

        def pe_pv(eng, n, act, lane, label, ready, use, par):
            kv = 2 * (n % 2) if label == "pv0" else 2 * ((n + 1) % 2) + 1
            bank_ready(eng, n, act, use)
            L[ready[0]].wait(eng, n, ready[1])
            for qt in range(2):
                for g in range(G):
                    o = BC[:, (qt * G + g) * VW:(qt * G + g + 1) * VW]
                    terms = [(0, 0)] if qt == 0 else [(1, 0), (2, 1)]
                    q = 0
                    for b, kt in terms:
                        for ph in (PH, PL):
                            mm = eng.matmul(o, ph[:, b, g, :], VS[:, par, kt, kv, :], start=(q == 0),
                                            stop=(q == 2 * len(terms) - 1))
                            q += 1
            L[lane].inc(mm, label)

        def pe_op_tp(eng, n, act):
            bank_ready(eng, n, act, "op.tp")
            L["g_op"].wait(eng, n, "os")
            for k in range(KD):
                mm = eng.transpose(BB[:, k * P:(k + 1) * P], OS[:, k * P:(k + 1) * P], ident[:, :])
            L["p_op"].inc(mm, "tp")

        def pe_op_mm(eng, n, act):
            L["a_op"].wait(eng, n, "ot")
            for k in range(KD):
                mm = eng.matmul(BB[:, 0:D], OT[:, k, :], WO[:, k, :], start=(k == 0), stop=(k == KD - 1))
            L["p_op"].inc(mm, "mm")

        def pe_body(eng, n, act):
            for p in range(16):
                i = p // 2
                if p % 2 == 0:
                    pe_gu(eng, n, act, i)
                elif not (isinstance(n, int) and n == 4 and i < 4):
                    pe_y(eng, n, i)
                if p == 0 and "a3" in act:
                    pe_a3(eng, n, act)
                if p == 1 and "pw" in act:
                    pe_pv(eng, n, act, "p_pw", "pv", ("v_pw", "l2"), "pw", ((n - 11) // 2) % 2)
                if p == 2 and "fp" in act:
                    pe_fp_tp(eng, n, act)
                if p == 3 and "hd" in act:
                    pe_scores(eng, n, act, 0)
                if p == 6 and "hd" in act:
                    pe_pt(eng, n, act, 0)
                if p == 8 and "ap" in act:
                    pe_ap_tp(eng, n, act)
                if p == 8 and "op" in act:
                    pe_op_tp(eng, n, act)
                if p == 9 and "hd" in act:
                    pe_pv(eng, n, act, "p_hd", "pv0", ("v_hd", "l0.2"), "pv0", ((n - 10) // 2) % 2)
                if p == 10 and "ap" in act:
                    pe_ap_qkv(eng, n, act)
                if p == 10 and "op" in act:
                    pe_op_mm(eng, n, act)
                if p == 11 and "fp" in act:
                    pe_fp_lg(eng, n, act)
                if p == 12 and "hd" in act:
                    pe_scores(eng, n, act, 1)
                if p == 15 and "hd" in act:
                    pe_pt(eng, n, act, 1)

        def act_tanh(eng, n, i):
            e = (n % 4) * 2 + i // 4
            L["p_gu"].wait(eng, n, f"gu{i}")
            wait_apart(L["v_ff"], eng, n - 1 if i < 2 else n, f"h{(i - 2) % 8}")
            L["a_ff"].inc(eng.activation(TS[:, i % 2, :], GB[i % 2][:, :], ACT.Tanh, scale=TSC[:, e, :]), f"tanh{i}")

        def act_hi(eng, n, i):
            h, m = divmod(i, 4)
            L["v_ff"].wait(eng, n, f"h{i}")
            if m == 0:
                L["p_y"].wait(eng, n if h else n - 1, "y3" if h else "y7")
            L["a_ff"].inc(eng.activation(HS[:, h, 0, m, :], H32[:, i % 2, :], ACT.Copy), f"hi{i}")

        def act_xt(eng, n):
            L["p_fp"].wait(eng, n, "tp")
            L["v_sp"].wait(eng, n - 1, "xl")
            L["p_lg"].wait(eng, n - 1, "lg")
            L["a_xt"].inc(eng.activation(LN["f"][5][:, :, :].rearrange("p a b -> p (a b)"), BA[:, 0:D], ACT.Copy), "xt")

        def act_rt(eng, n):
            L["p_lg"].wait(eng, n, "lg")
            L["v_rt"].wait(eng, n, "mx")
            L["a_rt"].inc(eng.activation(EX[:, :], BC[:, 0:E], ACT.Exp, bias=NM[:, 0:1], accum_out=ES[:, 0:1]), "ex")

        def act_wp(eng, n, x):
            e = 2 * (n - 3) + x
            wait_apart(L["v_wp"], eng, n, f"sc{x}")
            for j in range(3):
                L["a_wp"].inc(eng.activation(W[:, e, 0, j, :], stage[:, j, :], ACT.Copy, scale=SCW[:, j:j + 1]), f"hi{x}.{j}")

        def act_exps(eng, n, it):
            kv = 2 * (n % 2) + it
            L["v_hd"].wait(eng, n, f"nb{it}")
            wait_apart(L["p_hd"], eng, n if it else n - 1, "pt0.2" if it else "pt1.2")
            for g in range(G):
                L["a_hd"].inc(eng.activation(P32[:, 0, g, :], BA[:, g * P:(g + 1) * P], ACT.Exp,
                                             bias=NB[:, 0, g:g + 1], scale=AG[:, kv, g:g + 1]), f"e{it}.{g}")
            for g in range(G):
                bank = (BB, BC)[g // 2]
                s = bank[:, (g % 2) * 2 * P:(g % 2 + 1) * 2 * P].rearrange("p (a b) -> p a b", a=2)
                L["a_hd"].inc(eng.activation(P32[:, 1:3, g, :], s, ACT.Exp, bias=NB[:, 1, g:g + 1],
                                             scale=AG[:, kv, g:g + 1]), f"e{it}.{G + g}")

        def act_ph(eng, n, step, pv, lane, prefix, pt):
            L[pv[0]].wait(eng, pv[1], pv[2])
            for b, bank in enumerate((BA, BB, BC)):
                L["p_hd"].wait(eng, step, f"{pt}.{b}")
                L[lane].inc(eng.activation(PH[:, b, :, :].rearrange("p a b -> p (a b)"), bank[:, :], ACT.Copy), f"{prefix}{b}")

        def act_ap_xt(eng, n):
            L["p_ap"].wait(eng, n, "tp")
            L["p_ap"].wait(eng, n - 1, "qkv")
            L["a_ap"].inc(eng.activation(LN["a"][5][:, :, :].rearrange("p a b -> p (a b)"), BA[:, 0:D], ACT.Copy), "xt")

        def act_ap_hi(eng, n):
            L["v_ap"].wait(eng, n, "r")
            L["p_a3"].wait(eng, n, "kt") if not (isinstance(n, int) and n == 8) else None
            q = RA[:, 0:H * HD].rearrange("p (h c) -> p h c", c=HD)
            k = RA[:, H * HD:].rearrange("p (h c) -> p h c", c=HD)
            L["a_ap"].inc(eng.activation(QS[:, :, 0:4:2, :], q.unsqueeze(2).broadcast_to([P, H, 2, HD]), ACT.Copy), "qhi")
            for s in range(2):
                L["a_ap"].inc(eng.activation(KS[:, :, :, s, :], k.unsqueeze(2).broadcast_to([P, KVH, 2, HD]), ACT.Copy), f"khi{s}")

        def act_qe(eng, n):
            wait_apart(L["p_a3"], eng, n, "qt")
            L["a_a3"].inc(eng.activation(QT[:, ((n - 9) // 2) % 2, (n + 1) % 2, :, :].rearrange("p a b -> p (a b)"),
                                         BA[:, :].bitcast(F16), ACT.Copy), "qe")

        def act_ot(eng, n):
            L["p_op"].wait(eng, n, "tp")
            L["p_op"].wait(eng, n - 1, "mm")
            L["a_op"].inc(eng.activation(OT[:, :, :].rearrange("p a b -> p (a b)"), BB[:, 0:D], ACT.Copy), "ot")

        def act_body(eng, n, act):
            for p in range(16):
                i = p // 2
                if p % 2 == 0:
                    act_tanh(eng, n, i)
                if p == 0 and "pw" in act:
                    act_ph(eng, n, n - 1, ("p_hd", n - 1, "pv0"), "a_pw", "h", "pt1")
                if p == 0 and "a3" in act:
                    act_qe(eng, n)
                if p == 2 and "fp" in act:
                    act_xt(eng, n)
                if p == 4 and "hd" in act:
                    act_exps(eng, n, 0)
                if p == 7 and "hd" in act:
                    act_ph(eng, n, n, ("p_pw", n, "pv") if "pw" in act else ("p_pw", n, "pv"), "a_hd", "h0.", "pt0")
                if p == 9 and "ap" in act:
                    act_ap_xt(eng, n)
                if p == 9 and "op" in act:
                    act_ot(eng, n)
                if p == 12 and "fp" in act:
                    act_rt(eng, n)
                if p == 12 and "hd" in act:
                    act_exps(eng, n, 1)
                if p == 5 and "wp" in act:
                    act_wp(eng, n, 0)
                if p == 13 and "wp" in act:
                    act_wp(eng, n, 1)
                if p == 14 and "ap" in act:
                    act_ap_hi(eng, n)
                if p % 2 == 1:
                    act_hi(eng, n, i)

        def dve_gu(eng, n, i):
            L["a_ff"].wait(eng, n, f"tanh{i}")
            L["v_ff"].inc(eng.scalar_tensor_tensor(TS[:, i % 2, :], TS[:, i % 2, :], 1.0, GB[i % 2][:, :],
                                                   ALU.add, ALU.mult), f"t{i}")
            L["v_ff"].wait(eng, n, f"t{i}")
            m, j = (n, i - 2) if i >= 2 else (n - 1, i + 6)
            L["a_ff"].wait(eng, m, f"hi{j}")
            L["g_ff"].wait(eng, m, f"lo{j}")
            L["v_ff"].inc(eng.scalar_tensor_tensor(H32[:, i % 2, :], TS[:, i % 2, :], H_C, UB[i % 2][:, :],
                                                   ALU.mult, ALU.mult), f"h{i}")

        def dve_wc(eng, n, act, h):
            e = (n % 4) * 2 + h
            if h == 0:
                L["v_rt"].wait(eng, n - 1 if "fp" in act else 31, "wt")
            L["v_y"].wait(eng, n if h else n - 1, "y3" if h else "y7")
            L["v_wc"].inc(eng.tensor_tensor(WTC[:, h, :], WT[:, blk(n), :, e], CF[:, e, :].broadcast_to([P, BT]),
                                            ALU.mult), f"wc{h}")

        def dve_y(eng, n, i):
            h, m = divmod(i, 4)
            L["p_y"].wait(eng, n, f"y{i}")
            L["v_y"].wait(eng, n - 1 if h == 0 else n, f"y{(i + 4) % 8}")
            L["v_wc"].wait(eng, n - 1 if h == 0 else n, f"wc{1 - h}")
            b = blk(n) if h else blk(n - 1)
            x = X[:, b * BT + m, :]
            L["v_y"].inc(eng.scalar_tensor_tensor(x, YB[:, 0:D], WTC[:, 1 - h, m:m + 1], x, ALU.mult, ALU.add), f"y{i}")

        def dve_ln(eng, n, lane, glane, k, t, free):
            ST, MV, VE, RS, XN, _ = LN[k]
            L[lane].inc(eng.bn_stats(ST[:, :], X[:, t, :]), "stats")
            wait_apart(L[lane], eng, n, "stats")
            L[lane].inc(eng.bn_aggr(MV[:, :], ST[:, :]), "aggr")
            L[lane].wait(eng, n, "aggr")
            L[lane].inc(eng.tensor_scalar(VE[:, :], MV[:, 1:2], LN_EPS, None, ALU.add), "eps")
            L[glane].wait(eng, n, "rs")
            L[free].wait(eng, n - 1, "tp")
            L[lane].inc(eng.tensor_scalar(XN[:, :], X[:, t, :], MV[:, 0:1], RS[:, 0:1], ALU.subtract, ALU.mult), "xn")

        def dve_split(eng, n):
            XT = LN["f"][5]
            par, c = (n // BT) % 2, n % BT
            L["a_xt"].wait(eng, n, "xt")
            L["p_gu"].wait(eng, n - 1, "gu7") if not (isinstance(n, int) and n < 5) else None
            L["v_sp"].inc(eng.tensor_scalar(XS16[:, par, 0, :, c, :], XT[:, :, :], XS, None, ALU.mult), "xh")
            L["v_sp"].wait(eng, n, "xh")
            L["v_sp"].inc(eng.scalar_tensor_tensor(XS16[:, par, 1, :, c, :], XT[:, :, :], XS, XS16[:, par, 0, :, c, :],
                                                   ALU.mult, ALU.subtract), "xl")

        def dve_rt1(eng, n):
            L["p_lg"].wait(eng, n, "lg")
            L["v_rt"].inc(eng.tensor_reduce(NM[:, :], BC[:, 0:E], AX.X, ALU.max, negate=True), "mx")

        def dve_rt2(eng, n):
            L["a_rt"].wait(eng, n, "ex")
            L["v_rt"].inc(eng.reciprocal(EC[:, :], ES[:, :]), "rc")
            L["v_rt"].wait(eng, n, "rc")
            L["v_rt"].inc(eng.tensor_scalar(PR[:, :], EX[:, :], EC[:, 0:1], None, ALU.mult), "p")
            L["v_rt"].wait(eng, n, "p")
            pf = PR[:, :].unsqueeze(1).broadcast_to([P, E, E])
            pe = PR[:, :].unsqueeze(2).broadcast_to([P, E, E])
            L["v_rt"].inc(eng.tensor_tensor(EQ[:, :, :], pf, pe, ALU.is_equal), "eq")
            L["v_rt"].inc(eng.tensor_tensor(GT[:, :, :], pf, pe, ALU.is_gt), "gt")

        def dve_rt3(eng, n):
            L["g_rt"].wait(eng, n, "bp")
            L["v_rt"].inc(eng.tensor_reduce(CUM[:, :], EQ[:, :, :], AX.X, ALU.add), "cum")
            L["v_rt"].wait(eng, n, "cum")
            L["v_rt"].inc(eng.scalar_tensor_tensor(WT[:, (n // BT) % (NT // BT), n % BT, :], CUM[:, :], TOP_P, PR[:, :],
                                                   ALU.is_le, ALU.mult), "wt")

        def dve_wp1(eng, n, x):
            e = 2 * (n - 3) + x
            for j in range(3):
                eng.wait_ge(s_w[j], 16 * (e + 1))
                L["v_wp"].inc(eng.tensor_reduce(MXW[:, j:j + 1], stage[:, j, :], AX.X, ALU.max,
                                                apply_absolute_value=True), f"mx.{j}.{x}")
            L["g_wp"].wait(eng, n, f"ar{x}")
            L["v_wp"].inc(eng.tensor_scalar(MAW[:, :], MAW[:, :], 1e-30, None, ALU.max), f"cl{x}")
            L["v_wp"].wait(eng, n, f"cl{x}")
            L["v_wp"].inc(eng.tensor_scalar(PEW[:, :].bitcast(I32), MAW[:, :].bitcast(I32), 0x7F800000, None,
                                            ALU.bitwise_and), f"pe{x}")
            L["v_wp"].wait(eng, n, f"pe{x}")
            L["v_wp"].inc(eng.reciprocal(SCW[:, :], PEW[:, :]), f"rc{x}")
            L["v_wp"].wait(eng, n, f"rc{x}")
            L["v_wp"].inc(eng.tensor_scalar(SCW[:, :], SCW[:, :], 2.0 ** WTOP, None, ALU.mult), f"sc{x}")
            L["v_wp"].inc(eng.tensor_scalar(TSC[:, e, :], PEW[:, 0:1], TANH_C, None, ALU.mult), f"tsc{x}")
            L["v_wp"].inc(eng.tensor_tensor(GUD[:, :], PEW[:, 0:1], PEW[:, 1:2], ALU.mult), f"gu{x}")
            L["v_wp"].wait(eng, n, f"gu{x}")
            L["v_wp"].inc(eng.tensor_scalar(CF[:, e, :], GUD[:, :], PEW[:, 2:3], CF_C, ALU.mult, ALU.mult), f"cf{x}")

        def dve_wp2(eng, n, x):
            e = 2 * (n - 3) + x
            for j in range(3):
                L["a_wp"].wait(eng, n, f"hi{x}.{j}")
                L["v_wp"].inc(eng.scalar_tensor_tensor(W[:, e, 1, j, :], stage[:, j, :], SCW[:, j:j + 1], W[:, e, 0, j, :],
                                                       ALU.mult, ALU.subtract), f"lo.{j}.{x}")

        def dve_qb(eng, n):
            L["p_ap"].wait(eng, n, "qkv")
            L["g_ap"].wait(eng, n - 1, "v3")
            L["v_ap"].inc(eng.tensor_tensor(QKV[:, :], BA[:, 0:QKVW], BQKV[:, :], ALU.add), "qb")
            L["g_ap"].wait(eng, n, "sq")
            L["v_ap"].inc(eng.tensor_reduce(SS[:, :], SQ[:, :].rearrange("p (h c) -> p h c", c=HD), AX.X, ALU.add), "ss")
            L["v_ap"].wait(eng, n, "ss")
            L["v_ap"].inc(eng.tensor_scalar(MS[:, :], SS[:, :], 1.0 / HD, RMS_EPS, ALU.mult, ALU.add), "ms")

        def dve_rope(eng, n):
            c = n % 2
            L["g_ap"].wait(eng, n, "sg")
            q3 = QN[:, :].rearrange("p (h c) -> p h c", c=HD)
            L["v_ap"].inc(eng.tensor_tensor(q3, QKV[:, 0:QK * HD].rearrange("p (h c) -> p h c", c=HD),
                                            RR[:, :].unsqueeze(2).broadcast_to([P, QK, HD]), ALU.mult), "qn")
            L["v_ap"].wait(eng, n, "qn")
            q4 = QN[:, :].rearrange("p (h a c) -> p h a c", a=2, c=HD // 2)
            for a, table in ((0, SIN), (1, NSIN)):
                L["v_ap"].inc(eng.tensor_tensor(RB[:, :, a, :], q4[:, :, 1 - a, :],
                                                table[:, c, :].unsqueeze(1).broadcast_to([P, QK, HD // 2]), ALU.mult), f"rb{a}")
            L["v_ap"].wait(eng, n, "rb1")
            L["g_ap"].wait(eng, n, "ra")
            L["v_ap"].inc(eng.tensor_tensor(RA[:, :], RA[:, :], RB[:, :, :, :].rearrange("p h a c -> p (h a c)"), ALU.add), "r")

        def dve_lo(eng, n):
            q = RA[:, 0:H * HD].rearrange("p (h c) -> p h c", c=HD)
            k = RA[:, H * HD:].rearrange("p (h c) -> p h c", c=HD)
            L["a_ap"].wait(eng, n, "qhi")
            L["v_ap"].inc(eng.tensor_tensor(QS[:, :, 1:4:2, :], q.unsqueeze(2).broadcast_to([P, H, 2, HD]),
                                            QS[:, :, 0:4:2, :], ALU.subtract), "qlo")
            L["a_ap"].wait(eng, n, "khi1")
            for s in range(2):
                L["v_ap"].inc(eng.tensor_tensor(KS[:, :, :, 2 + s, :], k.unsqueeze(2).broadcast_to([P, KVH, 2, HD]),
                                                KS[:, :, :, s, :], ALU.subtract), f"klo{s}")

        def dve_ke(eng, n):
            L["p_a3"].wait(eng, n, "kt")
            b16 = BB[:, :].bitcast(F16)[:, 0:KVH * P].rearrange("p (a b) -> p a b", a=KVH)
            par, t = ((n - 9) // 2) % 2, (n + 1) % 2
            for h in range(2):
                lo, hi = h * P // 2, (h + 1) * P // 2
                L["v_a3"].inc(eng.tensor_copy(KT[lo:hi, par, :, h, t, :], b16[lo:hi, :, :]), f"ke{h}")

        def dve_max(eng, n, it):
            kv = 2 * (n % 2) + it
            L["p_hd"].wait(eng, n, f"sa{it}")
            L["v_hd"].inc(eng.tensor_reduce(MX[:, 0, :], BA[:, :].rearrange("p (g k) -> p g k", g=G), AX.X, ALU.max), f"mx{it}.0")
            L["p_hd"].wait(eng, n, f"sb{it}")
            for j, bank in ((0, BB), (1, BC)):
                L["v_hd"].inc(eng.tensor_reduce(MX[:, 1, 2 * j:2 * j + 2], bank[:, :].rearrange("p (g k) -> p g k", g=2),
                                                AX.X, ALU.max), f"mx{it}.{j + 1}")
            L["v_hd"].wait(eng, n, f"mx{it}.2")
            L["a_hd"].wait(eng, n if it else n - 1, "e0.7" if it else "e1.7")
            L["v_hd"].inc(eng.scalar_tensor_tensor(NB[:, :, :], MX[:, :, :], -1.0,
                                                   AG[:, kv, :].unsqueeze(1).broadcast_to([P, 2, G]), ALU.mult, ALU.mult), f"nb{it}")

        def dve_pl(eng, n, lane, prefix, alane, aprefix):
            for b, bank in enumerate((BA, BB, BC)):
                L[alane].wait(eng, n, f"{aprefix}{b}")
                L[lane].inc(eng.tensor_tensor(PL[:, b, :, :].rearrange("p a b -> p (a b)"), bank[:, :],
                                              PH[:, b, :, :].rearrange("p a b -> p (a b)"), ALU.subtract), f"{prefix}{b}")

        def dve_norm(eng, n, lane, sfx, plane, plabel, par, kv):
            o = BC[:, 0:2 * G * VW].rearrange("p (g c) -> p g c", c=VW)
            L[plane].wait(eng, n, plabel)
            L[lane].inc(eng.reciprocal(RC[:, :], o[:, :, VW - 1]), f"rc{sfx}")
            L[lane].inc(eng.tensor_reduce(RD[:, :, :], o[:, :, 0:3 * HD].rearrange("p g (s c) -> p g c s", s=3), AX.X, ALU.add),
                        f"rd{sfx}")
            L[lane].wait(eng, n, f"rd{sfx}")
            L["g_op"].wait(eng, n - 1, "os") if not (isinstance(n, int) and n < 13) else None
            L[lane].inc(eng.tensor_tensor(OB[:, par, :, kv, :].rearrange("p t (g c) -> p t g c", c=HD),
                                          RD[:, :, :].rearrange("p (t g) c -> p t g c", t=2),
                                          RC[:, :].rearrange("p (t g) -> p t g", t=2).unsqueeze(3).broadcast_to([P, 2, G, HD]),
                                          ALU.mult), f"ob{sfx}")

        def dve_op(eng, n):
            L["p_op"].wait(eng, n, "mm")
            L["g_al"].wait(eng, n - 4, "bo")
            x = X[:, n - 12, :]
            L["v_op"].inc(eng.tensor_tensor(x, BB[:, 0:D], x, ALU.add), "ad")

        def dve_fp_ln(eng, n, act=()):
            if isinstance(n, int) and n < 16:
                eng.wait_ge(s_x0, 16) if n < 4 else eng.wait_ge(s_x1, 16 * (NT // BT - 1))
            if "op" in act:
                L["v_op"].wait(eng, n - 1, "ad")
            elif "ff" in act and "ap" not in act and "hd" not in act and "wp" not in act and not (isinstance(n, int) and n < 28):
                L["v_op"].wait(eng, n - 4, "ad")
            dve_ln(eng, n, "v_ln", "g_ln", "f", n % NT, "p_fp")

        def dve_body(eng, n, act):
            for p in range(16):
                i = p // 2
                if p % 8 == 0:
                    dve_wc(eng, n, act, p // 8)
                if p % 2 == 0:
                    dve_gu(eng, n, i)
                elif not (isinstance(n, int) and n == 4 and i < 4):
                    dve_y(eng, n, i)
                if p == 0 and "pw" in act:
                    dve_pl(eng, n, "v_pw", "l", "a_pw", "h")
                if p == 0 and "fp" in act:
                    dve_fp_ln(eng, n, act)
                if p == 1 and "a3" in act:
                    dve_ke(eng, n)
                if p == 2 and "pw" in act:
                    dve_norm(eng, n, "v_pw", "", "p_pw", "pv", ((n - 11) // 2) % 2, 2 * ((n + 1) % 2) + 1)
                if p == 3 and "fp" in act:
                    dve_split(eng, n)
                if p == 3 and "hd" in act:
                    dve_max(eng, n, 0)
                if p == 2 and "wp" in act:
                    dve_wp1(eng, n, 0)
                if p == 5 and "wp" in act:
                    dve_wp2(eng, n, 0)
                if p == 5 and "ap" in act:
                    L["v_y"].wait(eng, n, "y2")
                    dve_ln(eng, n, "v_al", "g_al", "a", n - 8, "p_ap")
                if p == 7 and "hd" in act:
                    dve_pl(eng, n, "v_hd", "l0.", "a_hd", "h0.")
                if p == 10 and "hd" in act:
                    dve_norm(eng, n, "v_hd", "0", "p_hd", "pv0", ((n - 10) // 2) % 2, 2 * (n % 2))
                if p == 10 and "wp" in act:
                    dve_wp1(eng, n, 1)
                if p == 13 and "wp" in act:
                    dve_wp2(eng, n, 1)
                if p == 11 and "ap" in act:
                    dve_qb(eng, n)
                if p == 11 and "op" in act:
                    dve_op(eng, n)
                if p == 12 and "fp" in act:
                    dve_rt1(eng, n)
                if p == 12 and "hd" in act:
                    dve_max(eng, n, 1)
                if p == 13 and "fp" in act:
                    dve_rt2(eng, n)
                if p == 13 and "ap" in act:
                    dve_rope(eng, n)
                if p == 15 and "fp" in act:
                    dve_rt3(eng, n)
                if p == 15 and "ap" in act:
                    dve_lo(eng, n)

        def pool_lo(eng, n, i):
            h, m = divmod(i, 4)
            L["a_ff"].wait(eng, n, f"hi{i}")
            L["g_ff"].inc(eng.tensor_tensor(HS[:, h, 1, m, :], H32[:, i % 2, :], HS[:, h, 0, m, :], ALU.subtract), f"lo{i}")

        def pool_rs(eng, n, vlane, glane, k):
            _, _, VE, RS, _, _ = LN[k]
            L[vlane].wait(eng, n, "eps")
            L[glane].inc(eng.tensor_tensor(RS[:, :], VE[:, :], MH[:, 0:1], ALU.pow), "rs")

        def pool_rank(eng, n):
            L["v_rt"].wait(eng, n, "gt")
            L["g_rt"].inc(eng.tensor_tensor(EQ[:, :, :], EQ[:, :, :], LOW[:, :, :], ALU.mult), "eq")
            L["g_rt"].wait(eng, n, "eq")
            L["g_rt"].inc(eng.tensor_tensor(EQ[:, :, :], EQ[:, :, :], GT[:, :, :], ALU.add), "b")
            L["g_rt"].wait(eng, n, "b")
            L["g_rt"].inc(eng.tensor_tensor(EQ[:, :, :], EQ[:, :, :], PR[:, :].unsqueeze(1).broadcast_to([P, E, E]), ALU.mult), "bp")

        def pool_wp(eng, n, x):
            wait_apart(L["v_wp"], eng, n, f"mx.2.{x}")
            L["g_wp"].inc(eng.partition_all_reduce(MAW[:, :], MXW[:, :], P, bass.bass_isa.ReduceOp.max), f"ar{x}")

        def pool_ap1(eng, n):
            pool_rs(eng, n, "v_al", "g_al", "a")
            wait_apart(L["v_al"], eng, n, "xn")
            x = X[:, n - 8, :]
            L["g_al"].inc(eng.tensor_tensor(x, x, BO[:, :], ALU.add), "bo")

        def pool_ap2(eng, n):
            L["v_ap"].wait(eng, n, "qb")
            L["g_ap"].inc(eng.tensor_tensor(SQ[:, :], QKV[:, 0:QK * HD], QKV[:, 0:QK * HD], ALU.mult), "sq")
            L["v_ap"].wait(eng, n, "ms")
            L["g_ap"].inc(eng.tensor_tensor(RR[:, :], MS[:, :], MH[:, :], ALU.pow), "rr")
            L["g_ap"].wait(eng, n, "rr")
            L["g_ap"].inc(eng.tensor_tensor(RR[:, 0:H], RR[:, 0:H], SGN[:, :], ALU.mult), "sg")

        def pool_ap3(eng, n):
            L["v_ap"].wait(eng, n, "qn")
            L["v_ap"].wait(eng, n - 1, "klo1")
            L["a_ap"].wait(eng, n - 1, "khi1")
            c8 = HD // 2
            L["g_ap"].inc(eng.tensor_tensor(RA[:, :].rearrange("p (h c) -> p h c", c=c8), QN[:, :].rearrange("p (h c) -> p h c", c=c8),
                                            COS[:, n % 2, :].unsqueeze(1).broadcast_to([P, 2 * QK, c8]), ALU.mult), "ra")
            v = QKV[:, QK * HD:].rearrange("p (h c) -> p h c", c=HD)
            vs = VS[:, ((n - 8) // 2) % 2, n % 2, :, :]
            L["g_ap"].inc(eng.tensor_copy(vs[:, :, 0:HD], v), "v1")
            wait_apart(L["g_ap"], eng, n, "v1")
            L["g_ap"].inc(eng.tensor_tensor(VR[:, 0, :, :], v, vs[:, :, 0:HD], ALU.subtract), "r1")
            L["g_ap"].wait(eng, n, "r1")
            L["g_ap"].inc(eng.tensor_copy(vs[:, :, HD:2 * HD], VR[:, 0, :, :]), "v2")
            wait_apart(L["g_ap"], eng, n, "v2")
            L["g_ap"].inc(eng.tensor_tensor(VR[:, 1, :, :], VR[:, 0, :, :], vs[:, :, HD:2 * HD], ALU.subtract), "r2")
            L["g_ap"].wait(eng, n, "r2")
            L["g_ap"].inc(eng.tensor_copy(vs[:, :, 2 * HD:3 * HD], VR[:, 1, :, :]), "v3")

        def pool_os(eng, n):
            if isinstance(n, int) and n > 26:
                L["v_pw"].wait(eng, 26, "ob")
            else:
                L["v_pw"].wait(eng, n, "ob")
            L["p_op"].wait(eng, n - 1, "tp")
            L["g_op"].inc(eng.tensor_copy(OS[:, :], OB[:, ((n - 12) // 2) % 2, n % 2, :, :].rearrange("p a b -> p (a b)")), "os")

        def pool_mask(eng, n, it):
            for j, (b, e) in enumerate(((0, 3), (2, 7))):
                wait_apart(L["a_hd"], eng, n, f"e{it}.{e}")
                L["g_hd"].inc(eng.affine_select(out=P32[:, b, :, :], in_=P32[:, b, :, :], compare_op=ALU.is_ge, fill=0.0,
                                                base=0, pattern=[[0, G], [-1, P]], channel_multiplier=1), f"k{it}.{j}")

        def pool_body(eng, n, act):
            for p in range(16):
                i = p // 2
                if p == 0 and "fp" in act:
                    pool_rs(eng, n, "v_ln", "g_ln", "f")
                if p == 2 and "wp" in act:
                    pool_wp(eng, n, 0)
                if p == 10 and "wp" in act:
                    pool_wp(eng, n, 1)
                if p == 4 and "op" in act:
                    pool_os(eng, n)
                if p == 5 and "hd" in act:
                    pool_mask(eng, n, 0)
                if p == 5 and "ap" in act:
                    pool_ap1(eng, n)
                if p == 11 and "ap" in act:
                    pool_ap2(eng, n)
                if p == 13 and "fp" in act:
                    pool_rank(eng, n)
                if p == 13 and "ap" in act:
                    pool_ap3(eng, n)
                if p == 14 and "hd" in act:
                    pool_mask(eng, n, 1)
                if p % 2 == 1:
                    pool_lo(eng, n, i)

        block = ctx.enter_context(nc.Block())

        @block.sync
        def _(eng):
            xt = d["x"].rearrange("(n p) d -> p n d", p=P)
            eng.dma_start(X[:, 0:BT, :], xt[:, 0:BT, :]).then_inc(s_x0, 16)

            def load_expert(e):
                for j, w in enumerate(("gate", "up", "down")):
                    eng.dma_start(stage[:, j, :], d[w][e]).then_inc(s_w[j], 16)

            load_expert(0)
            for b in range(1, NT // BT):
                eng.dma_start(X[:, b * BT:(b + 1) * BT, :], xt[:, b * BT:(b + 1) * BT, :]).then_inc(s_x1, 16)
            for e in range(1, E):
                n, x = (e - 1) // 2 + 3, (e - 1) % 2
                for j, w in enumerate(("gate", "up", "down")):
                    L["v_wp"].wait(eng, n, f"lo.{j}.{x}")
                    eng.dma_start(stage[:, j, :], d[w][e]).then_inc(s_w[j], 16)

            def store(n, t):
                L["v_y"].wait(eng, n, "y3")
                eng.dma_start(d["out"][t, :, :], X[:, t, :]).then_inc(s_st, 16)

            for a, b in RUNS:
                if "st" in active(a):
                    if b - a == 1:
                        store(a, a - 24)
                    else:
                        with eng.Fori(a, b) as n:
                            store(n, n - 24)
            for t in range(NT - BT, NT):
                L["v_y"].wait(eng, 36, "y3")
                eng.dma_start(d["out"][t, :, :], X[:, t, :]).then_inc(s_st, 16)
            eng.wait_ge(s_st, 16 * NT)

        @block.gpsimd
        def _(eng):
            give_credit(eng, "g_")
            eng.memset(ident[:, :], 0.0).then_inc(s_i1, 1)
            eng.memset(MH[:, :], -0.5).then_inc(s_i1, 1)
            eng.memset(LOW[:, :, :], 1.0).then_inc(s_i1, 1)
            eng.memset(ident16[:, :], 0.0).then_inc(s_i1, 1)
            eng.memset(MB[:, :, :], 0.0).then_inc(s_i1, 1)
            eng.wait_ge(s_i1, 5)
            for t in (ident, ident16):
                eng.affine_select(out=t[:, :], in_=t[:, :], compare_op=ALU.not_equal, fill=1.0, base=0,
                                  pattern=[[-1, P]], channel_multiplier=1).then_inc(s_i1, 1)
            eng.affine_select(out=LOW[:, :, :], in_=LOW[:, :, :], compare_op=ALU.is_ge, fill=0.0, base=-1,
                              pattern=[[1, E], [-1, E]], channel_multiplier=0).then_inc(s_i1, 1)
            eng.wait_ge(s_i1, N_I1)
            for n in range(4):
                pool_rs(eng, n, "v_ln", "g_ln", "f")
                pool_rank(eng, n)
            for x in items:
                pool_wp(eng, 3, x)
            eng.affine_select(out=MB[:, :, :], in_=MB[:, :, :], compare_op=ALU.is_ge, fill=MASKED, base=0,
                              pattern=[[0, G], [-1, P]], channel_multiplier=1).then_inc(s_i2, 1)
            eng.memset(KT[:, :, :, :, :, :], 0.0).then_inc(s_i2, 1)
            eng.memset(VS[:, :, :, :, :], 1.0).then_inc(s_i2, 1)
            eng.wait_ge(s_i2, 3)
            eng.wait_ge(s_aw, 16 * 11)
            eng.wait_ge(s_ag, 4)
            steps(eng, lambda n, act: pool_body(eng, n, act))

        @block.scalar
        def _(eng):
            give_credit(eng, "a_")
            bc = lambda v: v.rearrange("(a n) -> a n", a=1).broadcast_to([P, v.shape[0]])
            eng.dma_start(RW[:, :, :], d["rw"]).then_inc(s_rw, 16)
            c = 0
            for w, width in (("wq", D), ("wk", KVH * HD), ("wv", KVH * HD)):
                eng.dma_start(WQKV[:, :, c:c + width], d[w]).then_inc(s_aw, 16)
                eng.dma_start(BQKV[:, c:c + width], bc(d["b" + w[1]])).then_inc(s_aw, 16)
                c += width
            eng.dma_start(WO[:, :, :], d["wo"]).then_inc(s_aw, 16)
            eng.dma_start(BO[:, :], bc(d["bo"])).then_inc(s_aw, 16)
            eng.dma_start(GN[:, :], bc(d["gain"])).then_inc(s_aw, 16)
            eng.dma_start(COS[:, :, :], d["cos"]).then_inc(s_aw, 16)
            eng.dma_start(SIN[:, :, :], d["sin"]).then_inc(s_aw, 16)
            for n in range(4):
                act_xt(eng, n)
                act_rt(eng, n)
            for x in items:
                act_wp(eng, 3, x)
            eng.wait_ge(s_ag, 4)
            steps(eng, lambda n, act: act_body(eng, n, act))

        @block.vector
        def _(eng):
            give_credit(eng, "v_")
            eng.wait_ge(s_i1, N_I1)
            for n in range(4):
                dve_fp_ln(eng, n)
                dve_split(eng, n)
                dve_rt1(eng, n)
                dve_rt2(eng, n)
                dve_rt3(eng, n)
            for x in items:
                dve_wp1(eng, 3, x)
                dve_wp2(eng, 3, x)
            eng.wait_ge(s_aw, 16 * 11)
            eng.tensor_scalar(SGN[:, :], GN[:, :], 0.0, 2.0, ALU.is_ge, ALU.mult).then_inc(s_ag, 1)
            eng.tensor_scalar(NSIN[:, :, :], SIN[:, :, :], -1.0, None, ALU.mult).then_inc(s_ag, 1)
            eng.wait_ge(s_ag, 1)
            eng.tensor_scalar(SGN[:, :], SGN[:, :], -1.0, None, ALU.add).then_inc(s_ag, 1)
            eng.wait_ge(s_ag, 3)
            eng.scalar_tensor_tensor(AG[:, :, :].rearrange("p a b -> p (a b)"), GN[:, :], float(HD) ** -0.5, SGN[:, :],
                                     ALU.mult, ALU.mult).then_inc(s_ag, 1)
            eng.wait_ge(s_ag, 4)
            steps(eng, lambda n, act: dve_body(eng, n, act))
            for m in range(4):
                dve_y(eng, 36, m)

        @block.tensor
        def _(eng):
            give_credit(eng, "p_")
            eng.wait_ge(s_i1, N_I1)
            eng.wait_ge(s_rw, 16)
            for n in range(4):
                pe_fp_tp(eng, n, active(n))
                pe_fp_lg(eng, n, active(n))
            steps(eng, lambda n, act: pe_body(eng, n, act))
            for m in range(4):
                pe_y(eng, 36, m)


def kernel(**inputs):
    import numpy as np
    import concourse.bacc as bacc
    from concourse.bass_utils import run_bass_kernel_spmd as run

    def ktile(w):
        return np.ascontiguousarray(w.T.reshape(-1, P, w.shape[0]).transpose(1, 0, 2))

    def experts(w):
        return np.ascontiguousarray(np.stack([ktile(w[e]).reshape(P, -1) for e in range(E)]))

    f = {k: np.asarray(v) for k, v in inputs.items()}
    a, m = "L0_attn_", "L0_ffn_"
    t = np.arange(S, dtype=np.float32)
    inv = (1.0 / 10000.0 ** (np.arange(0, HD, 2, dtype=np.float32) / HD)).astype(np.float32)
    freqs = np.outer(t, inv).astype(np.float32)
    rope = lambda z: np.ascontiguousarray(z.astype(np.float32).reshape(2, P, HD // 2).transpose(1, 0, 2))
    arrays = {
        "x": f[a + "x"].reshape(B * S, D),
        "gate": experts(f[m + "gate_w"]), "up": experts(f[m + "up_w"]), "down": experts(f[m + "down_w"]),
        "rw": ktile(f[m + "router_w"]),
        "wq": ktile(f[a + "Wq"]), "wk": ktile(f[a + "Wk"]), "wv": ktile(f[a + "Wv"]), "wo": ktile(f[a + "Wo"]),
        "bq": f[a + "bq"], "bk": f[a + "bk"], "bv": f[a + "bv"], "bo": f[a + "bo"], "gain": f[a + "q_gain"],
        "cos": rope(np.cos(freqs)), "sin": rope(np.sin(freqs)),
    }
    nc = bacc.Bacc("TRN2", target_bir_lowering=False, num_devices=1)
    aps = {k: nc.dram_tensor(f"in_{k}", v.shape, mybir.dt.from_np(v.dtype), kind="ExternalInput").ap()
           for k, v in arrays.items()}
    aps["out"] = nc.dram_tensor("out_y", (NT, P, D), F32, kind="ExternalOutput").ap()
    build(nc, aps)
    r = run(nc, [{f"in_{k}": v for k, v in arrays.items()}], core_ids=[0])
    return r.results[0]["out_y"].reshape(B, S, D)
```

```python
from contextlib import ExitStack

import concourse.bass as bass
from concourse import mybir

F32, F16, BF16 = mybir.dt.float32, mybir.dt.float16, mybir.dt.bfloat16
I32 = mybir.dt.int32
ALU, ACT, AX = mybir.AluOpType, mybir.ActivationFunctionType, mybir.AxisListType

P = 128
B, S, D = 8, 256, 256
H, KVH = 16, 4
HD = D // H
E, I = 8, 512
TOP_P = 0.9
LN_EPS = 1e-5
RMS_EPS = 1.1920929e-07
NT = B * S // P
BT = 4
BLK = BT * P
KD = D // P
KI = I // P
QKVW = D + 2 * KVH * HD
QK = H + KVH
G = H // KVH
W3 = KD * I
VW = 3 * HD + 1

XS = 1024.0
WTOP = 14
TANH_C = 0.5 * 2.0 ** -WTOP / XS
H_C = 2.0 ** (-3 - 1 - 2 * WTOP - 20)
CF_C = 0.5 * 2.0 ** (3 - WTOP)
MASKED = -64.0

RANGES = {"fp": (0, 31), "wp": (3, 7), "ff": (4, 35), "ap": (8, 23), "qk": (9, 24), "a3": (10, 25), "hd": (12, 27),
          "pw": (13, 28), "os": (14, 29), "op": (15, 30), "st": (24, 35)}
CUTS = sorted({n for a, b in RANGES.values() for n in (a, b + 1) if n >= 4} | {5, 7})
RUNS = list(zip(CUTS, CUTS[1:]))


def active(n):
    return {f for f, (a, b) in RANGES.items() if a <= n <= b}


class Lane:

    def __init__(self, sem, stage, labels, extra=0):
        self.sem, self.labels = sem, labels
        self.first = RANGES[stage][0]
        self.per = len(labels)
        self.credit = self.per + extra

    def inc(self, instr, label):
        assert label in self.labels
        instr.then_inc(self.sem, 1)

    def value(self, n, label):
        return self.per * (n - self.first + 1) + self.labels.index(label) + 1

    def wait(self, eng, n, label):
        eng.wait_ge(self.sem, self.value(n, label))


BANK_USES = [
    ("qk", {"A": ("v_qk", "qb")}),
    ("op", {"B": ("a_op", "ot")}),
    ("pw", {"C": ("v_pw", "rd")}),
    ("hd", {"A": ("a_hd", "e0.3"), "B": ("a_hd", "e0.7"), "C": ("a_hd", "e0.7")}),
    ("fp", {"A": ("a_xt", "xt")}),
    ("ap", {"A": ("a_ap", "xt")}),
    ("hd", {"A": ("v_hd", "l0.0"), "B": ("v_hd", "l0.1"), "C": ("v_hd", "l0.2")}),
    ("a3", {"A": ("a_a3", "qe"), "B": ("v_a3", "ke1")}),
    ("op", {"B": ("v_op", "ad")}),
    ("hd", {"C": ("v_hd", "rd0")}),
    ("hd", {"A": ("a_hd", "e1.3"), "B": ("a_hd", "e1.7"), "C": ("a_hd", "e1.7")}),
    ("fp", {"A": ("a_rt", "ex")}),
    ("hd", {"A": ("v_hd", "l1.0"), "B": ("v_hd", "l1.1"), "C": ("v_hd", "l1.2")}),
]
USE = {"qk": 0, "op.tp": 1, "pw": 2, "sc0": 3, "fp.tp": 4, "pt0": 6, "a3": 7, "op.mm": 8, "pv0": 9, "sc1": 10,
       "fp.lg": 11, "pt1": 12}


def build(nc, d):
    with ExitStack() as ctx:
        def sb(name, shape, dt):
            return ctx.enter_context(nc.sbuf_tensor(name, shape, dt))

        def sem(name):
            return ctx.enter_context(nc.semaphore(name))

        X = sb("X", [P, NT, D], F32)
        W = sb("W", [P, E, 2, 3, W3], F16)
        room = sb("room", [P, 3 * W3], F32)
        stage = room[:, :].rearrange("p (j w) -> p j w", j=3)
        NP3 = 3 * G * P
        P32 = room[:, 0:NP3].rearrange("p (b g k) -> p b g k", b=3, g=G)
        PH, PL = (room[:, NP3 + j * NP3 // 2:NP3 + (j + 1) * NP3 // 2].bitcast(F16).rearrange(
            "p (b g k) -> p b g k", b=3, g=G) for j in range(2))
        XS16 = sb("XS16", [P, 2, 2, KD, BT, P], F16)
        HS = sb("HS", [P, 2, 2, KI, BLK], F16)
        TS = sb("TS", [P, 2, BLK], F32)
        H32 = sb("H32", [P, 2, BLK], F32)
        WT = sb("WT", [P, NT // BT, BT, E], F32)
        WTC = sb("WTC", [P, 2, BT], F32)
        MXW = sb("MXW", [P, 3], F32)
        MAW = sb("MAW", [P, 3], F32)
        PEW = sb("PEW", [P, 3], F32)
        SCW = sb("SCW", [P, 3], F32)
        GUD = sb("GUD", [P, 1], F32)
        TSC = sb("TSC", [P, E, 1], F32)
        CF = sb("CF", [P, E, 1], F32)
        RW = sb("RW", [P, KD, E], F32)
        WQKV = sb("WQKV", [P, KD, QKVW], F32)
        WO = sb("WO", [P, KD, D], F32)
        BQKV = sb("BQKV", [P, QKVW], F32)
        BO = sb("BO", [P, D], F32)
        GN = sb("GN", [P, H], F32)
        AG = sb("AG", [P, KVH, G], F32)
        SGN = sb("SGN", [P, H], F32)
        COS = sb("COS", [P, 2, HD // 2], F32)
        SIN = sb("SIN", [P, 2, HD // 2], F32)
        NSIN = sb("NSIN", [P, 2, HD // 2], F32)
        ident = sb("ident", [P, P], F32)
        ident16 = sb("ident16", [P, P], F16)
        MB = sb("MB", [P, G, P], F16)
        LOW = sb("LOW", [P, E, E], F32)
        MH = sb("MH", [P, QK], F32)
        LN = {k: (sb(f"ST{k}", [P, 6], F32), sb(f"MV{k}", [P, 2], F32), sb(f"VE{k}", [P, 1], F32),
                  sb(f"RS{k}", [P, 1], F32), sb(f"XN{k}", [P, D], F32), sb(f"XT{k}", [P, KD, P], F32))
              for k in ("f", "a")}
        NM = sb("NM", [P, 1], F32)
        EX = sb("EX", [P, E], F32)
        ES = sb("ES", [P, 1], F32)
        EC = sb("EC", [P, 1], F32)
        PR = sb("PR", [P, E], F32)
        EQ = sb("EQ", [P, E, E], F32)
        GT = sb("GT", [P, E, E], F32)
        CUM = sb("CUM", [P, E], F32)
        QKV = sb("QKV", [P, QKVW], F32)
        SQ = sb("SQ", [P, QK * HD], F32)
        SS = sb("SS", [P, QK], F32)
        MS = sb("MS", [P, QK], F32)
        RR = sb("RR", [P, QK], F32)
        QN = sb("QN", [P, QK * HD], F32)
        RA = sb("RA", [P, QK * HD], F32)
        RB = sb("RB", [P, QK, 2, HD // 2], F32)
        QS = sb("QS", [P, H, 4, HD], F16)
        KS = sb("KS", [P, KVH, 2, 4, HD], F16)
        VR = sb("VR", [P, 2, KVH, HD], F32)
        VS = sb("VS", [P, 3, 2, KVH, VW], BF16)
        QT = sb("QT", [P, 2, 2, H // 2, P], F16)
        KT = sb("KT", [P, 2, KVH, 2, 2, P], F16)
        MX = sb("MX", [P, 2, G], F32)
        NB = sb("NB", [P, 2, G], F32)
        RC = sb("RC", [P, 2 * G], F32)
        RD = sb("RD", [P, 2 * G, HD], F32)
        OB = sb("OB", [P, 2, 2, KVH, G * HD], F32)
        OS = sb("OS", [P, D], F32)
        OT = sb("OT", [P, KD, P], F32)

        GB = [ctx.enter_context(nc.psum_tensor(f"G{i}", [P, BLK], F32)) for i in range(2)]
        UB = [ctx.enter_context(nc.psum_tensor(f"U{i}", [P, BLK], F32)) for i in range(2)]
        YB = ctx.enter_context(nc.psum_tensor("YB", [P, BLK], F32))
        BA, BB, BC = (ctx.enter_context(nc.psum_tensor(f"B{c}", [P, BLK], F32)) for c in "ABC")

        s_x0, s_x1 = sem("s_x0"), sem("s_x1")
        s_rw, s_aw = sem("s_rw"), sem("s_aw")
        s_w = [sem(f"s_w{j}") for j in range(3)]
        s_i1, s_i2 = sem("s_i1"), sem("s_i2")
        s_ag, s_apart = sem("s_ag"), sem("s_apart")
        N_I1 = 8
        s_st = sem("s_st")

        items = range(2)
        L = {}
        for name, stage_, labels in [
            ("p_gu", "ff", [f"gu{i}" for i in range(8)]),
            ("p_y", "ff", [f"y{i}" for i in range(8)]),
            ("p_fp", "fp", ["tp"]), ("p_lg", "fp", ["lg"]),
            ("p_ap", "ap", ["tp"]), ("p_qk", "qk", ["qkv"]), ("p_a3", "a3", ["qt", "kt"]),
            ("p_hd", "hd", ["sa0", "sb0", "pt0.0", "pt0.1", "pt0.2", "pv0", "sa1", "sb1", "pt1.0", "pt1.1", "pt1.2"]),
            ("p_pw", "pw", ["pv"]), ("p_op", "op", ["tp", "mm"]),
            ("a_ff", "ff", [f"{s}{i}" for i in range(8) for s in ("tanh", "hi")]),
            ("a_xt", "fp", ["xt"]), ("a_rt", "fp", ["ex"]),
            ("a_wp", "wp", [f"{s}{x}.{j}" for x in items for s, j in (("hi", 0), ("sc", 0), ("hi", 1), ("hi", 2))]),
            ("a_ap", "ap", ["xt"]), ("a_a3", "a3", ["qhi", "khi0", "khi1", "qe"]),
            ("a_hd", "hd", [f"{s}{x}.{i}" for x in items for s, c in (("e", 8), ("h", 3)) for i in range(c)]),
            ("a_op", "op", ["ot"]),
            ("v_ff", "ff", [f"{s}{i}" for i in range(8) for s in ("t", "h")]),
            ("v_y", "ff", [f"y{i}" for i in range(8)]), ("v_wc", "ff", ["wc0", "wc1"]),
            ("v_ln", "fp", ["stats", "aggr", "eps", "xn"]), ("v_sp", "fp", ["xh", "xl"]),
            ("v_rt", "fp", ["mx", "rc", "p", "eq", "gt", "cum", "wt"]),
            ("v_wp", "wp", [f"{s}{x}" for x in items for s in ("mx.0.", "mx.1.", "mx.2.", "cl", "pe", "rc", "sc", "tsc", "gu", "cf", "lo.1.", "lo.2.")]),
            ("v_al", "ap", ["stats", "aggr", "eps", "xn"]),
            ("v_qk", "qk", ["qb", "ss", "ms"]),
            ("v_a3", "a3", ["qn", "rb0", "rb1", "r", "qlo", "klo0", "klo1", "ke0", "ke1"]),
            ("v_hd", "hd", ["mx0.0", "mx0.1", "nb0.0", "mx0.2", "nb0.1", "l0.0", "l0.1", "l0.2", "rc0", "rd0", "ob0",
                            "mx1.0", "mx1.1", "nb1.0", "mx1.2", "nb1.1", "l1.0", "l1.1", "l1.2"]),
            ("v_pw", "pw", ["rc", "rd", "ob"]), ("v_op", "op", ["ad"]),
            ("g_ff", "ff", [f"lo{i}" for i in range(8)]),
            ("g_ln", "fp", ["rs"]), ("g_rt", "fp", ["eq", "b", "bp"]), ("g_wp", "wp", [f"{s}{x}" for x in items for s in ("ar", "lo.0.")]),
            ("g_al", "ap", ["rs", "bo"]), ("g_qk", "qk", ["sq", "rr", "sg", "v1", "r1", "v2", "r2", "v3"]), ("g_a3", "a3", ["ra"]),
            ("g_os", "os", ["os"]),
            ("g_hd", "hd", ["k0.0", "k0.1", "k1.0", "k1.1"]),
        ]:
            extra = {"p_y": 4, "v_y": 4, "a_wp": 4, "v_wp": 12, "g_wp": 2}.get(name, 0)
            L[name] = Lane(sem(name), stage_, labels, extra)

        def give_credit(eng, prefix):
            for name, lane in L.items():
                if name.startswith(prefix):
                    eng.sem_inc(lane.sem, lane.credit)

        def wait_apart(lane, eng, n, label):
            lane.wait(eng, n, label)
            if not isinstance(n, int):
                eng.sem_inc(s_apart, 1)

        def steps(eng, body):
            for a, b in RUNS:
                if b - a == 1:
                    body(a, active(a))
                else:
                    with eng.Fori(a, b) as n:
                        body(n, active(a))

        def blk(n):
            return ((n - 4) // BT) % (NT // BT)

        def xpar(n):
            return (n // BT + 1) % 2

        def bank_ready(eng, n, act, use, banks="ABC"):
            before = active(n - 1) if isinstance(n, int) else act
            if isinstance(n, int) and n == 4 and use == "fp.tp":
                L["a_rt"].wait(eng, 0, "ex")
                return
            for bank in banks:
                if bank not in BANK_USES[USE[use]][1]:
                    continue
                found = None
                for f, who in reversed(BANK_USES[:USE[use]]):
                    if f in act and bank in who:
                        found = (who[bank], n)
                        break
                if found is None:
                    for f, who in reversed(BANK_USES):
                        if f in before and bank in who:
                            found = (who[bank], n - 1)
                            break
                if found is not None:
                    (lane, label), m = found
                    L[lane].wait(eng, m, label)

        def pe_gu(eng, n, act, i):
            h, m = divmod(i, 4)
            e = (n % 4) * 2 + h
            if i == 0:
                L["v_sp"].wait(eng, n - 1 if "fp" in act else 31, "xl")
            if i % 4 == 0 and "wp" in act:
                L["a_wp"].wait(eng, n if h else n - 1, f"hi{1 - h}.1")
                L["v_wp"].wait(eng, n if h else n - 1, f"lo.1.{1 - h}")
                L["g_wp"].wait(eng, n if h else n - 1, f"lo.0.{1 - h}")
            if i < 2:
                L["v_ff"].wait(eng, n - 1, f"h{i + 6}")
            else:
                L["v_ff"].wait(eng, n, f"h{i - 2}")
            for j, bank in ((0, GB[i % 2]), (1, UB[i % 2])):
                q = 0
                for k in range(KD):
                    for wl, xl in ((0, 0), (0, 1), (1, 0)):
                        mm = eng.matmul(bank[:, :], W[:, e, wl, j, k * I + m * P:k * I + (m + 1) * P],
                                        XS16[:, xpar(n), xl, k, :, :].rearrange("p a b -> p (a b)"),
                                        start=(q == 0), stop=(q == 3 * KD - 1))
                        q += 1
            L["p_gu"].inc(mm, f"gu{i}")

        def pe_y(eng, n, act, i):
            h, m = divmod(i, 4)
            par = 1 - h
            e = (n % 4) * 2 if h else ((n + 3) % 4) * 2 + 1
            if i == 0:
                L["a_ff"].wait(eng, n - 1, "hi7")
            elif i == 4:
                L["a_ff"].wait(eng, n, "hi3")
            if i % 4 == 0 and "wp" in act or isinstance(n, int) and n == 8 and i == 0:
                L["v_wp"].wait(eng, n - 1, f"lo.2.{h}")
            L["v_y"].wait(eng, n - 1 if i == 0 else n, f"y{(i - 1) % 8}")
            if isinstance(n, int) and n == 4:
                L["a_rt"].wait(eng, 3, "ex")
            q = 0
            for hl, wl in ((0, 0), (0, 1), (1, 0)):
                if hl == 1 and i == 0:
                    L["g_ff"].wait(eng, n - 1, "lo7")
                if hl == 1 and i == 4:
                    L["g_ff"].wait(eng, n, "lo3")
                for k in range(KI):
                    mm = eng.matmul(YB[:, 0:D], HS[:, par, hl, k, m * P:(m + 1) * P],
                                    W[:, e, wl, 2, k * D:(k + 1) * D], start=(q == 0), stop=(q == 3 * KI - 1))
                    q += 1
            L["p_y"].inc(mm, f"y{i}")

        def pe_tp(eng, lane, ready, n, k_, bank, c):
            L[ready].wait(eng, n, "xn")
            for k in range(KD):
                mm = eng.transpose(bank[:, c + k * P:c + (k + 1) * P], LN[k_][4][:, k * P:(k + 1) * P], ident[:, :])
            L[lane].inc(mm, "tp")

        def pe_lg(eng, n, bank):
            L["a_xt"].wait(eng, n, "xt")
            for k in range(KD):
                mm = eng.matmul(bank[:, 0:E], LN["f"][5][:, k, :], RW[:, k, :], start=(k == 0), stop=(k == KD - 1))
            L["p_lg"].inc(mm, "lg")

        def pe_qkv(eng, n, act):
            bank_ready(eng, n, act, "qk")
            L["a_ap"].wait(eng, n - 1, "xt")
            for k in range(KD):
                mm = eng.matmul(BA[:, 0:QKVW], LN["a"][5][:, k, :], WQKV[:, k, :], start=(k == 0), stop=(k == KD - 1))
            L["p_qk"].inc(mm, "qkv")

        def pe_a3(eng, n, act):
            bank_ready(eng, n, act, "a3")
            L["v_a3"].wait(eng, n, "klo1")
            L["a_a3"].wait(eng, n, "khi1")
            qs = QS[:, :, :, :].rearrange("p h s c -> p (h s c)")
            ks = KS[:, :, :, :, :].rearrange("p h u s c -> p (h u s c)")
            a16, b16 = BA[:, :].bitcast(F16), BB[:, :].bitcast(F16)
            for j in range(H // 2):
                mm = eng.transpose(a16[:, j * P:(j + 1) * P], qs[:, j * P:(j + 1) * P], ident16[:, :])
            L["p_a3"].inc(mm, "qt")
            for j in range(KVH):
                mm = eng.transpose(b16[:, j * P:(j + 1) * P], ks[:, j * P:(j + 1) * P], ident16[:, :])
            L["p_a3"].inc(mm, "kt")

        def pe_scores(eng, n, act, it):
            par, kv = ((n - 12) // 2) % 2, 2 * (n % 2) + it
            if it == 0:
                L["a_a3"].wait(eng, n - 1 if "a3" in act else 25, "qe")
                L["v_a3"].wait(eng, n - 1 if "a3" in act else 25, "ke1")
            bank_ready(eng, n, act, f"sc{it}", "A")
            for jj in range(2):
                eng.matmul(BA[:, jj * 2 * P:(jj + 1) * 2 * P], QT[:, par, 0, 2 * kv + jj, :],
                           KT[:, par, kv, :, 0, :], start=(jj == 0), stop=False, skip_group_check=True)
            mm = eng.matmul(BA[:, :], ident16[:, :], MB[:, :, :].rearrange("p a b -> p (a b)"), start=False, stop=True,
                            skip_group_check=True)
            L["p_hd"].inc(mm, f"sa{it}")
            bank_ready(eng, n, act, f"sc{it}", "BC")
            for jj, bank in ((0, BB), (1, BC)):
                eng.matmul(bank[:, :], QT[:, par, 1, 2 * kv + jj, :],
                           KT[:, par, kv, :, :, :].rearrange("p a b c -> p (a b c)"), start=True, stop=False,
                           skip_group_check=True)
                mm = eng.matmul(bank[:, :].rearrange("p (a b) -> p a b", a=2)[:, :, P:2 * P], ident16[:, :],
                                MB[:, 0:2, :], start=False, stop=True, skip_group_check=True)
            L["p_hd"].inc(mm, f"sb{it}")

        def pe_pt(eng, n, act, it):
            for b, bank in enumerate((BA, BB, BC)):
                if b == 0:
                    L["g_hd"].wait(eng, n, f"k{it}.0")
                elif b == 1:
                    L["a_hd"].wait(eng, n, f"e{it}.7")
                else:
                    L["g_hd"].wait(eng, n, f"k{it}.1")
                bank_ready(eng, n, act, f"pt{it}", "ABC"[b])
                for g in range(G):
                    mm = eng.transpose(bank[:, g * P:(g + 1) * P], P32[:, b, g, :], ident[:, :])
                L["p_hd"].inc(mm, f"pt{it}.{b}")

        def pe_pv(eng, n, act, lane, label, use, m, ready, kv):
            bank_ready(eng, n, act, use)
            L["v_hd"].wait(eng, m, ready)
            par = ((m - 12) // 2) % 3
            for qt in range(2):
                for g in range(G):
                    o = BC[:, (qt * G + g) * VW:(qt * G + g + 1) * VW]
                    terms = [(0, 0)] if qt == 0 else [(1, 0), (2, 1)]
                    q = 0
                    for b, kt in terms:
                        for ph in (PH, PL):
                            mm = eng.matmul(o, ph[:, b, g, :], VS[:, par, kt, kv, :], start=(q == 0),
                                            stop=(q == 2 * len(terms) - 1))
                            q += 1
            L[lane].inc(mm, label)

        def pe_op_tp(eng, n, act):
            bank_ready(eng, n, act, "op.tp")
            L["g_os"].wait(eng, n - 1, "os")
            for k in range(KD):
                mm = eng.transpose(BB[:, k * P:(k + 1) * P], OS[:, k * P:(k + 1) * P], ident[:, :])
            L["p_op"].inc(mm, "tp")

        def pe_op_mm(eng, n, act):
            if "a3" not in act:
                bank_ready(eng, n, act, "op.mm")
            L["a_op"].wait(eng, n, "ot")
            for k in range(KD):
                mm = eng.matmul(BB[:, D:2 * D], OT[:, k, :], WO[:, k, :], start=(k == 0), stop=(k == KD - 1))
            L["p_op"].inc(mm, "mm")

        def pe_body(eng, n, act):
            for p in range(16):
                i = p // 2
                if p % 2 == 0:
                    pe_gu(eng, n, act, i)
                elif not (isinstance(n, int) and n == 4 and i < 4):
                    pe_y(eng, n, act, i)
                if p == 0 and "qk" in act:
                    pe_qkv(eng, n, act)
                if p == 0 and "op" in act:
                    pe_op_tp(eng, n, act)
                if p == 1 and "pw" in act:
                    pe_pv(eng, n, act, "p_pw", "pv", "pw", n - 1, "l1.2", 2 * ((n + 1) % 2) + 1)
                if p == 2 and "hd" in act:
                    pe_scores(eng, n, act, 0)
                if p == 5 and "fp" in act:
                    bank_ready(eng, n, act, "fp.tp")
                    pe_tp(eng, "p_fp", "v_ln", n, "f", BA, 0)
                    if "ap" in act:
                        pe_tp(eng, "p_ap", "v_al", n, "a", BA, D)
                if p == 6 and "hd" in act:
                    pe_pt(eng, n, act, 0)
                if p == 8 and "a3" in act:
                    pe_a3(eng, n, act)
                if p == 8 and "op" in act:
                    pe_op_mm(eng, n, act)
                if p == 9 and "hd" in act:
                    pe_pv(eng, n, act, "p_hd", "pv0", "pv0", n, "l0.2", 2 * (n % 2))
                if p == 10 and "hd" in act:
                    pe_scores(eng, n, act, 1)
                if p == 13 and "fp" in act:
                    bank_ready(eng, n, act, "fp.lg")
                    pe_lg(eng, n, BA)
                if p == 14 and "hd" in act:
                    pe_pt(eng, n, act, 1)

        def act_tanh(eng, n, i):
            e = (n % 4) * 2 + i // 4
            L["p_gu"].wait(eng, n, f"gu{i}")
            wait_apart(L["v_ff"], eng, n - 1 if i < 2 else n, f"h{(i - 2) % 8}")
            L["a_ff"].inc(eng.activation(TS[:, i % 2, :], GB[i % 2][:, :], ACT.Tanh, scale=TSC[:, e, :]), f"tanh{i}")

        def act_hi(eng, n, i):
            h, m = divmod(i, 4)
            L["v_ff"].wait(eng, n, f"h{i}")
            if m == 0:
                L["p_y"].wait(eng, n if h else n - 1, "y3" if h else "y7")
            L["a_ff"].inc(eng.activation(HS[:, h, 0, m, :], H32[:, i % 2, :], ACT.Copy), f"hi{i}")

        def act_xt(eng, n, bank=None, both=False):
            L["p_fp"].wait(eng, n, "tp")
            if both:
                L["p_ap"].wait(eng, n, "tp")
            L["v_sp"].wait(eng, n - 1, "xl")
            L["p_lg"].wait(eng, n - 1, "lg")
            L["a_xt"].inc(eng.activation(LN["f"][5][:, :, :].rearrange("p a b -> p (a b)"),
                                         (BA if bank is None else bank)[:, 0:D], ACT.Copy), "xt")

        def act_rt(eng, n, bank):
            L["p_lg"].wait(eng, n, "lg")
            L["v_rt"].wait(eng, n, "mx")
            L["a_rt"].inc(eng.activation(EX[:, :], bank[:, 0:E], ACT.Exp, bias=NM[:, 0:1], accum_out=ES[:, 0:1]), "ex")

        def act_wp(eng, n, x, js):
            e = 2 * (n - 4) + 1 + x
            wait_apart(L["v_wp"], eng, n, f"sc{x}")
            for j in js:
                L["a_wp"].inc(eng.activation(W[:, e, 0, j, :], stage[:, j, :], ACT.Copy, scale=SCW[:, j:j + 1]), f"hi{x}.{j}")
                if j == 0:
                    L["a_wp"].inc(eng.activation(stage[:, j, :], stage[:, j, :], ACT.Copy, scale=SCW[:, j:j + 1]), f"sc{x}.{j}")

        def act_exps(eng, n, it, qt, heads):
            kv = 2 * (n % 2) + it
            L["v_hd"].wait(eng, n, f"nb{it}.{qt}")
            wait_apart(L["p_hd"], eng, n if it else n - 1, "pt0.2" if it else "pt1.2")
            for g in heads:
                if qt == 0:
                    s, p = BA[:, g * P:(g + 1) * P], P32[:, 0, g, :]
                else:
                    s = (BB, BC)[g // 2][:, (g % 2) * 2 * P:(g % 2 + 1) * 2 * P].rearrange("p (a b) -> p a b", a=2)
                    p = P32[:, 1:3, g, :]
                L["a_hd"].inc(eng.activation(p, s, ACT.Exp, bias=NB[:, qt, g:g + 1], scale=AG[:, kv, g:g + 1]),
                              f"e{it}.{qt * G + g}")

        def act_ph(eng, n, it):
            L["p_hd" if it else "p_pw"].wait(eng, n, "pv0" if it else "pv")
            for b, bank in enumerate((BA, BB, BC)):
                L["p_hd"].wait(eng, n, f"pt{it}.{b}")
                L["a_hd"].inc(eng.activation(PH[:, b, :, :].rearrange("p a b -> p (a b)"), bank[:, :], ACT.Copy), f"h{it}.{b}")

        def act_ap_xt(eng, n):
            L["p_ap"].wait(eng, n, "tp")
            L["p_qk"].wait(eng, n, "qkv") if not isinstance(n, int) or n > 8 else None
            L["a_ap"].inc(eng.activation(LN["a"][5][:, :, :].rearrange("p a b -> p (a b)"), BA[:, D:2 * D], ACT.Copy), "xt")

        def act_a3_hi(eng, n):
            L["v_a3"].wait(eng, n, "r")
            L["p_a3"].wait(eng, n - 1, "kt")
            q = RA[:, 0:H * HD].rearrange("p (h c) -> p h c", c=HD)
            k = RA[:, H * HD:].rearrange("p (h c) -> p h c", c=HD)
            L["a_a3"].inc(eng.activation(QS[:, :, 0:4:2, :], q.unsqueeze(2).broadcast_to([P, H, 2, HD]), ACT.Copy), "qhi")
            for s in range(2):
                L["a_a3"].inc(eng.activation(KS[:, :, :, s, :], k.unsqueeze(2).broadcast_to([P, KVH, 2, HD]), ACT.Copy), f"khi{s}")

        def act_qe(eng, n):
            wait_apart(L["p_a3"], eng, n, "qt")
            L["a_a3"].inc(eng.activation(QT[:, ((n - 10) // 2) % 2, n % 2, :, :].rearrange("p a b -> p (a b)"),
                                         BA[:, :].bitcast(F16), ACT.Copy), "qe")

        def act_ot(eng, n):
            L["p_op"].wait(eng, n, "tp")
            L["p_op"].wait(eng, n - 1, "mm")
            L["a_op"].inc(eng.activation(OT[:, :, :].rearrange("p a b -> p (a b)"), BB[:, 0:D], ACT.Copy), "ot")

        def act_body(eng, n, act):
            first = isinstance(n, int) and n == 4
            last = isinstance(n, int) and n == 7
            for p in range(16):
                i = p // 2
                if first and p in (0, 2, 4, 6):
                    act_rt(eng, i, (BA, BB, BC, YB)[i])
                if p in (4, 12) and "hd" in act:
                    act_exps(eng, n, p // 8, 0, range(G))
                if p == 1 and "op" in act:
                    act_ot(eng, n)
                if p % 2 == 0:
                    act_tanh(eng, n, i)
                if p == 2 and "a3" in act:
                    act_a3_hi(eng, n)
                if p in (4, 12) and "hd" in act:
                    act_exps(eng, n, p // 8, 1, (0, 1))
                if p == 5 and "fp" in act:
                    act_xt(eng, n, both="ap" in act)
                if p == 5 and "ap" in act:
                    act_ap_xt(eng, n)
                if p in (7, 15) and "hd" in act:
                    act_ph(eng, n, p // 8)
                if p == 9 and "a3" in act:
                    act_qe(eng, n)
                if p % 2 == 1:
                    act_hi(eng, n, i)
                if p in (5, 13) and "hd" in act:
                    act_exps(eng, n, p // 8, 1, (2, 3))
                if p == 13 and "fp" in act:
                    act_rt(eng, n, BA)
                if "wp" in act and p % 8 in (4, 5, 6) and not (last and p > 7):
                    act_wp(eng, n, p // 8, (p % 8 - 4,))

        def dve_t(eng, n, i):
            L["a_ff"].wait(eng, n, f"tanh{i}")
            L["v_ff"].inc(eng.scalar_tensor_tensor(TS[:, i % 2, :], TS[:, i % 2, :], 1.0, GB[i % 2][:, :],
                                                   ALU.add, ALU.mult), f"t{i}")

        def dve_h(eng, n, i):
            L["v_ff"].wait(eng, n, f"t{i}")
            m, j = (n, i - 2) if i >= 2 else (n - 1, i + 6)
            L["a_ff"].wait(eng, m, f"hi{j}")
            L["g_ff"].wait(eng, m, f"lo{j}")
            L["v_ff"].inc(eng.scalar_tensor_tensor(H32[:, i % 2, :], TS[:, i % 2, :], H_C, UB[i % 2][:, :],
                                                   ALU.mult, ALU.mult), f"h{i}")

        def dve_wc(eng, n, act, h):
            e = (n % 4) * 2 + h
            if h == 0:
                L["v_rt"].wait(eng, n - 1 if "fp" in act else 31, "wt")
            L["v_y"].wait(eng, n if h else n - 1, "y3" if h else "y7")
            L["v_wc"].inc(eng.tensor_tensor(WTC[:, h, :], WT[:, blk(n), :, e], CF[:, e, :].broadcast_to([P, BT]),
                                            ALU.mult), f"wc{h}")

        def dve_y(eng, n, i):
            h, m = divmod(i, 4)
            L["p_y"].wait(eng, n, f"y{i}")
            L["v_y"].wait(eng, n - 1 if h == 0 else n, f"y{(i + 4) % 8}")
            L["v_wc"].wait(eng, n - 1 if h == 0 else n, f"wc{1 - h}")
            b = blk(n) if h else blk(n - 1)
            x = X[:, b * BT + m, :]
            L["v_y"].inc(eng.scalar_tensor_tensor(x, YB[:, 0:D], WTC[:, 1 - h, m:m + 1], x, ALU.mult, ALU.add), f"y{i}")

        def dve_ln(eng, n, lane, k, t):
            ST, MV, VE, _, _, _ = LN[k]
            L[lane].inc(eng.bn_stats(ST[:, :], X[:, t, :]), "stats")
            wait_apart(L[lane], eng, n, "stats")
            L[lane].inc(eng.bn_aggr(MV[:, :], ST[:, :]), "aggr")
            L[lane].wait(eng, n, "aggr")
            L[lane].inc(eng.tensor_scalar(VE[:, :], MV[:, 1:2], LN_EPS, None, ALU.add), "eps")

        def dve_xn(eng, n, lane, glane, k, t, free):
            _, MV, _, RS, XN, _ = LN[k]
            L[glane].wait(eng, n, "rs")
            L[free].wait(eng, n - 1, "tp")
            L[lane].inc(eng.tensor_scalar(XN[:, :], X[:, t, :], MV[:, 0:1], RS[:, 0:1], ALU.subtract, ALU.mult), "xn")

        def dve_split(eng, n):
            XT = LN["f"][5]
            par, c = (n // BT) % 2, n % BT
            L["a_xt"].wait(eng, n, "xt")
            L["p_gu"].wait(eng, n - 1, "gu7") if not (isinstance(n, int) and n < 5) else None
            L["v_sp"].inc(eng.tensor_scalar(XS16[:, par, 0, :, c, :], XT[:, :, :], XS, None, ALU.mult), "xh")
            L["v_sp"].wait(eng, n, "xh")
            L["v_sp"].inc(eng.scalar_tensor_tensor(XS16[:, par, 1, :, c, :], XT[:, :, :], XS, XS16[:, par, 0, :, c, :],
                                                   ALU.mult, ALU.subtract), "xl")

        def dve_rt1(eng, n, bank):
            L["p_lg"].wait(eng, n, "lg")
            L["v_rt"].inc(eng.tensor_reduce(NM[:, :], bank[:, 0:E], AX.X, ALU.max, negate=True), "mx")

        def dve_rt2(eng, n):
            L["a_rt"].wait(eng, n, "ex")
            L["v_rt"].inc(eng.reciprocal(EC[:, :], ES[:, :]), "rc")
            L["v_rt"].wait(eng, n, "rc")
            L["v_rt"].inc(eng.tensor_scalar(PR[:, :], EX[:, :], EC[:, 0:1], None, ALU.mult), "p")
            L["v_rt"].wait(eng, n, "p")
            pf = PR[:, :].unsqueeze(1).broadcast_to([P, E, E])
            pe = PR[:, :].unsqueeze(2).broadcast_to([P, E, E])
            L["v_rt"].inc(eng.tensor_tensor(EQ[:, :, :], pf, pe, ALU.is_equal), "eq")
            L["v_rt"].inc(eng.tensor_tensor(GT[:, :, :], pf, pe, ALU.is_gt), "gt")

        def dve_rt3(eng, n):
            L["g_rt"].wait(eng, n, "bp")
            L["v_rt"].inc(eng.tensor_reduce(CUM[:, :], EQ[:, :, :], AX.X, ALU.add), "cum")
            L["v_rt"].wait(eng, n, "cum")
            L["v_rt"].inc(eng.scalar_tensor_tensor(WT[:, (n // BT) % (NT // BT), n % BT, :], CUM[:, :], TOP_P, PR[:, :],
                                                   ALU.is_le, ALU.mult), "wt")

        def dve_mx(eng, n, x, js):
            e = 2 * (n - 4) + 1 + x
            for j in js:
                eng.wait_ge(s_w[j], 16 * (e + 1))
                L["v_wp"].inc(eng.tensor_reduce(MXW[:, j:j + 1], stage[:, j, :], AX.X, ALU.max,
                                                apply_absolute_value=True), f"mx.{j}.{x}")

        def dve_scale(eng, n, x):
            e = 2 * (n - 4) + 1 + x
            L["g_wp"].wait(eng, n, f"ar{x}")
            L["v_wp"].inc(eng.tensor_scalar(MAW[:, :], MAW[:, :], 1e-30, None, ALU.max), f"cl{x}")
            L["v_wp"].wait(eng, n, f"cl{x}")
            L["v_wp"].inc(eng.tensor_scalar(PEW[:, :].bitcast(I32), MAW[:, :].bitcast(I32), 0x7F800000, None,
                                            ALU.bitwise_and), f"pe{x}")
            L["v_wp"].wait(eng, n, f"pe{x}")
            L["v_wp"].inc(eng.reciprocal(SCW[:, :], PEW[:, :]), f"rc{x}")
            L["v_wp"].wait(eng, n, f"rc{x}")
            L["v_wp"].inc(eng.tensor_scalar(SCW[:, :], SCW[:, :], 2.0 ** WTOP, None, ALU.mult), f"sc{x}")
            L["v_wp"].inc(eng.tensor_scalar(TSC[:, e, :], PEW[:, 0:1], TANH_C, None, ALU.mult), f"tsc{x}")
            L["v_wp"].inc(eng.tensor_tensor(GUD[:, :], PEW[:, 0:1], PEW[:, 1:2], ALU.mult), f"gu{x}")
            L["v_wp"].wait(eng, n, f"gu{x}")
            L["v_wp"].inc(eng.tensor_scalar(CF[:, e, :], GUD[:, :], PEW[:, 2:3], CF_C, ALU.mult, ALU.mult), f"cf{x}")

        def dve_wlo(eng, n, x, j):
            e = 2 * (n - 4) + 1 + x
            L["a_wp"].wait(eng, n, f"hi{x}.{j}")
            L["v_wp"].inc(eng.scalar_tensor_tensor(W[:, e, 1, j, :], stage[:, j, :], SCW[:, j:j + 1], W[:, e, 0, j, :],
                                                   ALU.mult, ALU.subtract), f"lo.{j}.{x}")

        def dve_qb(eng, n):
            L["p_qk"].wait(eng, n, "qkv")
            L["g_qk"].wait(eng, n - 1, "v3")
            L["v_qk"].inc(eng.tensor_tensor(QKV[:, :], BA[:, 0:QKVW], BQKV[:, :], ALU.add), "qb")

        def dve_ss(eng, n):
            L["g_qk"].wait(eng, n, "sq")
            L["v_qk"].inc(eng.tensor_reduce(SS[:, :], SQ[:, :].rearrange("p (h c) -> p h c", c=HD), AX.X, ALU.add), "ss")
            L["v_qk"].wait(eng, n, "ss")
            L["v_qk"].inc(eng.tensor_scalar(MS[:, :], SS[:, :], 1.0 / HD, RMS_EPS, ALU.mult, ALU.add), "ms")

        def dve_qn(eng, n):
            L["g_qk"].wait(eng, n - 1, "sg")
            L["v_a3"].inc(eng.tensor_tensor(QN[:, :].rearrange("p (h c) -> p h c", c=HD),
                                            QKV[:, 0:QK * HD].rearrange("p (h c) -> p h c", c=HD),
                                            RR[:, :].unsqueeze(2).broadcast_to([P, QK, HD]), ALU.mult), "qn")

        def dve_rb(eng, n, a):
            L["v_a3"].wait(eng, n, "qn")
            q4 = QN[:, :].rearrange("p (h a c) -> p h a c", a=2, c=HD // 2)
            table = (SIN, NSIN)[a]
            L["v_a3"].inc(eng.tensor_tensor(RB[:, :, a, :], q4[:, :, 1 - a, :],
                                            table[:, n % 2, :].unsqueeze(1).broadcast_to([P, QK, HD // 2]), ALU.mult), f"rb{a}")

        def dve_r(eng, n):
            L["v_a3"].wait(eng, n, "rb1")
            L["g_a3"].wait(eng, n, "ra")
            L["v_a3"].inc(eng.tensor_tensor(RA[:, :], RA[:, :], RB[:, :, :, :].rearrange("p h a c -> p (h a c)"), ALU.add), "r")

        def dve_a3_lo(eng, n):
            q = RA[:, 0:H * HD].rearrange("p (h c) -> p h c", c=HD)
            k = RA[:, H * HD:].rearrange("p (h c) -> p h c", c=HD)
            L["a_a3"].wait(eng, n, "qhi")
            L["v_a3"].inc(eng.tensor_tensor(QS[:, :, 1:4:2, :], q.unsqueeze(2).broadcast_to([P, H, 2, HD]),
                                            QS[:, :, 0:4:2, :], ALU.subtract), "qlo")
            L["a_a3"].wait(eng, n, "khi1")
            for s in range(2):
                L["v_a3"].inc(eng.tensor_tensor(KS[:, :, :, 2 + s, :], k.unsqueeze(2).broadcast_to([P, KVH, 2, HD]),
                                                KS[:, :, :, s, :], ALU.subtract), f"klo{s}")

        def dve_ke(eng, n, act):
            L["p_a3"].wait(eng, n, "kt")
            if "op" in act:
                L["p_op"].wait(eng, n, "mm")
            b16 = BB[:, :].bitcast(F16)[:, 0:KVH * P].rearrange("p (a b) -> p a b", a=KVH)
            par, t = ((n - 10) // 2) % 2, n % 2
            for h in range(2):
                lo, hi = h * P // 2, (h + 1) * P // 2
                L["v_a3"].inc(eng.tensor_copy(KT[lo:hi, par, :, h, t, :], b16[lo:hi, :, :]), f"ke{h}")

        def dve_max(eng, n, it, qt):
            kv = 2 * (n % 2) + it

            def top(j):
                x = (BA[:, :].rearrange("p (g k) -> p g k", g=G) if j == 0 else
                     (BB, BC)[j - 1][:, :].rearrange("p (g k) -> p g k", g=2))
                out = MX[:, 0, :] if j == 0 else MX[:, 1, 2 * j - 2:2 * j]
                L["v_hd"].inc(eng.tensor_reduce(out, x, AX.X, ALU.max), f"mx{it}.{j}")

            def bias(qt, label):
                L["v_hd"].wait(eng, n, label)
                L["a_hd"].wait(eng, n if it else n - 1, f"e{1 - it}.{7 if qt else 3}")
                L["v_hd"].inc(eng.scalar_tensor_tensor(NB[:, qt, :], MX[:, qt, :], -1.0, AG[:, kv, :], ALU.mult, ALU.mult),
                              f"nb{it}.{qt}")

            if qt == 0:
                L["p_hd"].wait(eng, n, f"sa{it}")
                top(0)
                L["p_hd"].wait(eng, n, f"sb{it}")
                top(1)
                bias(0, f"mx{it}.0")
            else:
                top(2)
                bias(1, f"mx{it}.2")

        def dve_pl(eng, n, it, bs):
            for b in bs:
                L["a_hd"].wait(eng, n, f"h{it}.{b}")
                L["v_hd"].inc(eng.tensor_tensor(PL[:, b, :, :].rearrange("p a b -> p (a b)"), (BA, BB, BC)[b][:, :],
                                                PH[:, b, :, :].rearrange("p a b -> p (a b)"), ALU.subtract), f"l{it}.{b}")

        def dve_sum(eng, n, lane, sfx, plane, plabel):
            o = BC[:, 0:2 * G * VW].rearrange("p (g c) -> p g c", c=VW)
            L[plane].wait(eng, n, plabel)
            L[lane].inc(eng.reciprocal(RC[:, :], o[:, :, VW - 1]), f"rc{sfx}")
            L[lane].inc(eng.tensor_reduce(RD[:, :, :], o[:, :, 0:3 * HD].rearrange("p g (s c) -> p g c s", s=3), AX.X, ALU.add),
                        f"rd{sfx}")

        def dve_ob(eng, n, lane, sfx, m, kv):
            L[lane].wait(eng, n, f"rd{sfx}")
            L[lane].inc(eng.tensor_tensor(OB[:, ((m - 12) // 2) % 2, :, kv, :].rearrange("p t (g c) -> p t g c", c=HD),
                                          RD[:, :, :].rearrange("p (t g) c -> p t g c", t=2),
                                          RC[:, :].rearrange("p (t g) -> p t g", t=2).unsqueeze(3).broadcast_to([P, 2, G, HD]),
                                          ALU.mult), f"ob{sfx}")

        def dve_op(eng, n):
            L["p_op"].wait(eng, n, "mm")
            L["g_al"].wait(eng, n - 7, "bo")
            x = X[:, n - 15, :]
            L["v_op"].inc(eng.tensor_tensor(x, BB[:, D:2 * D], x, ALU.add), "ad")

        def dve_fp_ready(eng, n, act):
            if isinstance(n, int) and n < 5:
                eng.wait_ge(s_x0 if n < 4 else s_x1, 16 if n < 4 else 16 * (NT // BT - 1))
            if not isinstance(n, int) and "op" in act or isinstance(n, int) and n > 15:
                L["v_op"].wait(eng, n - 1, "ad")

        def dve_body(eng, n, act):
            first = isinstance(n, int) and n == 4
            last = isinstance(n, int) and n == 7
            for p in range(16):
                i = p // 2
                if p == 0 and "fp" in act:
                    dve_fp_ready(eng, n, act)
                    dve_ln(eng, n, "v_ln", "f", n % NT)
                if p == 0 and "a3" in act:
                    dve_qn(eng, n)
                if p == 1 and "qk" in act:
                    dve_qb(eng, n)
                if p == 1 and "fp" in act:
                    dve_xn(eng, n, "v_ln", "g_ln", "f", n % NT, "p_fp")
                if p == 1 and "a3" in act:
                    dve_rb(eng, n, 1)
                if p == 2 and "pw" in act:
                    dve_sum(eng, n, "v_pw", "", "p_pw", "pv")
                if p == 2 and "a3" in act:
                    dve_r(eng, n)
                if p in (3, 11):
                    if "hd" in act:
                        dve_max(eng, n, p // 8, 0)
                    if not (first and p == 3):
                        dve_y(eng, n, i)
                    if "hd" in act:
                        dve_max(eng, n, p // 8, 1)
                if p == 3 and "ap" in act:
                    dve_xn(eng, n, "v_al", "g_al", "a", n - 8, "p_ap")
                if p == 5 and "a3" in act:
                    dve_a3_lo(eng, n)
                if p == 5 and "qk" in act:
                    dve_ss(eng, n)
                if p == 6 and "fp" in act:
                    dve_split(eng, n)
                if p in (7, 15) and "hd" in act:
                    dve_pl(eng, n, p // 8, (0, 1, 2))
                if p == 8:
                    dve_wc(eng, n, act, 0)
                if p == 9 and "a3" in act:
                    dve_ke(eng, n, act)
                if p == 9 and "op" in act:
                    dve_op(eng, n)
                if p == 10 and "hd" in act:
                    dve_sum(eng, n, "v_hd", "0", "p_hd", "pv0")
                if p == 14 and "fp" in act:
                    dve_rt1(eng, n, BA)
                    dve_rt2(eng, n)
                if "wp" in act and not (last and p > 7):
                    if p % 8 == 1:
                        dve_mx(eng, n, p // 8, (0, 1))
                    if p % 8 == 4:
                        dve_scale(eng, n, p // 8)
                    if p % 8 == 7:
                        dve_wlo(eng, n, p // 8, 2)
                if first and p < 8 and p % 2 == 0:
                    dve_rt1(eng, i, (BA, BB, BC, YB)[i])
                if first and p < 8 and p % 2 == 1:
                    dve_rt2(eng, i)
                    dve_rt3(eng, i)
                if p % 2 == 0:
                    if i > 0 and i not in (2, 6) and not (first and i < 5):
                        dve_y(eng, n, i - 1)
                    if p in (2, 10) and "wp" in act and not (last and p == 10):
                        dve_mx(eng, n, p // 8, (2,))
                    if p in (6, 14) and "wp" in act and not (last and p == 14):
                        dve_wlo(eng, n, p // 8, 1)
                    if p == 2 and "ap" in act:
                        L["v_y"].wait(eng, n, "y0")
                        dve_ln(eng, n, "v_al", "a", n - 8)
                    dve_t(eng, n, i)
                    if p == 0 and "a3" in act:
                        dve_rb(eng, n, 0)
                    if p == 2 and "pw" in act:
                        dve_ob(eng, n, "v_pw", "", n - 1, 2 * ((n + 1) % 2) + 1)
                    if p == 10 and "hd" in act:
                        dve_ob(eng, n, "v_hd", "0", n, 2 * (n % 2))
                    dve_h(eng, n, i)
                if p == 15:
                    dve_y(eng, n, 7)
                    dve_wc(eng, n, act, 1)
                if p == 15 and "fp" in act:
                    dve_rt3(eng, n)

        def pool_lo(eng, n, i):
            h, m = divmod(i, 4)
            L["a_ff"].wait(eng, n, f"hi{i}")
            L["g_ff"].inc(eng.tensor_tensor(HS[:, h, 1, m, :], H32[:, i % 2, :], HS[:, h, 0, m, :], ALU.subtract), f"lo{i}")

        def pool_rs(eng, n, vlane, glane, k):
            _, _, VE, RS, _, _ = LN[k]
            L[vlane].wait(eng, n, "eps")
            L[glane].inc(eng.tensor_tensor(RS[:, :], VE[:, :], MH[:, 0:1], ALU.pow), "rs")

        def pool_rank(eng, n):
            L["v_rt"].wait(eng, n, "gt")
            L["g_rt"].inc(eng.tensor_tensor(EQ[:, :, :], EQ[:, :, :], LOW[:, :, :], ALU.mult), "eq")
            L["g_rt"].wait(eng, n, "eq")
            L["g_rt"].inc(eng.tensor_tensor(EQ[:, :, :], EQ[:, :, :], GT[:, :, :], ALU.add), "b")
            L["g_rt"].wait(eng, n, "b")
            L["g_rt"].inc(eng.tensor_tensor(EQ[:, :, :], EQ[:, :, :], PR[:, :].unsqueeze(1).broadcast_to([P, E, E]), ALU.mult), "bp")

        def pool_wp(eng, n, x):
            wait_apart(L["v_wp"], eng, n, f"mx.2.{x}")
            L["g_wp"].inc(eng.partition_all_reduce(MAW[:, :], MXW[:, :], P, bass.bass_isa.ReduceOp.max), f"ar{x}")

        def pool_wlo(eng, n, x):
            e = 2 * (n - 4) + 1 + x
            L["a_wp"].wait(eng, n, f"sc{x}.0")
            L["g_wp"].inc(eng.tensor_tensor(W[:, e, 1, 0, :], stage[:, 0, :], W[:, e, 0, 0, :], ALU.subtract), f"lo.0.{x}")

        def pool_bo(eng, n):
            wait_apart(L["v_al"], eng, n, "xn")
            x = X[:, n - 8, :]
            L["g_al"].inc(eng.tensor_tensor(x, x, BO[:, :], ALU.add), "bo")

        def pool_sq(eng, n):
            L["v_qk"].wait(eng, n, "qb")
            L["g_qk"].inc(eng.tensor_tensor(SQ[:, :], QKV[:, 0:QK * HD], QKV[:, 0:QK * HD], ALU.mult), "sq")

        def pool_rr(eng, n):
            L["v_qk"].wait(eng, n, "ms")
            L["g_qk"].inc(eng.tensor_tensor(RR[:, :], MS[:, :], MH[:, :], ALU.pow), "rr")
            L["g_qk"].wait(eng, n, "rr")
            L["g_qk"].inc(eng.tensor_tensor(RR[:, 0:H], RR[:, 0:H], SGN[:, :], ALU.mult), "sg")

        def pool_ra(eng, n):
            L["v_a3"].wait(eng, n, "qn")
            L["v_a3"].wait(eng, n - 1, "klo1")
            L["a_a3"].wait(eng, n - 1, "khi1")
            c8 = HD // 2
            L["g_a3"].inc(eng.tensor_tensor(RA[:, :].rearrange("p (h c) -> p h c", c=c8), QN[:, :].rearrange("p (h c) -> p h c", c=c8),
                                            COS[:, n % 2, :].unsqueeze(1).broadcast_to([P, 2 * QK, c8]), ALU.mult), "ra")

        def pool_v(eng, n):
            v = QKV[:, QK * HD:].rearrange("p (h c) -> p h c", c=HD)
            vs = VS[:, ((n - 9) // 2) % 3, (n + 1) % 2, :, :]
            L["g_qk"].inc(eng.tensor_copy(vs[:, :, 0:HD], v), "v1")
            wait_apart(L["g_qk"], eng, n, "v1")
            L["g_qk"].inc(eng.tensor_tensor(VR[:, 0, :, :], v, vs[:, :, 0:HD], ALU.subtract), "r1")
            L["g_qk"].wait(eng, n, "r1")
            L["g_qk"].inc(eng.tensor_copy(vs[:, :, HD:2 * HD], VR[:, 0, :, :]), "v2")
            wait_apart(L["g_qk"], eng, n, "v2")
            L["g_qk"].inc(eng.tensor_tensor(VR[:, 1, :, :], VR[:, 0, :, :], vs[:, :, HD:2 * HD], ALU.subtract), "r2")
            L["g_qk"].wait(eng, n, "r2")
            L["g_qk"].inc(eng.tensor_copy(vs[:, :, 2 * HD:3 * HD], VR[:, 1, :, :]), "v3")

        def pool_mask(eng, n, it, j):
            b, e = ((0, 3), (2, 7))[j]
            wait_apart(L["a_hd"], eng, n, f"e{it}.{e}")
            L["g_hd"].inc(eng.affine_select(out=P32[:, b, :, :], in_=P32[:, b, :, :], compare_op=ALU.is_ge, fill=0.0,
                                            base=0, pattern=[[0, G], [-1, P]], channel_multiplier=1), f"k{it}.{j}")

        def pool_os(eng, n, act):
            L["v_pw"].wait(eng, n if "pw" in act else 28, "ob")
            if "op" in act:
                L["p_op"].wait(eng, n, "tp")
            L["g_os"].inc(eng.tensor_copy(OS[:, :], OB[:, ((n - 14) // 2) % 2, n % 2, :, :].rearrange("p a b -> p (a b)")), "os")

        def pool_body(eng, n, act):
            first = isinstance(n, int) and n == 4
            last = isinstance(n, int) and n == 7
            for p in range(16):
                i = p // 2
                if p == 0 and "fp" in act:
                    pool_rs(eng, n, "v_ln", "g_ln", "f")
                if p == 1 and "a3" in act:
                    pool_ra(eng, n)
                if "wp" in act and not (last and p > 7):
                    if p % 8 == 3:
                        pool_wp(eng, n, p // 8)
                if p == 2 and "ap" in act:
                    pool_rs(eng, n, "v_al", "g_al", "a")
                if p == 4 and "os" in act:
                    pool_os(eng, n, act)
                if p == 4 and "ap" in act:
                    pool_bo(eng, n)
                if first and p < 8 and p % 2 == 1:
                    pool_rank(eng, i)
                if p in (5, 13) and "hd" in act:
                    pool_mask(eng, n, p // 8, 0)
                if p in (6, 14) and "hd" in act:
                    pool_mask(eng, n, p // 8, 1)
                if p == 14 and "fp" in act:
                    pool_rank(eng, n)
                if "wp" in act and p % 8 == 5 and not (last and p > 7):
                    pool_wlo(eng, n, p // 8)
                if p % 2 == 1:
                    pool_lo(eng, n, i)
                if p == 3 and "qk" in act:
                    pool_sq(eng, n)
                if p == 7 and "qk" in act:
                    pool_rr(eng, n)
                if p == 9 and "qk" in act:
                    pool_v(eng, n)

        block = ctx.enter_context(nc.Block())

        @block.sync
        def _(eng):
            xt = d["x"].rearrange("(n p) d -> p n d", p=P)
            eng.dma_start(X[:, 0:BT, :], xt[:, 0:BT, :]).then_inc(s_x0, 16)

            def load_expert(e):
                for j, w in enumerate(("gate", "up", "down")):
                    eng.dma_start(stage[:, j, :], d[w][e]).then_inc(s_w[j], 16)

            load_expert(0)
            for b in range(1, NT // BT):
                eng.dma_start(X[:, b * BT:(b + 1) * BT, :], xt[:, b * BT:(b + 1) * BT, :]).then_inc(s_x1, 16)
            for e in range(1, E):
                n, x = (e - 1) // 2 + 4 - e % 2, e % 2
                for j, w in enumerate(("gate", "up", "down")):
                    L["v_wp" if j else "g_wp"].wait(eng, n, f"lo.{j}.{x}")
                    eng.dma_start(stage[:, j, :], d[w][e]).then_inc(s_w[j], 16)

            def store(n, t):
                L["v_y"].wait(eng, n, "y3")
                eng.dma_start(d["out"][t, :, :], X[:, t, :]).then_inc(s_st, 16)

            for a, b in RUNS:
                if "st" in active(a):
                    if b - a == 1:
                        store(a, a - 24)
                    else:
                        with eng.Fori(a, b) as n:
                            store(n, n - 24)
            for t in range(NT - BT, NT):
                L["v_y"].wait(eng, 36, "y3")
                eng.dma_start(d["out"][t, :, :], X[:, t, :]).then_inc(s_st, 16)
            eng.wait_ge(s_st, 16 * NT)

        @block.gpsimd
        def _(eng):
            give_credit(eng, "g_")
            eng.memset(ident[:, :], 0.0).then_inc(s_i1, 1)
            eng.memset(MH[:, :], -0.5).then_inc(s_i1, 1)
            eng.memset(LOW[:, :, :], 1.0).then_inc(s_i1, 1)
            eng.memset(ident16[:, :], 0.0).then_inc(s_i1, 1)
            eng.memset(MB[:, :, :], 0.0).then_inc(s_i1, 1)
            eng.wait_ge(s_i1, 5)
            for t in (ident, ident16):
                eng.affine_select(out=t[:, :], in_=t[:, :], compare_op=ALU.not_equal, fill=1.0, base=0,
                                  pattern=[[-1, P]], channel_multiplier=1).then_inc(s_i1, 1)
            eng.affine_select(out=LOW[:, :, :], in_=LOW[:, :, :], compare_op=ALU.is_ge, fill=0.0, base=-1,
                              pattern=[[1, E], [-1, E]], channel_multiplier=0).then_inc(s_i1, 1)
            eng.wait_ge(s_i1, N_I1)
            for n in range(4):
                pool_rs(eng, n, "v_ln", "g_ln", "f")
                if n == 1:
                    pool_wp(eng, 3, 1)
            pool_wlo(eng, 3, 1)
            eng.affine_select(out=MB[:, :, :], in_=MB[:, :, :], compare_op=ALU.is_ge, fill=MASKED, base=0,
                              pattern=[[0, G], [-1, P]], channel_multiplier=1).then_inc(s_i2, 1)
            eng.memset(KT[:, :, :, :, :, :], 0.0).then_inc(s_i2, 1)
            eng.memset(VS[:, :, :, :, :], 1.0).then_inc(s_i2, 1)
            eng.wait_ge(s_i2, 3)
            eng.wait_ge(s_aw, 16 * 11)
            eng.wait_ge(s_ag, 4)
            steps(eng, lambda n, act: pool_body(eng, n, act))

        @block.scalar
        def _(eng):
            give_credit(eng, "a_")
            bc = lambda v: v.rearrange("(a n) -> a n", a=1).broadcast_to([P, v.shape[0]])
            eng.dma_start(RW[:, :, :], d["rw"]).then_inc(s_rw, 16)
            c = 0
            for w, width in (("wq", D), ("wk", KVH * HD), ("wv", KVH * HD)):
                eng.dma_start(WQKV[:, :, c:c + width], d[w]).then_inc(s_aw, 16)
                eng.dma_start(BQKV[:, c:c + width], bc(d["b" + w[1]])).then_inc(s_aw, 16)
                c += width
            eng.dma_start(WO[:, :, :], d["wo"]).then_inc(s_aw, 16)
            eng.dma_start(BO[:, :], bc(d["bo"])).then_inc(s_aw, 16)
            eng.dma_start(GN[:, :], bc(d["gain"])).then_inc(s_aw, 16)
            eng.dma_start(COS[:, :, :], d["cos"]).then_inc(s_aw, 16)
            eng.dma_start(SIN[:, :, :], d["sin"]).then_inc(s_aw, 16)
            for n in range(4):
                act_xt(eng, n, GB[n % 2])
                if n == 2:
                    act_wp(eng, 3, 1, range(3))
            eng.wait_ge(s_ag, 4)
            steps(eng, lambda n, act: act_body(eng, n, act))

        @block.vector
        def _(eng):
            give_credit(eng, "v_")
            eng.wait_ge(s_i1, N_I1)
            for n in range(5):
                if n < 4:
                    dve_fp_ready(eng, n, set())
                    dve_ln(eng, n, "v_ln", "f", n)
                if n == 2:
                    dve_scale(eng, 3, 1)
                if n > 0:
                    dve_split(eng, n - 1)
                if n < 4:
                    dve_xn(eng, n, "v_ln", "g_ln", "f", n, "p_fp")
                if n == 1:
                    dve_mx(eng, 3, 1, range(3))
            dve_wlo(eng, 3, 1, 1)
            dve_wlo(eng, 3, 1, 2)
            eng.wait_ge(s_aw, 16 * 11)
            eng.tensor_scalar(SGN[:, :], GN[:, :], 0.0, 2.0, ALU.is_ge, ALU.mult).then_inc(s_ag, 1)
            eng.tensor_scalar(NSIN[:, :, :], SIN[:, :, :], -1.0, None, ALU.mult).then_inc(s_ag, 1)
            eng.wait_ge(s_ag, 1)
            eng.tensor_scalar(SGN[:, :], SGN[:, :], -1.0, None, ALU.add).then_inc(s_ag, 1)
            eng.wait_ge(s_ag, 3)
            eng.scalar_tensor_tensor(AG[:, :, :].rearrange("p a b -> p (a b)"), GN[:, :], float(HD) ** -0.5, SGN[:, :],
                                     ALU.mult, ALU.mult).then_inc(s_ag, 1)
            eng.wait_ge(s_ag, 4)
            steps(eng, lambda n, act: dve_body(eng, n, act))
            for m in range(4):
                dve_y(eng, 36, m)

        @block.tensor
        def _(eng):
            give_credit(eng, "p_")
            eng.wait_ge(s_i1, N_I1)
            eng.wait_ge(s_rw, 16)
            for n in range(4):
                if n > 1:
                    L["a_xt"].wait(eng, n - 2, "xt")
                pe_tp(eng, "p_fp", "v_ln", n, "f", GB[n % 2], 0)
                pe_lg(eng, n, (BA, BB, BC, YB)[n])
            steps(eng, lambda n, act: pe_body(eng, n, act))
            for m in range(4):
                pe_y(eng, 36, set(), m)


def kernel(**inputs):
    import numpy as np
    import concourse.bacc as bacc
    from concourse.bass_utils import run_bass_kernel_spmd as run

    def ktile(w):
        return np.ascontiguousarray(w.T.reshape(-1, P, w.shape[0]).transpose(1, 0, 2))

    def experts(w):
        return np.ascontiguousarray(np.stack([ktile(w[e]).reshape(P, -1) for e in range(E)]))

    f = {k: np.asarray(v) for k, v in inputs.items()}
    a, m = "L0_attn_", "L0_ffn_"
    t = np.arange(S, dtype=np.float32)
    inv = (1.0 / 10000.0 ** (np.arange(0, HD, 2, dtype=np.float32) / HD)).astype(np.float32)
    freqs = np.outer(t, inv).astype(np.float32)
    rope = lambda z: np.ascontiguousarray(z.astype(np.float32).reshape(2, P, HD // 2).transpose(1, 0, 2))
    arrays = {
        "x": f[a + "x"].reshape(B * S, D),
        "gate": experts(f[m + "gate_w"]), "up": experts(f[m + "up_w"]), "down": experts(f[m + "down_w"]),
        "rw": ktile(f[m + "router_w"]),
        "wq": ktile(f[a + "Wq"]), "wk": ktile(f[a + "Wk"]), "wv": ktile(f[a + "Wv"]), "wo": ktile(f[a + "Wo"]),
        "bq": f[a + "bq"], "bk": f[a + "bk"], "bv": f[a + "bv"], "bo": f[a + "bo"], "gain": f[a + "q_gain"],
        "cos": rope(np.cos(freqs)), "sin": rope(np.sin(freqs)),
    }
    nc = bacc.Bacc("TRN2", target_bir_lowering=False, num_devices=1)
    aps = {k: nc.dram_tensor(f"in_{k}", v.shape, mybir.dt.from_np(v.dtype), kind="ExternalInput").ap()
           for k, v in arrays.items()}
    aps["out"] = nc.dram_tensor("out_y", (NT, P, D), F32, kind="ExternalOutput").ap()
    build(nc, aps)
    r = run(nc, [{f"in_{k}": v for k, v in arrays.items()}], core_ids=[0])
    return r.results[0]["out_y"].reshape(B, S, D)
```

```python
from contextlib import ExitStack

import numpy as np

import concourse.bass as bass
from concourse import mybir

F32, F16, BF16 = mybir.dt.float32, mybir.dt.float16, mybir.dt.bfloat16
I32 = mybir.dt.int32
ALU, ACT, AX = mybir.AluOpType, mybir.ActivationFunctionType, mybir.AxisListType

P = 128
B, S, D = 8, 256, 256
H, KVH = 16, 4
HD = D // H
E, I = 8, 512
TOP_P = 0.9
LN_EPS = 1e-5
RMS_EPS = 1.1920929e-07
NT = B * S // P
BT = 4
BLK = BT * P
KD = D // P
KI = I // P
QKVW = D + 2 * KVH * HD
QK = H + KVH
G = H // KVH
W3 = KD * I
VW = 3 * HD + 1

XS = 1024.0
WTOP = 14
TANH_C = 0.5 * 2.0 ** -WTOP / XS
H_C = 2.0 ** (-3 - 1 - 2 * WTOP - 20)
CF_C = 0.5 * 2.0 ** (3 - WTOP)
MASKED = -64.0

RANGES = {"pre": (3, 3), "fp": (4, 31), "wp": (3, 7), "ff": (4, 35), "ap": (8, 23), "qk": (9, 24), "a3": (10, 25),
          "hd": (12, 27), "pw": (13, 28), "os": (14, 29), "op": (15, 30), "st": (24, 35)}
CUTS = sorted({n for a, b in RANGES.values() for n in (a, b + 1) if n >= 4} | {5, 7})
RUNS = list(zip(CUTS, CUTS[1:]))


def active(n):
    return {f for f, (a, b) in RANGES.items() if a <= n <= b}


class Lane:

    def __init__(self, sem, stage, labels, extra=0):
        self.sem, self.labels = sem, labels
        self.first = RANGES[stage][0]
        self.per = len(labels)
        self.credit = self.per + extra

    def inc(self, instr, label):
        assert label in self.labels
        instr.then_inc(self.sem, 1)

    def value(self, n, label):
        return self.per * (n - self.first + 1) + self.labels.index(label) + 1

    def wait(self, eng, n, label):
        eng.wait_ge(self.sem, self.value(n, label))


BANK_USES = [
    ("qk", {"A": ("v_qk", "qb")}),
    ("op", {"B": ("a_op", "ot")}),
    ("pw", {"C": ("v_pw", "rd")}),
    ("hd", {"A": ("a_hd", "e0.3"), "B": ("a_hd", "e0.7"), "C": ("a_hd", "e0.7")}),
    ("fp", {"A": ("a_xt", "xt")}),
    ("ap", {"A": ("a_ap", "xt")}),
    ("hd", {"A": ("v_hd", "l0.0"), "B": ("v_hd", "l0.1"), "C": ("v_hd", "l0.2")}),
    ("a3", {"A": ("a_a3", "qe"), "B": ("v_a3", "ke1")}),
    ("op", {"B": ("v_op", "ad")}),
    ("hd", {"C": ("v_hd", "rd0")}),
    ("hd", {"A": ("a_hd", "e1.3"), "B": ("a_hd", "e1.7"), "C": ("a_hd", "e1.7")}),
    ("fp", {"A": ("a_rt", "ex")}),
    ("hd", {"A": ("v_hd", "l1.0"), "B": ("v_hd", "l1.1"), "C": ("v_hd", "l1.2")}),
]
USE = {"qk": 0, "op.tp": 1, "pw": 2, "sc0": 3, "fp.tp": 4, "pt0": 6, "a3": 7, "op.mm": 8, "pv0": 9, "sc1": 10,
       "fp.lg": 11, "pt1": 12}


def build(nc, d):
    with ExitStack() as ctx:
        def sb(name, shape, dt):
            return ctx.enter_context(nc.sbuf_tensor(name, shape, dt))

        def sem(name):
            return ctx.enter_context(nc.semaphore(name))

        X = sb("X", [P, NT, D], F32)
        W = sb("W", [P, E, 2, 3, W3], F16)
        room = sb("room", [P, 3 * W3], F32)
        stage = room[:, :].rearrange("p (j w) -> p j w", j=3)
        NP3 = 3 * G * P
        P32 = room[:, 0:NP3].rearrange("p (b g k) -> p b g k", b=3, g=G)
        PH, PL = (room[:, NP3 + j * NP3 // 2:NP3 + (j + 1) * NP3 // 2].bitcast(F16).rearrange(
            "p (b g k) -> p b g k", b=3, g=G) for j in range(2))
        early = W[:, E - 2, :, :, :].rearrange("p a j w -> p (a j w)").bitcast(F32).rearrange("p (j w) -> p j w", j=3)
        scratch = W[:, E - 1, :, :, :].rearrange("p a j w -> p (a j w)").bitcast(F32)
        used = 0

        def part(*shape):
            nonlocal used
            size = int(np.prod(shape))
            used += size
            names = "abcd"[:len(shape)]
            return scratch[:, used - size:used].rearrange(f"p ({' '.join(names)}) -> p {' '.join(names)}", **dict(zip(names, shape)))

        ST4, MV4, XN4, XT4 = part(BT, 6), part(BT, 2), part(BT, D), part(BT, KD, P)
        VE4, RS4, MX4, ES4, EC4 = (part(BT) for _ in range(5))
        LG4, EX4, PR4, CUM4 = (part(BT, E) for _ in range(4))
        EQ4, GT4 = part(BT, E, E), part(BT, E, E)
        XS16 = sb("XS16", [P, 2, 2, KD, BT, P], F16)
        HS = sb("HS", [P, 2, 2, KI, BLK], F16)
        TS = sb("TS", [P, 2, BLK], F32)
        H32 = sb("H32", [P, 2, BLK], F32)
        WT = sb("WT", [P, NT // BT, BT, E], F32)
        WTC = sb("WTC", [P, 2, BT], F32)
        MXW = sb("MXW", [P, 3], F32)
        MAW = sb("MAW", [P, 3], F32)
        PEW = sb("PEW", [P, 3], F32)
        SCW = sb("SCW", [P, 3], F32)
        GUD = sb("GUD", [P, 1], F32)
        TSC = sb("TSC", [P, E, 1], F32)
        CF = sb("CF", [P, E, 1], F32)
        RW = sb("RW", [P, KD, E], F32)
        WQKV = sb("WQKV", [P, KD, QKVW], F32)
        WO = sb("WO", [P, KD, D], F32)
        BQKV = sb("BQKV", [P, QKVW], F32)
        BO = sb("BO", [P, D], F32)
        GN = sb("GN", [P, H], F32)
        AG = sb("AG", [P, KVH, G], F32)
        SGN = sb("SGN", [P, H], F32)
        COS = sb("COS", [P, 2, HD // 2], F32)
        SIN = sb("SIN", [P, 2, HD // 2], F32)
        NSIN = sb("NSIN", [P, 2, HD // 2], F32)
        ident = sb("ident", [P, P], F32)
        ident16 = sb("ident16", [P, P], F16)
        MB = sb("MB", [P, G, P], F16)
        LOW = sb("LOW", [P, E, E], F32)
        MH = sb("MH", [P, QK], F32)
        LN = {k: (sb(f"ST{k}", [P, 6], F32), sb(f"MV{k}", [P, 2], F32), sb(f"VE{k}", [P, 1], F32),
                  sb(f"RS{k}", [P, 1], F32), sb(f"XN{k}", [P, D], F32), sb(f"XT{k}", [P, KD, P], F32))
              for k in ("f", "a")}
        NM = sb("NM", [P, 1], F32)
        EX = sb("EX", [P, E], F32)
        ES = sb("ES", [P, 1], F32)
        EC = sb("EC", [P, 1], F32)
        PR = sb("PR", [P, E], F32)
        EQ = sb("EQ", [P, E, E], F32)
        GT = sb("GT", [P, E, E], F32)
        CUM = sb("CUM", [P, E], F32)
        QKV = sb("QKV", [P, QKVW], F32)
        SQ = sb("SQ", [P, QK * HD], F32)
        SS = sb("SS", [P, QK], F32)
        MS = sb("MS", [P, QK], F32)
        RR = sb("RR", [P, QK], F32)
        QN = sb("QN", [P, QK * HD], F32)
        RA = sb("RA", [P, QK * HD], F32)
        RB = sb("RB", [P, QK, 2, HD // 2], F32)
        QS = sb("QS", [P, H, 4, HD], F16)
        KS = sb("KS", [P, KVH, 2, 4, HD], F16)
        VR = sb("VR", [P, 2, KVH, HD], F32)
        VS = sb("VS", [P, 3, 2, KVH, VW], BF16)
        QT = sb("QT", [P, 2, 2, H // 2, P], F16)
        KT = sb("KT", [P, 2, KVH, 2, 2, P], F16)
        MX = sb("MX", [P, 2, G], F32)
        NB = sb("NB", [P, 2, G], F32)
        RC = sb("RC", [P, 2 * G], F32)
        RD = sb("RD", [P, 2 * G, HD], F32)
        OB = sb("OB", [P, 2, 2, KVH, G * HD], F32)
        OS = sb("OS", [P, D], F32)
        OT = sb("OT", [P, KD, P], F32)

        GB = [ctx.enter_context(nc.psum_tensor(f"G{i}", [P, BLK], F32)) for i in range(2)]
        UB = [ctx.enter_context(nc.psum_tensor(f"U{i}", [P, BLK], F32)) for i in range(2)]
        YB = ctx.enter_context(nc.psum_tensor("YB", [P, BLK], F32))
        BA, BB, BC = (ctx.enter_context(nc.psum_tensor(f"B{c}", [P, BLK], F32)) for c in "ABC")

        LAST = (YB, BA, BB, GB[0])

        s_x0, s_x1 = sem("s_x0"), sem("s_x1")
        s_rw, s_aw = sem("s_rw"), sem("s_aw")
        s_w = [sem(f"s_w{j}") for j in range(3)]
        s_early = [sem(f"s_early{j}") for j in range(3)]
        s_i1, s_i2 = sem("s_i1"), sem("s_i2")
        s_ag, s_apart = sem("s_ag"), sem("s_apart")
        N_I1 = 8
        s_st = sem("s_st")

        items = range(2)
        L = {}
        for name, stage_, labels in [
            ("p_gu", "ff", [f"gu{i}" for i in range(8)]),
            ("p_y", "ff", [f"y{i}" for i in range(8)]),
            ("p_fp", "fp", ["tp"]), ("p_lg", "fp", ["lg"]),
            ("p_ap", "ap", ["tp"]), ("p_qk", "qk", ["qkv"]), ("p_a3", "a3", ["qt", "kt"]),
            ("p_hd", "hd", ["sa0", "sb0", "pt0.0", "pt0.1", "pt0.2", "pv0", "sa1", "sb1", "pt1.0", "pt1.1", "pt1.2"]),
            ("p_pw", "pw", ["pv"]), ("p_op", "op", ["tp", "mm"]),
            ("a_ff", "ff", [f"{s}{i}" for i in range(8) for s in ("tanh", "hi")]),
            ("a_xt", "fp", ["xt"]), ("a_rt", "fp", ["ex"]),
            ("a_wp", "wp", [f"{s}{x}.{j}" for x in items for s, j in (("hi", 0), ("hi", 1), ("hi", 2), ("sc", 2))]),
            ("a_ap", "ap", ["xt"]), ("a_a3", "a3", ["qhi", "khi0", "khi1", "qe"]),
            ("a_hd", "hd", [f"{s}{x}.{i}" for x in items for s, c in (("e", 8), ("h", 3)) for i in range(c)]),
            ("a_op", "op", ["ot"]),
            ("p_pre", "pre", ["tp0", "tp1", "tp2", "tp3", "lg"]),
            ("a_pre", "pre", [f"{s}{t}" for t in range(BT) for s in ("xt", "xh")] + ["ex"]),
            ("v_pre", "pre", [f"{s}{t}" for s in ("stats", "aggr") for t in range(BT)] + ["eps"] +
             [f"{s}{t}" for s in ("xn", "xl") for t in range(BT)] + ["mx", "sub", "sum", "rc", "p", "eq", "gt", "cum", "wt"]),
            ("g_pre", "pre", ["rs", "eq", "b", "bp"]),
            ("v_ff", "ff", [f"{s}{i}" for i in range(8) for s in ("t", "h")]),
            ("v_y", "ff", [f"y{i}" for i in range(8)]), ("v_wc", "ff", ["wc0", "wc1"]),
            ("v_ln", "fp", ["stats", "aggr", "eps", "xn"]), ("v_sp", "fp", ["xh", "xl"]),
            ("v_rt", "fp", ["mx", "rc", "p", "eq", "gt", "cum", "wt"]),
            ("v_wp", "wp", [f"{s}{x}" for x in items for s in ("mx.0.", "mx.1.", "mx.2.", "cl", "pe", "rc", "sc", "tsc", "gu", "cf", "lo.0.", "lo.1.")]),
            ("v_al", "ap", ["stats", "aggr", "eps", "xn"]),
            ("v_qk", "qk", ["qb", "ss", "ms"]),
            ("v_a3", "a3", ["qn", "rb0", "rb1", "r", "qlo", "klo0", "klo1", "ke0", "ke1"]),
            ("v_hd", "hd", ["mx0.0", "mx0.1", "nb0.0", "mx0.2", "nb0.1", "l0.0", "l0.1", "l0.2", "rc0", "rd0", "ob0",
                            "mx1.0", "mx1.1", "nb1.0", "mx1.2", "nb1.1", "l1.0", "l1.1", "l1.2"]),
            ("v_pw", "pw", ["rc", "rd", "ob"]), ("v_op", "op", ["ad"]),
            ("g_ff", "ff", [f"lo{i}" for i in range(8)]),
            ("g_ln", "fp", ["rs"]), ("g_rt", "fp", ["eq", "b", "bp"]), ("g_wp", "wp", [f"{s}{x}" for x in items for s in ("ar", "lo.2.")]),
            ("g_al", "ap", ["rs", "bo"]), ("g_qk", "qk", ["sq", "rr", "sg", "v1", "r1", "v2", "r2", "v3"]), ("g_a3", "a3", ["ra"]),
            ("g_os", "os", ["os"]),
            ("g_hd", "hd", ["k0.0", "k0.1", "k1.0", "k1.1"]),
        ]:
            extra = {"p_y": 4, "v_y": 4, "a_wp": 4, "v_wp": 12, "g_wp": 2}.get(name, 0)
            L[name] = Lane(sem(name), stage_, labels, extra)

        def give_credit(eng, prefix):
            for name, lane in L.items():
                if name.startswith(prefix):
                    eng.sem_inc(lane.sem, lane.credit)

        def wait_apart(lane, eng, n, label):
            lane.wait(eng, n, label)
            if not isinstance(n, int):
                eng.sem_inc(s_apart, 1)

        def steps(eng, body):
            for a, b in RUNS:
                if b - a == 1:
                    body(a, active(a))
                else:
                    with eng.Fori(a, b) as n:
                        body(n, active(a))

        def blk(n):
            return ((n - 4) // BT) % (NT // BT)

        def xpar(n):
            return (n // BT + 1) % 2

        def loaded(n, x):
            return early if isinstance(n, int) and (n, x) == (4, 0) else stage

        def bank_ready(eng, n, act, use, banks="ABC"):
            before = active(n - 1) if isinstance(n, int) else act
            for bank in banks:
                if bank not in BANK_USES[USE[use]][1]:
                    continue
                found = None
                for f, who in reversed(BANK_USES[:USE[use]]):
                    if f in act and bank in who:
                        found = (who[bank], n)
                        break
                if found is None:
                    for f, who in reversed(BANK_USES):
                        if f in before and bank in who:
                            found = (who[bank], n - 1)
                            break
                if found is not None:
                    (lane, label), m = found
                    L[lane].wait(eng, m, label)

        def pe_gu(eng, n, act, i):
            h, m = divmod(i, 4)
            e = (n % 4) * 2 + h
            if isinstance(n, int) and n == 4:
                if i == 0:
                    for t in range(BT):
                        L["v_pre"].wait(eng, 3, f"xl{t}")
            elif i == 0:
                L["v_sp"].wait(eng, n - 1 if "fp" in act else 31, "xl")
            new = i % 4 == 0 and "wp" in act
            if i < 2:
                L["v_ff"].wait(eng, n - 1, f"h{i + 6}")
            else:
                L["v_ff"].wait(eng, n, f"h{i - 2}")
            for j, bank in ((0, GB[i % 2]), (1, UB[i % 2])):
                q = 0
                if new:
                    L["a_wp"].wait(eng, n if h else n - 1, f"hi{1 - h}.{j}")
                for k in range(KD):
                    for wl, xl in ((0, 0), (0, 1), (1, 0)):
                        if new and wl == 1 and k == 0:
                            L["v_wp"].wait(eng, n if h else n - 1, f"lo.{j}.{1 - h}")
                        mm = eng.matmul(bank[:, :], W[:, e, wl, j, k * I + m * P:k * I + (m + 1) * P],
                                        XS16[:, xpar(n), xl, k, :, :].rearrange("p a b -> p (a b)"),
                                        start=(q == 0), stop=(q == 3 * KD - 1))
                        q += 1
            L["p_gu"].inc(mm, f"gu{i}")

        def y_bank(act, i):
            return YB if i % 2 == 0 or act & {"hd", "pw"} else BC

        def pe_y(eng, n, act, i, bank=None, ks=range(KI)):
            h, m = divmod(i, 4)
            par = 1 - h
            last_y = bank is not None
            bank = bank or y_bank(act, i)
            e = (n % 4) * 2 if h else ((n + 3) % 4) * 2 + 1
            if i % 4 == 0 and "wp" in act or isinstance(n, int) and n == 8 and i == 0:
                L["g_wp"].wait(eng, n - 1, f"lo.2.{h}")
            if isinstance(n, int) and n == 4 and i == 4:
                L["v_pre"].wait(eng, 3, "sub")
            back = 1 if act & {"hd", "pw"} else 2
            if isinstance(n, int) and active(n - 1) & {"hd", "pw"} and i == 0:
                back = 1
            if not last_y or (m == 0 and ks[0] == 0):
                L["v_y"].wait(eng, n if i >= back else n - 1, f"y{(i - back) % 8}")
            for k in ks:
                for hl, wl in ((0, 0), (0, 1), (1, 0)):
                    if m == 0 and wl == 0:
                        L["g_ff" if hl else "a_ff"].wait(eng, n if h else n - 1, f"{'lo' if hl else 'hi'}{KI * par + k}")
                    mm = eng.matmul(bank[:, 0:D], HS[:, par, hl, k, m * P:(m + 1) * P], W[:, e, wl, 2, k * D:(k + 1) * D],
                                    start=(k + hl + wl == 0), stop=(k == KI - 1 and hl == 1))
            if ks[-1] == KI - 1:
                L["p_y"].inc(mm, f"y{i}")

        def pe_tp(eng, lane, ready, n, k_, bank, c):
            L[ready].wait(eng, n, "xn")
            for k in range(KD):
                mm = eng.transpose(bank[:, c + k * P:c + (k + 1) * P], LN[k_][4][:, k * P:(k + 1) * P], ident[:, :])
            L[lane].inc(mm, "tp")

        def pe_lg(eng, n, bank):
            L["a_xt"].wait(eng, n, "xt")
            for k in range(KD):
                mm = eng.matmul(bank[:, 0:E], LN["f"][5][:, k, :], RW[:, k, :], start=(k == 0), stop=(k == KD - 1))
            L["p_lg"].inc(mm, "lg")

        def pe_qkv(eng, n, act):
            bank_ready(eng, n, act, "qk")
            L["a_ap"].wait(eng, n - 1, "xt")
            for k in range(KD):
                mm = eng.matmul(BA[:, 0:QKVW], LN["a"][5][:, k, :], WQKV[:, k, :], start=(k == 0), stop=(k == KD - 1))
            L["p_qk"].inc(mm, "qkv")

        def pe_a3(eng, n, act):
            bank_ready(eng, n, act, "a3")
            L["v_a3"].wait(eng, n, "klo1")
            L["a_a3"].wait(eng, n, "khi1")
            qs = QS[:, :, :, :].rearrange("p h s c -> p (h s c)")
            ks = KS[:, :, :, :, :].rearrange("p h u s c -> p (h u s c)")
            a16, b16 = BA[:, :].bitcast(F16), BB[:, :].bitcast(F16)
            for j in range(H // 2):
                mm = eng.transpose(a16[:, j * P:(j + 1) * P], qs[:, j * P:(j + 1) * P], ident16[:, :])
            L["p_a3"].inc(mm, "qt")
            for j in range(KVH):
                mm = eng.transpose(b16[:, j * P:(j + 1) * P], ks[:, j * P:(j + 1) * P], ident16[:, :])
            L["p_a3"].inc(mm, "kt")

        def pe_scores(eng, n, act, it):
            par, kv = ((n - 12) // 2) % 2, 2 * (n % 2) + it
            if it == 0:
                L["a_a3"].wait(eng, n - 1 if "a3" in act else 25, "qe")
                L["v_a3"].wait(eng, n - 1 if "a3" in act else 25, "ke1")
            bank_ready(eng, n, act, f"sc{it}", "A")
            for jj in range(2):
                eng.matmul(BA[:, jj * 2 * P:(jj + 1) * 2 * P], QT[:, par, 0, 2 * kv + jj, :],
                           KT[:, par, kv, :, 0, :], start=(jj == 0), stop=False, skip_group_check=True)
            mm = eng.matmul(BA[:, :], ident16[:, :], MB[:, :, :].rearrange("p a b -> p (a b)"), start=False, stop=True,
                            skip_group_check=True)
            L["p_hd"].inc(mm, f"sa{it}")
            bank_ready(eng, n, act, f"sc{it}", "BC")
            for jj, bank in ((0, BB), (1, BC)):
                eng.matmul(bank[:, :], QT[:, par, 1, 2 * kv + jj, :],
                           KT[:, par, kv, :, :, :].rearrange("p a b c -> p (a b c)"), start=True, stop=False,
                           skip_group_check=True)
                mm = eng.matmul(bank[:, :].rearrange("p (a b) -> p a b", a=2)[:, :, P:2 * P], ident16[:, :],
                                MB[:, 0:2, :], start=False, stop=True, skip_group_check=True)
            L["p_hd"].inc(mm, f"sb{it}")

        def pe_pt(eng, n, act, it):
            for b, bank in enumerate((BA, BB, BC)):
                if b == 0:
                    L["g_hd"].wait(eng, n, f"k{it}.0")
                elif b == 1:
                    L["a_hd"].wait(eng, n, f"e{it}.7")
                else:
                    L["g_hd"].wait(eng, n, f"k{it}.1")
                bank_ready(eng, n, act, f"pt{it}", "ABC"[b])
                for g in range(G):
                    mm = eng.transpose(bank[:, g * P:(g + 1) * P], P32[:, b, g, :], ident[:, :])
                L["p_hd"].inc(mm, f"pt{it}.{b}")

        def pe_pv(eng, n, act, lane, label, use, m, ready, kv):
            bank_ready(eng, n, act, use)
            L["v_hd"].wait(eng, m, ready)
            par = ((m - 12) // 2) % 3
            for qt in range(2):
                for g in range(G):
                    o = BC[:, (qt * G + g) * VW:(qt * G + g + 1) * VW]
                    terms = [(0, 0)] if qt == 0 else [(1, 0), (2, 1)]
                    q = 0
                    for b, kt in terms:
                        for ph in (PH, PL):
                            mm = eng.matmul(o, ph[:, b, g, :], VS[:, par, kt, kv, :], start=(q == 0),
                                            stop=(q == 2 * len(terms) - 1))
                            q += 1
            L[lane].inc(mm, label)

        def pe_op_tp(eng, n, act):
            bank_ready(eng, n, act, "op.tp")
            L["g_os"].wait(eng, n - 1, "os")
            for k in range(KD):
                mm = eng.transpose(BB[:, k * P:(k + 1) * P], OS[:, k * P:(k + 1) * P], ident[:, :])
            L["p_op"].inc(mm, "tp")

        def pe_op_mm(eng, n, act):
            if "a3" not in act:
                bank_ready(eng, n, act, "op.mm")
            L["a_op"].wait(eng, n, "ot")
            for k in range(KD):
                mm = eng.matmul(BB[:, D:2 * D], OT[:, k, :], WO[:, k, :], start=(k == 0), stop=(k == KD - 1))
            L["p_op"].inc(mm, "mm")

        def pe_body(eng, n, act):
            for p in range(16):
                i = p // 2
                if p % 2 == 0:
                    pe_gu(eng, n, act, i)
                elif not (isinstance(n, int) and n == 4 and i < 4):
                    pe_y(eng, n, act, i)
                if p == 0 and isinstance(n, int) and n == RANGES["qk"][0]:
                    eng.wait_ge(s_aw, 16 * 11)
                if p == 0 and "qk" in act:
                    pe_qkv(eng, n, act)
                if p == 0 and "op" in act:
                    pe_op_tp(eng, n, act)
                if p == 1 and "pw" in act:
                    pe_pv(eng, n, act, "p_pw", "pv", "pw", n - 1, "l1.2", 2 * ((n + 1) % 2) + 1)
                if p == 2 and "hd" in act:
                    pe_scores(eng, n, act, 0)
                if p == 5 and "fp" in act:
                    bank_ready(eng, n, act, "fp.tp")
                    pe_tp(eng, "p_fp", "v_ln", n, "f", BA, 0)
                    if "ap" in act:
                        pe_tp(eng, "p_ap", "v_al", n, "a", BA, D)
                if p == 6 and "hd" in act:
                    pe_pt(eng, n, act, 0)
                if p == 8 and "a3" in act:
                    pe_a3(eng, n, act)
                if p == 8 and "op" in act:
                    pe_op_mm(eng, n, act)
                if p == 9 and "hd" in act:
                    pe_pv(eng, n, act, "p_hd", "pv0", "pv0", n, "l0.2", 2 * (n % 2))
                if p == 10 and "hd" in act:
                    pe_scores(eng, n, act, 1)
                if p == 13 and "fp" in act:
                    bank_ready(eng, n, act, "fp.lg")
                    pe_lg(eng, n, BA)
                if p == 14 and "hd" in act:
                    pe_pt(eng, n, act, 1)

        def act_tanh(eng, n, i):
            e = (n % 4) * 2 + i // 4
            L["p_gu"].wait(eng, n, f"gu{i}")
            wait_apart(L["v_ff"], eng, n - 1 if i < 2 else n, f"h{(i - 2) % 8}")
            L["a_ff"].inc(eng.activation(TS[:, i % 2, :], GB[i % 2][:, :], ACT.Tanh, scale=TSC[:, e, :]), f"tanh{i}")

        def act_hi(eng, n, i):
            h, m = divmod(i, 4)
            L["v_ff"].wait(eng, n, f"h{i}")
            if m == 0:
                L["p_y"].wait(eng, n if h else n - 1, "y3" if h else "y7")
            L["a_ff"].inc(eng.activation(HS[:, h, 0, m, :], H32[:, i % 2, :], ACT.Copy), f"hi{i}")

        def act_xt(eng, n, both):
            L["p_fp"].wait(eng, n, "tp")
            if both:
                L["p_ap"].wait(eng, n, "tp")
            L["v_sp"].wait(eng, n - 1, "xl")
            L["p_lg"].wait(eng, n - 1, "lg")
            L["a_xt"].inc(eng.activation(LN["f"][5][:, :, :].rearrange("p a b -> p (a b)"),
                                         BA[:, 0:D], ACT.Copy), "xt")

        def act_rt(eng, n, bank):
            L["p_lg"].wait(eng, n, "lg")
            L["v_rt"].wait(eng, n, "mx")
            L["a_rt"].inc(eng.activation(EX[:, :], bank[:, 0:E], ACT.Exp, bias=NM[:, 0:1], accum_out=ES[:, 0:1]), "ex")

        def act_wp(eng, n, x, js):
            e = 2 * (n - 4) + 1 + x
            raw = loaded(n, x)
            wait_apart(L["v_wp"], eng, n, f"sc{x}")
            for j in js:
                L["a_wp"].inc(eng.activation(W[:, e, 0, j, :], raw[:, j, :], ACT.Copy, scale=SCW[:, j:j + 1]), f"hi{x}.{j}")
                if j == 2:
                    L["a_wp"].inc(eng.activation(raw[:, j, :], raw[:, j, :], ACT.Copy, scale=SCW[:, j:j + 1]), f"sc{x}.{j}")

        def act_exps(eng, n, it, qt, heads):
            kv = 2 * (n % 2) + it
            L["v_hd"].wait(eng, n, f"nb{it}.{qt}")
            wait_apart(L["p_hd"], eng, n if it else n - 1, "pt0.2" if it else "pt1.2")
            for g in heads:
                if qt == 0:
                    s, p = BA[:, g * P:(g + 1) * P], P32[:, 0, g, :]
                else:
                    s = (BB, BC)[g // 2][:, (g % 2) * 2 * P:(g % 2 + 1) * 2 * P].rearrange("p (a b) -> p a b", a=2)
                    p = P32[:, 1:3, g, :]
                L["a_hd"].inc(eng.activation(p, s, ACT.Exp, bias=NB[:, qt, g:g + 1], scale=AG[:, kv, g:g + 1]),
                              f"e{it}.{qt * G + g}")

        def act_ph(eng, n, it):
            L["p_hd" if it else "p_pw"].wait(eng, n, "pv0" if it else "pv")
            for b, bank in enumerate((BA, BB, BC)):
                L["p_hd"].wait(eng, n, f"pt{it}.{b}")
                L["a_hd"].inc(eng.activation(PH[:, b, :, :].rearrange("p a b -> p (a b)"), bank[:, :], ACT.Copy), f"h{it}.{b}")

        def act_ap_xt(eng, n):
            L["p_ap"].wait(eng, n, "tp")
            if not (isinstance(n, int) and n == 8):
                L["p_qk"].wait(eng, n, "qkv")
            L["a_ap"].inc(eng.activation(LN["a"][5][:, :, :].rearrange("p a b -> p (a b)"), BA[:, D:2 * D], ACT.Copy), "xt")

        def act_a3_hi(eng, n):
            L["v_a3"].wait(eng, n, "r")
            L["p_a3"].wait(eng, n - 1, "kt")
            q = RA[:, 0:H * HD].rearrange("p (h c) -> p h c", c=HD)
            k = RA[:, H * HD:].rearrange("p (h c) -> p h c", c=HD)
            L["a_a3"].inc(eng.activation(QS[:, :, 0:4:2, :], q.unsqueeze(2).broadcast_to([P, H, 2, HD]), ACT.Copy), "qhi")
            for s in range(2):
                L["a_a3"].inc(eng.activation(KS[:, :, :, s, :], k.unsqueeze(2).broadcast_to([P, KVH, 2, HD]), ACT.Copy), f"khi{s}")

        def act_qe(eng, n):
            wait_apart(L["p_a3"], eng, n, "qt")
            L["a_a3"].inc(eng.activation(QT[:, ((n - 10) // 2) % 2, n % 2, :, :].rearrange("p a b -> p (a b)"),
                                         BA[:, :].bitcast(F16), ACT.Copy), "qe")

        def act_ot(eng, n):
            L["p_op"].wait(eng, n, "tp")
            L["p_op"].wait(eng, n - 1, "mm")
            L["a_op"].inc(eng.activation(OT[:, :, :].rearrange("p a b -> p (a b)"), BB[:, 0:D], ACT.Copy), "ot")

        def act_body(eng, n, act):
            first = isinstance(n, int) and n == 4
            last = isinstance(n, int) and n == 7
            for p in range(16):
                i = p // 2
                if first and p == 0:
                    L["v_pre"].wait(eng, 3, "sub")
                    L["a_pre"].inc(eng.activation(EX4[:, :, :], LG4[:, :, :], ACT.Exp), "ex")
                if isinstance(n, int) and n == RANGES["a3"][0] and p == 0:
                    eng.wait_ge(s_ag, 4)
                if p in (4, 12) and "hd" in act:
                    act_exps(eng, n, p // 8, 0, range(G))
                if p == 1 and "op" in act:
                    act_ot(eng, n)
                if p % 2 == 0:
                    act_tanh(eng, n, i)
                if p == 2 and "a3" in act:
                    act_a3_hi(eng, n)
                if p in (4, 12) and "hd" in act:
                    act_exps(eng, n, p // 8, 1, (0, 1))
                if p == 5 and "fp" in act:
                    act_xt(eng, n, "ap" in act)
                if p == 5 and "ap" in act:
                    act_ap_xt(eng, n)
                if p in (7, 15) and "hd" in act:
                    act_ph(eng, n, p // 8)
                if p == 9 and "a3" in act:
                    act_qe(eng, n)
                if p in (5, 13) and "hd" in act:
                    act_exps(eng, n, p // 8, 1, (2, 3))
                if p % 2 == 1:
                    act_hi(eng, n, i)
                if p == 13 and "fp" in act:
                    act_rt(eng, n, BA)
                if "wp" in act and p % 8 in (4, 5, 6) and not (last and p > 7):
                    act_wp(eng, n, p // 8, (p % 8 - 4,))

        def dve_t(eng, n, i):
            L["a_ff"].wait(eng, n, f"tanh{i}")
            L["v_ff"].inc(eng.scalar_tensor_tensor(TS[:, i % 2, :], TS[:, i % 2, :], 1.0, GB[i % 2][:, :],
                                                   ALU.add, ALU.mult), f"t{i}")

        def dve_h(eng, n, i):
            L["v_ff"].wait(eng, n, f"t{i}")
            m, j = (n, i - 2) if i >= 2 else (n - 1, i + 6)
            L["a_ff"].wait(eng, m, f"hi{j}")
            L["g_ff"].wait(eng, m, f"lo{j}")
            L["v_ff"].inc(eng.scalar_tensor_tensor(H32[:, i % 2, :], TS[:, i % 2, :], H_C, UB[i % 2][:, :],
                                                   ALU.mult, ALU.mult), f"h{i}")

        def dve_wc(eng, n, act, h):
            e = (n % 4) * 2 + h
            if h == 0:
                if isinstance(n, int) and n == 4:
                    L["v_pre"].wait(eng, 3, "wt")
                else:
                    L["v_rt"].wait(eng, n - 1 if "fp" in act else 31, "wt")
            L["v_y"].wait(eng, n if h else n - 1, "y3" if h else "y7")
            L["v_wc"].inc(eng.tensor_tensor(WTC[:, h, :], WT[:, blk(n), :, e], CF[:, e, :].broadcast_to([P, BT]),
                                            ALU.mult), f"wc{h}")

        def dve_y(eng, n, act, i, bank=None):
            h, m = divmod(i, 4)
            L["p_y"].wait(eng, n, f"y{i}")
            L["v_y"].wait(eng, n - 1 if h == 0 else n, f"y{(i + 4) % 8}")
            L["v_wc"].wait(eng, n - 1 if h == 0 else n, f"wc{1 - h}")
            b = blk(n) if h else blk(n - 1)
            x = X[:, b * BT + m, :]
            L["v_y"].inc(eng.scalar_tensor_tensor(x, (bank or y_bank(act, i))[:, 0:D], WTC[:, 1 - h, m:m + 1], x, ALU.mult, ALU.add), f"y{i}")

        def dve_ln(eng, n, lane, k, t):
            ST, MV, VE, _, _, _ = LN[k]
            L[lane].inc(eng.bn_stats(ST[:, :], X[:, t, :]), "stats")
            wait_apart(L[lane], eng, n, "stats")
            L[lane].inc(eng.bn_aggr(MV[:, :], ST[:, :]), "aggr")
            L[lane].wait(eng, n, "aggr")
            L[lane].inc(eng.tensor_scalar(VE[:, :], MV[:, 1:2], LN_EPS, None, ALU.add), "eps")

        def dve_xn(eng, n, lane, glane, k, t, free):
            _, MV, _, RS, XN, _ = LN[k]
            L[glane].wait(eng, n, "rs")
            L[free].wait(eng, n - 1, "tp")
            L[lane].inc(eng.tensor_scalar(XN[:, :], X[:, t, :], MV[:, 0:1], RS[:, 0:1], ALU.subtract, ALU.mult), "xn")

        def dve_split(eng, n):
            XT = LN["f"][5]
            par, c = (n // BT) % 2, n % BT
            L["a_xt"].wait(eng, n, "xt")
            if not (isinstance(n, int) and n == 4):
                L["p_gu"].wait(eng, n - 1, "gu7")
            L["v_sp"].inc(eng.tensor_scalar(XS16[:, par, 0, :, c, :], XT[:, :, :], XS, None, ALU.mult), "xh")
            L["v_sp"].wait(eng, n, "xh")
            L["v_sp"].inc(eng.scalar_tensor_tensor(XS16[:, par, 1, :, c, :], XT[:, :, :], XS, XS16[:, par, 0, :, c, :],
                                                   ALU.mult, ALU.subtract), "xl")

        def dve_rt1(eng, n, bank):
            L["p_lg"].wait(eng, n, "lg")
            L["v_rt"].inc(eng.tensor_reduce(NM[:, :], bank[:, 0:E], AX.X, ALU.max, negate=True), "mx")

        def dve_rt2(eng, n):
            L["a_rt"].wait(eng, n, "ex")
            L["v_rt"].inc(eng.reciprocal(EC[:, :], ES[:, :]), "rc")
            L["v_rt"].wait(eng, n, "rc")
            L["v_rt"].inc(eng.tensor_scalar(PR[:, :], EX[:, :], EC[:, 0:1], None, ALU.mult), "p")
            L["v_rt"].wait(eng, n, "p")
            pf = PR[:, :].unsqueeze(1).broadcast_to([P, E, E])
            pe = PR[:, :].unsqueeze(2).broadcast_to([P, E, E])
            L["v_rt"].inc(eng.tensor_tensor(EQ[:, :, :], pf, pe, ALU.is_equal), "eq")
            L["v_rt"].inc(eng.tensor_tensor(GT[:, :, :], pf, pe, ALU.is_gt), "gt")

        def dve_rt3(eng, n):
            L["g_rt"].wait(eng, n, "bp")
            L["v_rt"].inc(eng.tensor_reduce(CUM[:, :], EQ[:, :, :], AX.X, ALU.add), "cum")
            L["v_rt"].wait(eng, n, "cum")
            L["v_rt"].inc(eng.scalar_tensor_tensor(WT[:, (n // BT) % (NT // BT), n % BT, :], CUM[:, :], TOP_P, PR[:, :],
                                                   ALU.is_le, ALU.mult), "wt")

        def dve_mx(eng, n, x, js):
            e = 2 * (n - 4) + 1 + x
            raw = loaded(n, x)
            for j in js:
                if raw is early:
                    eng.wait_ge(s_early[j], 16)
                else:
                    eng.wait_ge(s_w[j], 16 * e if not isinstance(n, int) or e > 1 else 16)
                L["v_wp"].inc(eng.tensor_reduce(MXW[:, j:j + 1], raw[:, j, :], AX.X, ALU.max,
                                                apply_absolute_value=True), f"mx.{j}.{x}")

        def dve_scale(eng, n, x):
            e = 2 * (n - 4) + 1 + x
            L["g_wp"].wait(eng, n, f"ar{x}")
            L["v_wp"].inc(eng.tensor_scalar(MAW[:, :], MAW[:, :], 1e-30, None, ALU.max), f"cl{x}")
            L["v_wp"].wait(eng, n, f"cl{x}")
            L["v_wp"].inc(eng.tensor_scalar(PEW[:, :].bitcast(I32), MAW[:, :].bitcast(I32), 0x7F800000, None,
                                            ALU.bitwise_and), f"pe{x}")
            L["v_wp"].wait(eng, n, f"pe{x}")
            L["v_wp"].inc(eng.reciprocal(SCW[:, :], PEW[:, :]), f"rc{x}")
            L["v_wp"].wait(eng, n, f"rc{x}")
            L["v_wp"].inc(eng.tensor_scalar(SCW[:, :], SCW[:, :], 2.0 ** WTOP, None, ALU.mult), f"sc{x}")
            L["v_wp"].inc(eng.tensor_scalar(TSC[:, e, :], PEW[:, 0:1], TANH_C, None, ALU.mult), f"tsc{x}")
            L["v_wp"].inc(eng.tensor_tensor(GUD[:, :], PEW[:, 0:1], PEW[:, 1:2], ALU.mult), f"gu{x}")
            L["v_wp"].wait(eng, n, f"gu{x}")
            L["v_wp"].inc(eng.tensor_scalar(CF[:, e, :], GUD[:, :], PEW[:, 2:3], CF_C, ALU.mult, ALU.mult), f"cf{x}")

        def dve_wlo(eng, n, x, j):
            e = 2 * (n - 4) + 1 + x
            L["a_wp"].wait(eng, n, f"hi{x}.{j}")
            L["v_wp"].inc(eng.scalar_tensor_tensor(W[:, e, 1, j, :], loaded(n, x)[:, j, :], SCW[:, j:j + 1], W[:, e, 0, j, :],
                                                   ALU.mult, ALU.subtract), f"lo.{j}.{x}")

        def dve_qb(eng, n):
            L["p_qk"].wait(eng, n, "qkv")
            L["g_qk"].wait(eng, n - 1, "v3")
            L["v_qk"].inc(eng.tensor_tensor(QKV[:, :], BA[:, 0:QKVW], BQKV[:, :], ALU.add), "qb")

        def dve_ss(eng, n):
            L["g_qk"].wait(eng, n, "sq")
            L["v_qk"].inc(eng.tensor_reduce(SS[:, :], SQ[:, :].rearrange("p (h c) -> p h c", c=HD), AX.X, ALU.add), "ss")
            L["v_qk"].wait(eng, n, "ss")
            L["v_qk"].inc(eng.tensor_scalar(MS[:, :], SS[:, :], 1.0 / HD, RMS_EPS, ALU.mult, ALU.add), "ms")

        def dve_qn(eng, n):
            L["g_qk"].wait(eng, n - 1, "sg")
            L["v_a3"].inc(eng.tensor_tensor(QN[:, :].rearrange("p (h c) -> p h c", c=HD),
                                            QKV[:, 0:QK * HD].rearrange("p (h c) -> p h c", c=HD),
                                            RR[:, :].unsqueeze(2).broadcast_to([P, QK, HD]), ALU.mult), "qn")

        def dve_rb(eng, n, a):
            L["v_a3"].wait(eng, n, "qn")
            q4 = QN[:, :].rearrange("p (h a c) -> p h a c", a=2, c=HD // 2)
            table = (SIN, NSIN)[a]
            L["v_a3"].inc(eng.tensor_tensor(RB[:, :, a, :], q4[:, :, 1 - a, :],
                                            table[:, n % 2, :].unsqueeze(1).broadcast_to([P, QK, HD // 2]), ALU.mult), f"rb{a}")

        def dve_r(eng, n):
            L["v_a3"].wait(eng, n, "rb1")
            L["g_a3"].wait(eng, n, "ra")
            L["v_a3"].inc(eng.tensor_tensor(RA[:, :], RA[:, :], RB[:, :, :, :].rearrange("p h a c -> p (h a c)"), ALU.add), "r")

        def dve_a3_lo(eng, n):
            q = RA[:, 0:H * HD].rearrange("p (h c) -> p h c", c=HD)
            k = RA[:, H * HD:].rearrange("p (h c) -> p h c", c=HD)
            L["a_a3"].wait(eng, n, "qhi")
            L["v_a3"].inc(eng.tensor_tensor(QS[:, :, 1:4:2, :], q.unsqueeze(2).broadcast_to([P, H, 2, HD]),
                                            QS[:, :, 0:4:2, :], ALU.subtract), "qlo")
            L["a_a3"].wait(eng, n, "khi1")
            for s in range(2):
                L["v_a3"].inc(eng.tensor_tensor(KS[:, :, :, 2 + s, :], k.unsqueeze(2).broadcast_to([P, KVH, 2, HD]),
                                                KS[:, :, :, s, :], ALU.subtract), f"klo{s}")

        def dve_ke(eng, n, act):
            L["p_a3"].wait(eng, n, "kt")
            if "op" in act:
                L["p_op"].wait(eng, n, "mm")
            b16 = BB[:, :].bitcast(F16)[:, 0:KVH * P].rearrange("p (a b) -> p a b", a=KVH)
            par, t = ((n - 10) // 2) % 2, n % 2
            for h in range(2):
                lo, hi = h * P // 2, (h + 1) * P // 2
                L["v_a3"].inc(eng.tensor_copy(KT[lo:hi, par, :, h, t, :], b16[lo:hi, :, :]), f"ke{h}")

        def dve_max(eng, n, it, qt):
            kv = 2 * (n % 2) + it

            def top(j):
                x = (BA[:, :].rearrange("p (g k) -> p g k", g=G) if j == 0 else
                     (BB, BC)[j - 1][:, :].rearrange("p (g k) -> p g k", g=2))
                out = MX[:, 0, :] if j == 0 else MX[:, 1, 2 * j - 2:2 * j]
                L["v_hd"].inc(eng.tensor_reduce(out, x, AX.X, ALU.max), f"mx{it}.{j}")

            def bias(qt, label):
                L["v_hd"].wait(eng, n, label)
                L["a_hd"].wait(eng, n if it else n - 1, f"e{1 - it}.{7 if qt else 3}")
                L["v_hd"].inc(eng.scalar_tensor_tensor(NB[:, qt, :], MX[:, qt, :], -1.0, AG[:, kv, :], ALU.mult, ALU.mult),
                              f"nb{it}.{qt}")

            if qt == 0:
                L["p_hd"].wait(eng, n, f"sa{it}")
                top(0)
                L["p_hd"].wait(eng, n, f"sb{it}")
                top(1)
                bias(0, f"mx{it}.0")
            else:
                top(2)
                bias(1, f"mx{it}.2")

        def dve_pl(eng, n, it, bs):
            for b in bs:
                L["a_hd"].wait(eng, n, f"h{it}.{b}")
                L["v_hd"].inc(eng.tensor_tensor(PL[:, b, :, :].rearrange("p a b -> p (a b)"), (BA, BB, BC)[b][:, :],
                                                PH[:, b, :, :].rearrange("p a b -> p (a b)"), ALU.subtract), f"l{it}.{b}")

        def dve_sum(eng, n, lane, sfx, plane, plabel):
            o = BC[:, 0:2 * G * VW].rearrange("p (g c) -> p g c", c=VW)
            L[plane].wait(eng, n, plabel)
            L[lane].inc(eng.reciprocal(RC[:, :], o[:, :, VW - 1]), f"rc{sfx}")
            L[lane].inc(eng.tensor_reduce(RD[:, :, :], o[:, :, 0:3 * HD].rearrange("p g (s c) -> p g c s", s=3), AX.X, ALU.add),
                        f"rd{sfx}")

        def dve_ob(eng, n, lane, sfx, m, kv):
            L[lane].wait(eng, n, f"rd{sfx}")
            L[lane].inc(eng.tensor_tensor(OB[:, ((m - 12) // 2) % 2, :, kv, :].rearrange("p t (g c) -> p t g c", c=HD),
                                          RD[:, :, :].rearrange("p (t g) c -> p t g c", t=2),
                                          RC[:, :].rearrange("p (t g) -> p t g", t=2).unsqueeze(3).broadcast_to([P, 2, G, HD]),
                                          ALU.mult), f"ob{sfx}")

        def dve_op(eng, n):
            L["p_op"].wait(eng, n, "mm")
            L["g_al"].wait(eng, n - 7, "bo")
            x = X[:, n - 15, :]
            L["v_op"].inc(eng.tensor_tensor(x, BB[:, D:2 * D], x, ALU.add), "ad")

        def dve_fp_ready(eng, n, act):
            if isinstance(n, int) and n == 4:
                eng.wait_ge(s_x1, 16 * (NT // BT - 1))
            if not isinstance(n, int) and "op" in act or isinstance(n, int) and n > 15:
                L["v_op"].wait(eng, n - 1, "ad")

        def dve_rt4_probs(eng):
            lane = L["v_pre"]
            L["a_pre"].wait(eng, 3, "ex")
            lane.inc(eng.tensor_reduce(ES4[:, :], EX4[:, :, :], AX.X, ALU.add), "sum")
            lane.wait(eng, 3, "sum")
            lane.inc(eng.reciprocal(EC4[:, :], ES4[:, :]), "rc")
            lane.wait(eng, 3, "rc")
            lane.inc(eng.tensor_tensor(PR4[:, :, :], EX4[:, :, :], EC4[:, :].unsqueeze(2).broadcast_to([P, BT, E]), ALU.mult), "p")
            lane.wait(eng, 3, "p")
            pf = PR4[:, :, :].unsqueeze(2).broadcast_to([P, BT, E, E])
            pe = PR4[:, :, :].unsqueeze(3).broadcast_to([P, BT, E, E])
            lane.inc(eng.tensor_tensor(EQ4[:, :, :, :], pf, pe, ALU.is_equal), "eq")
            lane.inc(eng.tensor_tensor(GT4[:, :, :, :], pf, pe, ALU.is_gt), "gt")

        def dve_rt4_weights(eng):
            lane = L["v_pre"]
            L["g_pre"].wait(eng, 3, "bp")
            lane.inc(eng.tensor_reduce(CUM4[:, :, :], EQ4[:, :, :, :], AX.X, ALU.add), "cum")
            lane.wait(eng, 3, "cum")
            lane.inc(eng.scalar_tensor_tensor(WT[:, 0, :, :], CUM4[:, :, :], TOP_P, PR4[:, :, :], ALU.is_le, ALU.mult), "wt")

        def dve_constants(eng):
            eng.wait_ge(s_aw, 16 * 11)
            eng.tensor_scalar(SGN[:, :], GN[:, :], 0.0, 2.0, ALU.is_ge, ALU.mult).then_inc(s_ag, 1)
            eng.tensor_scalar(NSIN[:, :, :], SIN[:, :, :], -1.0, None, ALU.mult).then_inc(s_ag, 1)
            eng.wait_ge(s_ag, 1)
            eng.tensor_scalar(SGN[:, :], SGN[:, :], -1.0, None, ALU.add).then_inc(s_ag, 1)
            eng.wait_ge(s_ag, 3)
            eng.scalar_tensor_tensor(AG[:, :, :].rearrange("p a b -> p (a b)"), GN[:, :], float(HD) ** -0.5, SGN[:, :],
                                     ALU.mult, ALU.mult).then_inc(s_ag, 1)
            eng.wait_ge(s_ag, 4)

        def dve_body(eng, n, act):
            first = isinstance(n, int) and n == 4
            last = isinstance(n, int) and n == 7
            moved_y = (2, 6) if "wp" not in act else (1, 2, 3, 6) if last else (1, 2, 3, 5, 6, 7)
            for p in range(16):
                i = p // 2
                if p == 0 and "fp" in act:
                    dve_fp_ready(eng, n, act)
                    dve_ln(eng, n, "v_ln", "f", n % NT)
                if p == 0 and "a3" in act:
                    dve_qn(eng, n)
                if p == 1 and "qk" in act:
                    dve_qb(eng, n)
                if p == 1 and "fp" in act:
                    dve_xn(eng, n, "v_ln", "g_ln", "f", n % NT, "p_fp")
                if p == 1 and "a3" in act:
                    dve_rb(eng, n, 1)
                if p == 2 and "pw" in act:
                    dve_sum(eng, n, "v_pw", "", "p_pw", "pv")
                if p == 2 and "a3" in act:
                    dve_r(eng, n)
                if p in (3, 11):
                    if "hd" in act:
                        dve_max(eng, n, p // 8, 0)
                    if not (first and p == 3):
                        dve_y(eng, n, act, i)
                    if "hd" in act:
                        dve_max(eng, n, p // 8, 1)
                if p == 3 and "ap" in act:
                    dve_xn(eng, n, "v_al", "g_al", "a", n - 8, "p_ap")
                if p == 5 and "a3" in act:
                    dve_a3_lo(eng, n)
                if p == 5 and "qk" in act:
                    dve_ss(eng, n)
                if p in (7, 15) and "hd" in act:
                    dve_pl(eng, n, p // 8, (0, 1, 2))
                if p == 8:
                    dve_wc(eng, n, act, 0)
                if p == 9 and "a3" in act:
                    dve_ke(eng, n, act)
                if p == 9 and "op" in act:
                    dve_op(eng, n)
                if p == 10 and "hd" in act:
                    dve_sum(eng, n, "v_hd", "0", "p_hd", "pv0")
                if p == 14 and "fp" in act:
                    dve_rt1(eng, n, BA)
                    dve_rt2(eng, n)
                if "wp" in act and not (last and p > 7):
                    if p % 8 == 1:
                        if not (first and p == 1):
                            dve_y(eng, n, act, i)
                        dve_mx(eng, n, p // 8, (0, 1))
                    if p % 8 == 4:
                        dve_scale(eng, n, p // 8)
                    if p % 8 == 7 and not (first and p == 7):
                        dve_y(eng, n, act, i - 1)
                    if p == 7:
                        dve_split(eng, n)
                    if p % 8 == 5:
                        dve_wlo(eng, n, p // 8, 0)
                if first and p == 4:
                    dve_rt4_probs(eng)
                if first and p == 7:
                    dve_rt4_weights(eng)
                if isinstance(n, int) and n == RANGES["ap"][0] and p == 0:
                    dve_constants(eng)
                if p % 2 == 0:
                    if i > 0 and i not in moved_y and not (first and i < 5):
                        dve_y(eng, n, act, i - 1)
                    if p in (2, 10) and "wp" in act and not (last and p == 10):
                        dve_mx(eng, n, p // 8, (2,))
                    if p == 6 and "wp" not in act and "fp" in act:
                        dve_split(eng, n)
                    if p in (6, 14) and "wp" in act and not (last and p == 14):
                        dve_wlo(eng, n, p // 8, 1)
                    if p == 2 and "ap" in act:
                        L["v_y"].wait(eng, n, "y0")
                        dve_ln(eng, n, "v_al", "a", n - 8)
                    dve_t(eng, n, i)
                    if p == 0 and "a3" in act:
                        dve_rb(eng, n, 0)
                    if p == 2 and "pw" in act:
                        dve_ob(eng, n, "v_pw", "", n - 1, 2 * ((n + 1) % 2) + 1)
                    if p == 10 and "hd" in act:
                        dve_ob(eng, n, "v_hd", "0", n, 2 * (n % 2))
                    dve_h(eng, n, i)
                if p == 15:
                    dve_y(eng, n, act, 7)
                    dve_wc(eng, n, act, 1)
                if p == 15 and "fp" in act:
                    dve_rt3(eng, n)

        def pool_lo(eng, n, i):
            h, m = divmod(i, 4)
            L["a_ff"].wait(eng, n, f"hi{i}")
            L["g_ff"].inc(eng.tensor_tensor(HS[:, h, 1, m, :], H32[:, i % 2, :], HS[:, h, 0, m, :], ALU.subtract), f"lo{i}")

        def pool_rs(eng, n, vlane, glane, k):
            _, _, VE, RS, _, _ = LN[k]
            L[vlane].wait(eng, n, "eps")
            L[glane].inc(eng.tensor_tensor(RS[:, :], VE[:, :], MH[:, 0:1], ALU.pow), "rs")

        def pool_rank(eng, n):
            L["v_rt"].wait(eng, n, "gt")
            L["g_rt"].inc(eng.tensor_tensor(EQ[:, :, :], EQ[:, :, :], LOW[:, :, :], ALU.mult), "eq")
            L["g_rt"].wait(eng, n, "eq")
            L["g_rt"].inc(eng.tensor_tensor(EQ[:, :, :], EQ[:, :, :], GT[:, :, :], ALU.add), "b")
            L["g_rt"].wait(eng, n, "b")
            L["g_rt"].inc(eng.tensor_tensor(EQ[:, :, :], EQ[:, :, :], PR[:, :].unsqueeze(1).broadcast_to([P, E, E]), ALU.mult), "bp")

        def pool_rank4(eng):
            lane = L["g_pre"]
            eq = EQ4[:, :, :, :].rearrange("p a b c -> p a (b c)")
            L["v_pre"].wait(eng, 3, "gt")
            lane.inc(eng.tensor_tensor(eq, eq, LOW[:, :, :].rearrange("p b c -> p (b c)").unsqueeze(1).broadcast_to([P, BT, E * E]),
                                       ALU.mult), "eq")
            lane.wait(eng, 3, "eq")
            lane.inc(eng.tensor_tensor(EQ4[:, :, :, :], EQ4[:, :, :, :], GT4[:, :, :, :], ALU.add), "b")
            lane.wait(eng, 3, "b")
            lane.inc(eng.tensor_tensor(EQ4[:, :, :, :], EQ4[:, :, :, :],
                                       PR4[:, :, :].unsqueeze(2).broadcast_to([P, BT, E, E]), ALU.mult), "bp")

        def pool_wp(eng, n, x):
            wait_apart(L["v_wp"], eng, n, f"mx.2.{x}")
            L["g_wp"].inc(eng.partition_all_reduce(MAW[:, :], MXW[:, :], P, bass.bass_isa.ReduceOp.max), f"ar{x}")

        def pool_wlo(eng, n, x):
            e = 2 * (n - 4) + 1 + x
            L["a_wp"].wait(eng, n, f"sc{x}.2")
            L["g_wp"].inc(eng.tensor_tensor(W[:, e, 1, 2, :], loaded(n, x)[:, 2, :], W[:, e, 0, 2, :], ALU.subtract), f"lo.2.{x}")

        def pool_bo(eng, n):
            wait_apart(L["v_al"], eng, n, "xn")
            x = X[:, n - 8, :]
            L["g_al"].inc(eng.tensor_tensor(x, x, BO[:, :], ALU.add), "bo")

        def pool_sq(eng, n):
            L["v_qk"].wait(eng, n, "qb")
            L["g_qk"].inc(eng.tensor_tensor(SQ[:, :], QKV[:, 0:QK * HD], QKV[:, 0:QK * HD], ALU.mult), "sq")

        def pool_rr(eng, n):
            L["v_qk"].wait(eng, n, "ms")
            L["g_qk"].inc(eng.tensor_tensor(RR[:, :], MS[:, :], MH[:, :], ALU.pow), "rr")
            L["g_qk"].wait(eng, n, "rr")
            L["g_qk"].inc(eng.tensor_tensor(RR[:, 0:H], RR[:, 0:H], SGN[:, :], ALU.mult), "sg")

        def pool_ra(eng, n):
            L["v_a3"].wait(eng, n, "qn")
            L["v_a3"].wait(eng, n - 1, "klo1")
            L["a_a3"].wait(eng, n - 1, "khi1")
            c8 = HD // 2
            L["g_a3"].inc(eng.tensor_tensor(RA[:, :].rearrange("p (h c) -> p h c", c=c8), QN[:, :].rearrange("p (h c) -> p h c", c=c8),
                                            COS[:, n % 2, :].unsqueeze(1).broadcast_to([P, 2 * QK, c8]), ALU.mult), "ra")

        def pool_v(eng, n):
            v = QKV[:, QK * HD:].rearrange("p (h c) -> p h c", c=HD)
            vs = VS[:, ((n - 9) // 2) % 3, (n + 1) % 2, :, :]
            L["g_qk"].inc(eng.tensor_copy(vs[:, :, 0:HD], v), "v1")
            wait_apart(L["g_qk"], eng, n, "v1")
            L["g_qk"].inc(eng.tensor_tensor(VR[:, 0, :, :], v, vs[:, :, 0:HD], ALU.subtract), "r1")
            L["g_qk"].wait(eng, n, "r1")
            L["g_qk"].inc(eng.tensor_copy(vs[:, :, HD:2 * HD], VR[:, 0, :, :]), "v2")
            wait_apart(L["g_qk"], eng, n, "v2")
            L["g_qk"].inc(eng.tensor_tensor(VR[:, 1, :, :], VR[:, 0, :, :], vs[:, :, HD:2 * HD], ALU.subtract), "r2")
            L["g_qk"].wait(eng, n, "r2")
            L["g_qk"].inc(eng.tensor_copy(vs[:, :, 2 * HD:3 * HD], VR[:, 1, :, :]), "v3")

        def pool_mask(eng, n, it, j):
            b, e = ((0, 3), (2, 7))[j]
            wait_apart(L["a_hd"], eng, n, f"e{it}.{e}")
            L["g_hd"].inc(eng.affine_select(out=P32[:, b, :, :], in_=P32[:, b, :, :], compare_op=ALU.is_ge, fill=0.0,
                                            base=0, pattern=[[0, G], [-1, P]], channel_multiplier=1), f"k{it}.{j}")

        def pool_os(eng, n, act):
            L["v_pw"].wait(eng, n if "pw" in act else 28, "ob")
            if "op" in act:
                L["p_op"].wait(eng, n, "tp")
            L["g_os"].inc(eng.tensor_copy(OS[:, :], OB[:, ((n - 14) // 2) % 2, n % 2, :, :].rearrange("p a b -> p (a b)")), "os")

        def pool_body(eng, n, act):
            first = isinstance(n, int) and n == 4
            last = isinstance(n, int) and n == 7
            for p in range(16):
                i = p // 2
                if p == 0 and "fp" in act:
                    pool_rs(eng, n, "v_ln", "g_ln", "f")
                if p == 1 and "a3" in act:
                    pool_ra(eng, n)
                if "wp" in act and not (last and p > 7):
                    if p % 8 == 3:
                        pool_wp(eng, n, p // 8)
                if p == 2 and "ap" in act:
                    pool_rs(eng, n, "v_al", "g_al", "a")
                if p == 4 and "os" in act:
                    pool_os(eng, n, act)
                if p == 4 and "ap" in act:
                    pool_bo(eng, n)
                if first and p == 5:
                    pool_rank4(eng)
                if isinstance(n, int) and p == 0 and n == RANGES["ap"][0]:
                    eng.wait_ge(s_aw, 16 * 11)
                if isinstance(n, int) and p == 0 and n == RANGES["qk"][0]:
                    eng.wait_ge(s_ag, 4)
                if p in (5, 13) and "hd" in act:
                    pool_mask(eng, n, p // 8, 0)
                    pool_mask(eng, n, p // 8, 1)
                if p == 14 and "fp" in act:
                    pool_rank(eng, n)
                if p % 2 == 1:
                    pool_lo(eng, n, i)
                if "wp" in act and p % 8 == 7 and not (last and p > 7):
                    pool_wlo(eng, n, p // 8)
                if p == 3 and "qk" in act:
                    pool_sq(eng, n)
                if p == 7 and "qk" in act:
                    pool_rr(eng, n)
                if p == 9 and "qk" in act:
                    pool_v(eng, n)

        block = ctx.enter_context(nc.Block())

        @block.sync
        def _(eng):
            xt = d["x"].rearrange("(n p) d -> p n d", p=P)
            eng.dma_start(X[:, 0:BT, :], xt[:, 0:BT, :]).then_inc(s_x0, 16)

            def load(j, e, to, by):
                eng.dma_start(to[:, j, :], d[("gate", "up", "down")[j]][e]).then_inc(by[j], 16)

            for j in range(3):
                load(j, 0, stage, s_w)
            for j in range(3):
                load(j, 1, early, s_early)
            for b in range(1, NT // BT):
                eng.dma_start(X[:, b * BT:(b + 1) * BT, :], xt[:, b * BT:(b + 1) * BT, :]).then_inc(s_x1, 16)

            def load_next(e):
                n, x = (3, 1) if e == 2 else ((e - 1) // 2 + 4 - e % 2, e % 2)
                for j in range(3):
                    L["g_wp" if j == 2 else "v_wp"].wait(eng, n, f"lo.{j}.{x}")
                    load(j, e, stage, s_w)

            load_next(2)
            bc = lambda v: v.rearrange("(a n) -> a n", a=1).broadcast_to([P, v.shape[0]])
            c = 0
            for w, width in (("wq", D), ("wk", KVH * HD), ("wv", KVH * HD)):
                eng.dma_start(WQKV[:, :, c:c + width], d[w]).then_inc(s_aw, 16)
                eng.dma_start(BQKV[:, c:c + width], bc(d["b" + w[1]])).then_inc(s_aw, 16)
                c += width
            eng.dma_start(WO[:, :, :], d["wo"]).then_inc(s_aw, 16)
            eng.dma_start(BO[:, :], bc(d["bo"])).then_inc(s_aw, 16)
            eng.dma_start(GN[:, :], bc(d["gain"])).then_inc(s_aw, 16)
            eng.dma_start(COS[:, :, :], d["cos"]).then_inc(s_aw, 16)
            eng.dma_start(SIN[:, :, :], d["sin"]).then_inc(s_aw, 16)
            for e in range(3, E):
                load_next(e)

            def store(n, t):
                L["v_y"].wait(eng, n, "y3")
                eng.dma_start(d["out"][t, :, :], X[:, t, :]).then_inc(s_st, 16)

            for a, b in RUNS:
                if "st" in active(a):
                    if b - a == 1:
                        store(a, a - 24)
                    else:
                        with eng.Fori(a, b) as n:
                            store(n, n - 24)
            for m in range(BT):
                t = NT - BT + m
                L["v_y"].wait(eng, 36, f"y{m}")
                eng.dma_start(d["out"][t, :, :], X[:, t, :]).then_inc(s_st, 16)
            eng.wait_ge(s_st, 16 * NT)

        @block.gpsimd
        def _(eng):
            give_credit(eng, "g_")
            eng.memset(ident[:, :], 0.0).then_inc(s_i1, 1)
            eng.memset(MH[:, :], -0.5).then_inc(s_i1, 1)
            eng.memset(LOW[:, :, :], 1.0).then_inc(s_i1, 1)
            eng.memset(ident16[:, :], 0.0).then_inc(s_i1, 1)
            eng.memset(MB[:, :, :], 0.0).then_inc(s_i1, 1)
            eng.wait_ge(s_i1, 5)
            for t in (ident, ident16):
                eng.affine_select(out=t[:, :], in_=t[:, :], compare_op=ALU.not_equal, fill=1.0, base=0,
                                  pattern=[[-1, P]], channel_multiplier=1).then_inc(s_i1, 1)
            eng.affine_select(out=LOW[:, :, :], in_=LOW[:, :, :], compare_op=ALU.is_ge, fill=0.0, base=-1,
                              pattern=[[1, E], [-1, E]], channel_multiplier=0).then_inc(s_i1, 1)
            eng.wait_ge(s_i1, N_I1)
            L["v_pre"].wait(eng, 3, "eps")
            L["g_pre"].inc(eng.tensor_tensor(RS4[:, :], VE4[:, :], MH[:, 0:BT], ALU.pow), "rs")
            pool_wp(eng, 3, 1)
            eng.affine_select(out=MB[:, :, :], in_=MB[:, :, :], compare_op=ALU.is_ge, fill=MASKED, base=0,
                              pattern=[[0, G], [-1, P]], channel_multiplier=1).then_inc(s_i2, 1)
            eng.memset(KT[:, :, :, :, :, :], 0.0).then_inc(s_i2, 1)
            eng.memset(VS[:, :, :, :, :], 1.0).then_inc(s_i2, 1)
            pool_wlo(eng, 3, 1)
            eng.wait_ge(s_i2, 3)
            steps(eng, lambda n, act: pool_body(eng, n, act))

        @block.scalar
        def _(eng):
            give_credit(eng, "a_")
            eng.dma_start(RW[:, :, :], d["rw"]).then_inc(s_rw, 16)
            for t in range(BT):
                L["p_pre"].wait(eng, 3, f"tp{t}")
                bank = (GB[0], UB[0], GB[1], UB[1])[t][:, 0:D]
                L["a_pre"].inc(eng.activation(XT4[:, t, :, :].rearrange("p k c -> p (k c)"), bank, ACT.Copy), f"xt{t}")
                L["a_pre"].inc(eng.activation(XS16[:, 0, 0, :, t, :], bank.rearrange("p (k c) -> p k c", k=KD), ACT.Copy, scale=XS), f"xh{t}")
            act_wp(eng, 3, 1, range(3))
            steps(eng, lambda n, act: act_body(eng, n, act))

        @block.vector
        def _(eng):
            give_credit(eng, "v_")
            lane = L["v_pre"]

            def each(label, op):
                for t in range(BT):
                    lane.inc(op(t), f"{label}{t}")

            def xl(t):
                L["a_pre"].wait(eng, 3, f"xh{t}")
                lane.inc(eng.scalar_tensor_tensor(XS16[:, 0, 1, :, t, :], XT4[:, t, :, :], XS, XS16[:, 0, 0, :, t, :],
                                                  ALU.mult, ALU.subtract), f"xl{t}")

            eng.wait_ge(s_x0, 16)
            each("stats", lambda t: eng.bn_stats(ST4[:, t, :], X[:, t, :]))
            for t in range(BT):
                lane.wait(eng, 3, f"stats{t}")
                lane.inc(eng.bn_aggr(MV4[:, t, :], ST4[:, t, :]), f"aggr{t}")
            lane.wait(eng, 3, f"aggr{BT - 1}")
            lane.inc(eng.tensor_scalar(VE4[:, :], MV4[:, :, 1], LN_EPS, None, ALU.add), "eps")
            dve_mx(eng, 3, 1, (0,))
            L["g_pre"].wait(eng, 3, "rs")
            each("xn", lambda t: eng.tensor_scalar(XN4[:, t, :], X[:, t, :], MV4[:, t, 0:1], RS4[:, t:t + 1],
                                                   ALU.subtract, ALU.mult))
            dve_mx(eng, 3, 1, (1, 2))
            for t in range(BT):
                xl(t)
            dve_scale(eng, 3, 1)
            L["p_pre"].wait(eng, 3, "lg")
            lg = YB[:, 0:BT * E].rearrange("p (t e) -> p t e", t=BT)
            lane.inc(eng.tensor_reduce(MX4[:, :], lg, AX.X, ALU.max), "mx")
            lane.wait(eng, 3, "mx")
            lane.inc(eng.tensor_tensor(LG4[:, :, :], lg, MX4[:, :].unsqueeze(2).broadcast_to([P, BT, E]), ALU.subtract), "sub")
            dve_wlo(eng, 3, 1, 0)
            dve_wlo(eng, 3, 1, 1)
            steps(eng, lambda n, act: dve_body(eng, n, act))
            for m in range(BT):
                dve_y(eng, 36, set(), m, LAST[m])

        @block.tensor
        def _(eng):
            give_credit(eng, "p_")
            eng.wait_ge(s_i1, N_I1)
            eng.wait_ge(s_rw, 16)
            for t in range(BT):
                L["v_pre"].wait(eng, 3, f"xn{t}")
                bank = (GB[0], UB[0], GB[1], UB[1])[t]
                for k in range(KD):
                    mm = eng.transpose(bank[:, k * P:(k + 1) * P], XN4[:, t, k * P:(k + 1) * P], ident[:, :])
                L["p_pre"].inc(mm, f"tp{t}")
            for t in range(BT):
                L["a_pre"].wait(eng, 3, f"xt{t}")
                for k in range(KD):
                    mm = eng.matmul(YB[:, t * E:(t + 1) * E], XT4[:, t, k, :], RW[:, k, :], start=(k == 0), stop=(k == KD - 1))
            L["p_pre"].inc(mm, "lg")
            steps(eng, lambda n, act: pe_body(eng, n, act))
            for ks in (range(KI - 1), range(KI - 1, KI)):
                for m in range(BT):
                    if LAST[m] is GB[0] and ks[0] == 0:
                        L["v_ff"].wait(eng, 35, "h6")
                    pe_y(eng, 36, set(), m, LAST[m], ks)


def kernel(**inputs):
    import concourse.bacc as bacc
    from concourse.bass_utils import run_bass_kernel_spmd as run

    def ktile(w):
        return np.ascontiguousarray(w.T.reshape(-1, P, w.shape[0]).transpose(1, 0, 2))

    def experts(w):
        return np.ascontiguousarray(np.stack([ktile(w[e]).reshape(P, -1) for e in range(E)]))

    f = {k: np.asarray(v) for k, v in inputs.items()}
    a, m = "L0_attn_", "L0_ffn_"
    t = np.arange(S, dtype=np.float32)
    inv = (1.0 / 10000.0 ** (np.arange(0, HD, 2, dtype=np.float32) / HD)).astype(np.float32)
    freqs = np.outer(t, inv).astype(np.float32)
    rope = lambda z: np.ascontiguousarray(z.astype(np.float32).reshape(2, P, HD // 2).transpose(1, 0, 2))
    arrays = {
        "x": f[a + "x"].reshape(B * S, D),
        "gate": experts(f[m + "gate_w"]), "up": experts(f[m + "up_w"]), "down": experts(f[m + "down_w"]),
        "rw": ktile(f[m + "router_w"]),
        "wq": ktile(f[a + "Wq"]), "wk": ktile(f[a + "Wk"]), "wv": ktile(f[a + "Wv"]), "wo": ktile(f[a + "Wo"]),
        "bq": f[a + "bq"], "bk": f[a + "bk"], "bv": f[a + "bv"], "bo": f[a + "bo"], "gain": f[a + "q_gain"],
        "cos": rope(np.cos(freqs)), "sin": rope(np.sin(freqs)),
    }
    nc = bacc.Bacc("TRN2", target_bir_lowering=False, num_devices=1)
    aps = {k: nc.dram_tensor(f"in_{k}", v.shape, mybir.dt.from_np(v.dtype), kind="ExternalInput").ap()
           for k, v in arrays.items()}
    aps["out"] = nc.dram_tensor("out_y", (NT, P, D), F32, kind="ExternalOutput").ap()
    build(nc, aps)
    r = run(nc, [{f"in_{k}": v for k, v in arrays.items()}], core_ids=[0])
    return r.results[0]["out_y"].reshape(B, S, D)
```
